# Optimizing a Trainium2 kernel written in Bass

```python
import numpy as np
import jax
import jax.numpy as jnp

def _softmax(x, axis=-1):
    return jax.nn.softmax(x, axis=axis)

def _gelu(x):
    return jax.nn.gelu(x, approximate=True)

def _silu(x):
    return jax.nn.silu(x)

def _sigmoid(x):
    return jax.nn.sigmoid(x)

def _layernorm(x, axis=-1, eps=1e-05):
    m = jnp.mean(x, axis=axis, keepdims=True)
    v = jnp.var(x, axis=axis, keepdims=True)
    return (x - m) / jnp.sqrt(v + eps)

def _scatter_add(tgt, idx, src, axis=0):
    return tgt.at[idx].add(src)

def _segment_sum(src, seg, n):
    return jax.ops.segment_sum(src, seg, n)
kernel_name = 'mk_xattn_ffn_d1_seqx_r4_a50a85'

def setup_inputs(seed: int=0):
    np.random.seed(seed)
    _w = jnp.asarray

    def _rec_inputs():
        import jax
        import jax.numpy as jnp
        _rk = jax.random.key(seed)
        x = -0.0002928 + 1 * jax.random.normal(jax.random.fold_in(_rk, 1), (8, 256, 256), jnp.float32)
        _lenS = 256 - jax.random.randint(jax.random.fold_in(_rk, 7), (8,), 0, max(1, 256 // 4) + 1, jnp.int32)
        _lenS2 = 256 - jax.random.randint(jax.random.fold_in(_rk, 8), (8,), 0, max(1, 256 // 4) + 1, jnp.int32)
        _ctx_1024P = jax.random.normal(jax.random.fold_in(_rk, 11), (8, 16, 256), jnp.float32)
        _ctx_1024c = jax.random.dirichlet(jax.random.fold_in(_rk, 511), 0.3 * jnp.ones((16,), jnp.float32), (8, 256))
        _ctx_1024t = jnp.einsum('bsk,bkd->bsd', _ctx_1024c, _ctx_1024P)
        _ctx_1024t = _ctx_1024t * jax.lax.rsqrt(jnp.mean(jnp.square(_ctx_1024t)) + 1e-12) * 0.953939
        ctx_1024 = -1.39393e-06 + 0.999914 * (_ctx_1024t + 0.3 * jax.random.normal(jax.random.fold_in(_rk, 611), (8, 256, 256), jnp.float32))
        return (x, ctx_1024)
    x, ctx_1024 = _rec_inputs()

    def _L0_xattn_setup():
        import jax, jax.numpy as jnp
        import numpy as np
        EMBED = 256
        HEADS = 16
        HEAD_DIM = EMBED // HEADS
        B, S = (2, 512)

        def _split_heads(x):
            b, s, _ = x.shape
            return x.reshape(b, s, HEADS, HEAD_DIM).transpose(0, 2, 1, 3)
        key = jax.random.key(seed)
        ks = jax.random.split(key, 12)
        std = 0.02
        inp = {'query': jax.random.normal(ks[0], (B, S, EMBED), jnp.float32), 'key': jax.random.normal(ks[1], (B, S, EMBED), jnp.float32), 'value': jax.random.normal(ks[2], (B, S, EMBED), jnp.float32), 'Wq': jax.random.normal(ks[3], (EMBED, EMBED), jnp.float32) * std, 'bq': jnp.zeros((EMBED,), jnp.float32), 'Wk': jax.random.normal(ks[4], (EMBED, EMBED), jnp.float32) * std, 'bk': jnp.zeros((EMBED,), jnp.float32), 'Wv': jax.random.normal(ks[5], (EMBED, EMBED), jnp.float32) * std, 'bv': jnp.zeros((EMBED,), jnp.float32), 'Wo': jax.random.normal(ks[6], (EMBED, EMBED), jnp.float32) * std, 'bo': jnp.zeros((EMBED,), jnp.float32)}
        return inp
    _L0_xattn_all = _L0_xattn_setup()
    _L0_xattn_in = {k: v for k, v in _L0_xattn_all.items() if k in ('Wq', 'bq', 'Wk', 'bk', 'Wv', 'bv', 'Wo', 'bo')}
    del _L0_xattn_all

    def _L0_ffn_setup():
        import jax, jax.numpy as jnp
        import numpy as np
        DIM = 256
        EXPERT_DIM = 128
        N_EXPERTS = 16
        TOPK = 2
        SHARED_HIDDEN = EXPERT_DIM * TOPK
        B, T = (4, 256)

        def _moe_forward(x, router_w, router_bias, up_proj, gate_proj, down_proj, sh_gate, sh_up, sh_down):
            Bb, Tt, D = x.shape
            flat = x.reshape(Bb * Tt, D)
            N = flat.shape[0]
            logits = flat @ router_w.T
            topk_scores, topk_idx = jax.lax.top_k(logits + router_bias, TOPK)
            topk_scores = jax.nn.softmax(topk_scores, axis=-1)
            combine = jnp.zeros((N, N_EXPERTS), flat.dtype)
            combine = combine.at[jnp.arange(N)[:, None], topk_idx].add(topk_scores)
            up_all = jnp.einsum('nd,kde->nke', flat, up_proj)
            gate_all = jnp.einsum('nd,kde->nke', flat, gate_proj)
            hidden = jax.nn.silu(gate_all) * up_all
            down_all = jnp.einsum('nke,ked->nkd', hidden, down_proj)
            out = jnp.einsum('nk,nkd->nd', combine, down_all)
            sh_hidden = jax.nn.silu(flat @ sh_gate.T) * (flat @ sh_up.T)
            out = out + sh_hidden @ sh_down.T
            return out.reshape(Bb, Tt, D)
        key = jax.random.key(seed)
        ks = jax.random.split(key, 9)
        std = 0.02
        return {'x': jax.random.normal(ks[0], (B, T, DIM), jnp.float32), 'router_w': jax.random.normal(ks[1], (N_EXPERTS, DIM), jnp.float32) * std, 'router_bias': jnp.zeros((N_EXPERTS,), jnp.float32), 'up_proj': jax.random.normal(ks[2], (N_EXPERTS, DIM, EXPERT_DIM), jnp.float32) * std, 'gate_proj': jax.random.normal(ks[3], (N_EXPERTS, DIM, EXPERT_DIM), jnp.float32) * std, 'down_proj': jax.random.normal(ks[4], (N_EXPERTS, EXPERT_DIM, DIM), jnp.float32) * std, 'sh_gate': jax.random.normal(ks[5], (SHARED_HIDDEN, DIM), jnp.float32) * std, 'sh_up': jax.random.normal(ks[6], (SHARED_HIDDEN, DIM), jnp.float32) * std, 'sh_down': jax.random.normal(ks[7], (DIM, SHARED_HIDDEN), jnp.float32) * std}
    _L0_ffn_all = _L0_ffn_setup()
    _L0_ffn_in = {k: v for k, v in _L0_ffn_all.items() if k in ('router_w', 'router_bias', 'up_proj', 'gate_proj', 'down_proj', 'sh_gate', 'sh_up', 'sh_down')}
    del _L0_ffn_all
    return {'x': x, 'ctx_1024': ctx_1024, 'L0_xattn_Wq': _L0_xattn_in['Wq'], 'L0_xattn_bq': _L0_xattn_in['bq'], 'L0_xattn_Wk': _L0_xattn_in['Wk'], 'L0_xattn_bk': _L0_xattn_in['bk'], 'L0_xattn_Wv': _L0_xattn_in['Wv'], 'L0_xattn_bv': _L0_xattn_in['bv'], 'L0_xattn_Wo': _L0_xattn_in['Wo'], 'L0_xattn_bo': _L0_xattn_in['bo'], 'L0_ffn_router_w': _L0_ffn_in['router_w'], 'L0_ffn_router_bias': _L0_ffn_in['router_bias'], 'L0_ffn_up_proj': _L0_ffn_in['up_proj'], 'L0_ffn_gate_proj': _L0_ffn_in['gate_proj'], 'L0_ffn_down_proj': _L0_ffn_in['down_proj'], 'L0_ffn_sh_gate': _L0_ffn_in['sh_gate'], 'L0_ffn_sh_up': _L0_ffn_in['sh_up'], 'L0_ffn_sh_down': _L0_ffn_in['sh_down']}

def reference(x, ctx_1024, L0_xattn_Wq, L0_xattn_bq, L0_xattn_Wk, L0_xattn_bk, L0_xattn_Wv, L0_xattn_bv, L0_xattn_Wo, L0_xattn_bo, L0_ffn_router_w, L0_ffn_router_bias, L0_ffn_up_proj, L0_ffn_gate_proj, L0_ffn_down_proj, L0_ffn_sh_gate, L0_ffn_sh_up, L0_ffn_sh_down):
    import jax
    import jax.numpy as jnp

    def _L0_xattn_ref(query, key, value, Wq, bq, Wk, bk, Wv, bv, Wo, bo):
        import jax, jax.numpy as jnp
        import numpy as np
        EMBED = 256
        HEADS = 16
        HEAD_DIM = EMBED // HEADS
        B, S = (2, 512)

        def _split_heads(x):
            b, s, _ = x.shape
            return x.reshape(b, s, HEADS, HEAD_DIM).transpose(0, 2, 1, 3)
        Q = _split_heads(query @ Wq.T + bq)
        K = _split_heads(key @ Wk.T + bk)
        V = _split_heads(value @ Wv.T + bv)
        Qf = jnp.fft.fft(Q, axis=-1)
        Kf = jnp.fft.fft(K, axis=-1)
        scores = jnp.abs(jnp.einsum('bhsd,bhtd->bhst', Qf, Kf)) / np.sqrt(HEAD_DIM).astype(np.float32)
        w = jax.nn.softmax(scores, axis=-1)
        out = jnp.einsum('bhst,bhtd->bhsd', w, V)
        out = out.transpose(0, 2, 1, 3).reshape(query.shape[0], query.shape[1], EMBED)
        return out @ Wo.T + bo

    def _L0_ffn_ref(x, router_w, router_bias, up_proj, gate_proj, down_proj, sh_gate, sh_up, sh_down):
        import jax, jax.numpy as jnp
        import numpy as np
        DIM = 256
        EXPERT_DIM = 128
        N_EXPERTS = 16
        TOPK = 2
        SHARED_HIDDEN = EXPERT_DIM * TOPK
        B, T = (4, 256)

        def _moe_forward(x, router_w, router_bias, up_proj, gate_proj, down_proj, sh_gate, sh_up, sh_down):
            Bb, Tt, D = x.shape
            flat = x.reshape(Bb * Tt, D)
            N = flat.shape[0]
            logits = flat @ router_w.T
            topk_scores, topk_idx = jax.lax.top_k(logits + router_bias, TOPK)
            topk_scores = jax.nn.softmax(topk_scores, axis=-1)
            combine = jnp.zeros((N, N_EXPERTS), flat.dtype)
            combine = combine.at[jnp.arange(N)[:, None], topk_idx].add(topk_scores)
            up_all = jnp.einsum('nd,kde->nke', flat, up_proj)
            gate_all = jnp.einsum('nd,kde->nke', flat, gate_proj)
            hidden = jax.nn.silu(gate_all) * up_all
            down_all = jnp.einsum('nke,ked->nkd', hidden, down_proj)
            out = jnp.einsum('nk,nkd->nd', combine, down_all)
            sh_hidden = jax.nn.silu(flat @ sh_gate.T) * (flat @ sh_up.T)
            out = out + sh_hidden @ sh_down.T
            return out.reshape(Bb, Tt, D)
        return _moe_forward(x, router_w, router_bias, up_proj, gate_proj, down_proj, sh_gate, sh_up, sh_down)
    x = x + _L0_xattn_ref(_layernorm(x, axis=-1), ctx_1024, ctx_1024, L0_xattn_Wq, L0_xattn_bq, L0_xattn_Wk, L0_xattn_bk, L0_xattn_Wv, L0_xattn_bv, L0_xattn_Wo, L0_xattn_bo)
    x = x + _L0_ffn_ref(_layernorm(x, axis=-1), L0_ffn_router_w, L0_ffn_router_bias, L0_ffn_up_proj, L0_ffn_gate_proj, L0_ffn_down_proj, L0_ffn_sh_gate, L0_ffn_sh_up, L0_ffn_sh_down)
    return x

_drawn_inputs = setup_inputs


def setup_inputs(seed=0):
    import zlib

    import numpy as np

    out = dict(_drawn_inputs(seed))
    spreads = {'L0_xattn_bq': (0.0, 0.549),
     'L0_xattn_bk': (0.0, 0.655),
     'L0_xattn_bv': (0.0, 0.1),
     'L0_xattn_bo': (0.0, 0.1),
     'L0_ffn_router_bias': (0.0, 0.8)}
    factors = {'L0_ffn_router_w': 7.259,
     'L0_ffn_up_proj': 6.671,
     'L0_ffn_gate_proj': 6.771,
     'L0_ffn_down_proj': 6.672,
     'L0_ffn_sh_gate': 3.408,
     'L0_ffn_sh_up': 3.38,
     'L0_ffn_sh_down': 3.367}
    for name, (base, spread) in spreads.items():
        noise = np.random.default_rng([zlib.crc32(name.encode()), seed]).standard_normal(out[name].shape)
        drawn = base * np.exp(spread * noise) if base else spread * noise
        out[name] = jnp.asarray(drawn.astype(out[name].dtype))
    for name, factor in factors.items():
        out[name] = (out[name] * factor).astype(out[name].dtype)
    return out
```

```python
from contextlib import ExitStack

import numpy as np

import concourse.bass as bass
from concourse import mybir

F32 = mybir.dt.float32
BF16 = mybir.dt.bfloat16
I32 = mybir.dt.int32
U32 = mybir.dt.uint32
ALU = mybir.AluOpType
ACT = mybir.ActivationFunctionType
AX = mybir.AxisListType

P = 128
B, S, D = 8, 256, 256
H, HD = 16, 16
KT = D // P
ST = S // P
NT = B * ST
TOK = B * S
NU = 4
SLOT = 32
E, EH, TOPK = 16, 128, 2
PAIRS = TOPK * TOK
TILES = 48
SCALE = float(HD) ** 0.5
EPS = 1e-5
RING = 4
PEEL = RING + 2
HOTS = 4
CHUNKS = 4
MISC = 2
assert PAIRS // P + E - 1 <= TILES and (TILES - 2 * PEEL) % RING == 0

PLAN = [
    ([], ["f_slots0", "f_slots1"]),
    (["p_x", "f_heads"], ["f_out"]),
    (["p_q", "p_k"], []),
    (["p_v"], ["f_h", "f_router"]),
]
PROLOGUE = ["p_x", "p_q", "p_k", "p_v"]
EPILOGUE = ["f_slots0", "f_slots1", "f_heads", "f_out", "f_h", "f_router"]


class Step:

    def __init__(self, b, par, half, first=False, last=False):
        self.b, self.par, self.half, self.first, self.last = b, par, half, first, last
        self.uses = []
        for u, (before, between) in enumerate(PLAN):
            self.uses += [n for n in before + between if self.has(n)] + [f"o{u}"]

    def has(self, name):
        return not ((self.first and name[0] == "f") or (self.last and name[0] == "p"))

    def number(self, name):
        if self.first:
            return len(PROLOGUE) + self.uses.index(name)
        return self.b * USES + (FIRST_USES - USES + self.uses.index(name))

    def bank(self, name):
        return (len(PROLOGUE) + self.uses.index(name)) % MISC


USES = len(Step(1, 1, 0).uses)
FIRST_USES = len(PROLOGUE) + len(Step(0, 0, 0, first=True).uses)
LAST_STEP = Step(B - 1, 1, B // 2 - 1, last=True)
END_USES = LAST_STEP.number("o3") + 1
assert USES % MISC == 0 and FIRST_USES % MISC == 0 and END_USES % MISC == 0


def program(nc, a, out):
    with ExitStack() as ctx:
        def sb(name, shape, dt=F32):
            return ctx.enter_context(nc.sbuf_tensor(name, shape, dt))

        def sem(name):
            return ctx.enter_context(nc.semaphore(name))

        ps = ctx.enter_context(nc.psum_tensor("ps", [P, 8, 512], F32))
        ps_scores = ps[:, 0:4, :]
        ps_probs = [ps[:, 4 + i, :] for i in range(2)]
        ps_misc = [ps[:, 6 + i, :] for i in range(MISC)]

        ident = sb("ident", [P, P])
        part_mask = sb("part_mask", [P, 4])
        onehot = sb("onehot", [P, 4, P], BF16)
        before = sb("before", [P, P], BF16)
        ones_bf = sb("ones_bf", [P, P], BF16)
        head_mask = sb("head_mask", [P, 2])
        expert_iota = sb("expert_iota", [P, E])
        tile_iota = sb("tile_iota", [P, TILES])
        row_iota = sb("row_iota", [P, P])
        row_number = sb("row_number", [P, 1])
        minus_half = sb("minus_half", [P, ST])
        eps_tile = sb("eps_tile", [P, ST])
        zeros = sb("zeros", [P, 4 * ST])
        dve_carrier = sb("dve_carrier", [P, 1])
        pool_carrier = sb("pool_carrier", [P, RING])

        wq = sb("wq", [P, KT, D])
        wk = sb("wk", [P, KT, D])
        wv = sb("wv", [P, KT, D])
        wo = sb("wo", [P, KT, D])
        bq = sb("bq", [P, KT])
        bk = sb("bk", [P, KT])
        bv = sb("bv", [P, D])
        bo = sb("bo", [P, D])
        rw = sb("rw", [P, KT, E])
        rb = sb("rb", [P, E])
        sh_gu = sb("sh_gu", [P, KT, 2 * D])
        sh_d = sb("sh_d", [P, KT, D])
        w_gu = sb("w_gu", [P, E, KT, 2 * EH])
        w_d = sb("w_d", [P, E, D])

        x_in = sb("x_in", [P, 2, ST, D])
        ctx_t = sb("ctx_t", [P, 2, KT, S])
        x_bo = sb("x_bo", [P, 2, ST, D])
        ln_stats = sb("ln_stats", [P, 2, ST, 6])
        ln_mv = sb("ln_mv", [P, 2, ST, 2])
        ln_var = sb("ln_var", [P, 2, ST])
        ln_rstd = sb("ln_rstd", [P, 2, ST])
        ln_shift = sb("ln_shift", [P, 2, ST])
        xn = sb("xn", [P, 2, ST, D])
        xn_t = sb("xn_t", [P, 2, KT, S])
        q_t = sb("q_t", [P, 2, 2, S])
        k_t = sb("k_t", [P, 2, 2, 2, S])
        v_one = sb("v_one", [P, 2, ST, H, SLOT])
        scores = sb("scores", [P, 2, 4, ST, S])
        neg_max = sb("neg_max", [P, 2, 4 * ST])
        rest1 = sb("rest1", [P, 2, 4 * ST])
        start_marks = sb("start_marks", [P, 2])
        max_parts = sb("max_parts", [P, 2, ST, SLOT], BF16)
        max_rows = sb("max_rows", [P, 2, ST, P], BF16)
        attn = sb("attn", [P, NT * D])
        h_all = attn[:, :].rearrange("p (t d) -> p t d", d=D)
        probs = attn[:, 0:8 * S].rearrange("p (s j q) -> p s j q", s=4, j=2)
        o_slots = attn[:, 8 * S:12 * S].rearrange("p (u q) -> p u q", u=NU)
        inv_sum = sb("inv_sum", [P, ST, H])
        o_norm = attn[:, 12 * S:14 * S].rearrange("p (t d) -> p t d", t=ST)
        o_t = attn[:, 14 * S:16 * S].rearrange("p (k s) -> p k s", k=KT)
        h = sb("h", [P, 2, ST, D])
        h_tp = sb("h_tp", [P, 2, KT, S])

        x1 = sb("x1", [P, NT, D])
        h_t = sb("h_t", [P, KT, TOK])
        logits = sb("logits", [P, NT, E])

        top8 = sb("top8", [P, NT, 8])
        top8_at = sb("top8_at", [P, NT, 8], U32)
        choice = sb("choice", [P, NT, TOPK])
        chosen = sb("chosen", [P, TOPK, NT, E])
        chosen_any = sb("chosen_any", [P, NT, E], BF16)
        tiles_i = sb("tiles_i", [P, E], I32)
        tiles_s = sb("tiles_s", [P, E], I32)
        tiles_f = sb("tiles_f", [P, E])
        tiles_end = sb("tiles_end", [P, E])
        row_start = sb("row_start", [P, E])
        ones_f = sb("ones_f", [P, E])
        rank = sb("rank", [P, NT, E])
        rank_of = sb("rank_of", [P, TOPK, NT, E])
        pos_f = sb("pos_f", [P, TOPK, NT])
        pos_i = sb("pos_i", [P, TOPK, NT], I32)
        pos_lo = sb("pos_lo", [P, TOPK, NT], I32)
        pos_hi = sb("pos_hi", [P, TOPK, NT], I32)
        pos_lof = sb("pos_lof", [P, TOPK, NT])
        pos_hif = sb("pos_hif", [P, TOPK, NT])
        pos_at = sb("pos_at", [P, TOPK, NT], U32)
        past = sb("past", [P, TILES, E])
        tile_expert_f = sb("tile_expert_f", [P, TILES])
        tile_expert = sb("tile_expert", [P, TILES], I32)
        gap = sb("gap", [P, NT])
        gap_exp = sb("gap_exp", [P, NT])
        gap_sum = sb("gap_sum", [P, NT])
        weight = sb("weight", [P, TOPK, NT])
        ids = sb("ids", [P, TILES], U32)
        id_sums = sb("id_sums", [P, 3, TILES])
        hot_row = sb("hot_row", [P, HOTS, P], BF16)
        hot_tile = sb("hot_tile", [P, HOTS, 3, TILES], BF16)

        sh_act, sh_hid = [scores[:, i].rearrange("p j t k -> p (j t k)").rearrange("p (a m n) -> p a m n", a=2, m=KT)
                          for i in range(2)]
        scatter_at = [sb(f"scatter_at{i}", [P, 1], U32) for i in range(RING)]
        rows = [x_in[:, i // ST, i % ST, :] for i in range(RING)]
        rows_t = sb("rows_t", [P, 2, KT, P])
        gate_act = sb("gate_act", [P, 2, EH])
        hid = sb("hid", [P, 2, EH])
        hid_t = sb("hid_t", [P, 2, P])
        y_rows = [sb(f"y_rows{i}", [P, D]) for i in range(RING)]
        zero_rows = sb("zero_rows", [P, D])
        y_in = w_gu[:, :, :, :].rearrange("p e k n -> p (e k n)").rearrange("p (c t d) -> p c t d", c=TOPK, t=NT)
        part = xn[:, 0]

        h_rows = nc.dram_tensor("h_rows", (TOK, D), F32).ap()
        sorted_rows = nc.dram_tensor("sorted_rows", (TILES * P, D), F32).ap()
        y_dram = nc.dram_tensor("y_dram", (PAIRS, D), F32).ap()
        x_rows = a["x"].rearrange("b (st p) d -> b p st d", p=P)
        ctx_rows = a["ctx_t"].rearrange("b (kt p) t -> b p kt t", p=P)
        sorted_out = sorted_rows.rearrange("(t p) d -> p t d", p=P)
        h_out = h_rows.rearrange("(t p) d -> p t d", p=P)
        out_rows = out.rearrange("b (st p) d -> p (b st) d", p=P)
        y_rows_in = y_dram.rearrange("(c t p) d -> p c t d", c=TOPK, p=P)

        const_in = sem("const_in")
        attn_w_in = sem("attn_w_in")
        out_w_in = sem("out_w_in")
        route_const_in = sem("route_const_in")
        expert_w_in = sem("expert_w_in")
        entry_in = [sem("entry_in0"), sem("entry_in1")]
        set_up = sem("set_up")
        misc_full = sem("misc_full")
        misc_read = sem("misc_read")
        ln1_stats = sem("ln1_stats")
        ln2_stats = sem("ln2_stats")
        ln1_coeff = sem("ln1_coeff")
        ln2_coeff = sem("ln2_coeff")
        xn_ready = sem("xn_ready")
        h_ready = sem("h_ready")
        x_bo_ready = sem("x_bo_ready")
        h_free = [sem("h_free0"), sem("h_free1")]
        scores_full = sem("scores_full")
        scores_abs = sem("scores_abs")
        max_done = sem("max_done")
        parts_done = sem("parts_done")
        max_rows_done = sem("max_rows_done")
        probs_full = sem("probs_full")
        probs_done = sem("probs_done")
        x1_sum = sem("x1_sum")
        ln1_bn = sem("ln1_bn")
        ln2_bn = sem("ln2_bn")
        inv_sum_done = sem("inv_sum_done")
        ln1_link = sem("ln1_link")
        ln2_link = sem("ln2_link")
        split_link = sem("split_link")

        def in_steps(eng, step):
            step(Step(0, 0, 0, first=True))
            with eng.Fori(0, B // 2 - 1) as i:
                step(Step(i * 2 + 1, 1, i))
                step(Step(i * 2 + 2, 0, i + 1))
            step(LAST_STEP)

        def entry_half(s):
            return s.half + s.par

        rows_cleared = sem("rows_cleared")
        gap_done = sem("gap_done")
        gap_exp_done = sem("gap_exp_done")
        chosen_done = sem("chosen_done")
        rank_full = sem("rank_full")
        rank_read = sem("rank_read")
        pos_done = sem("pos_done")
        table_done = sem("table_done")
        route_link = sem("route_link")
        h_in = sem("h_in")
        rows_sorted = sem("rows_sorted")
        hot_done = sem("hot_done")
        hot_used = sem("hot_used")
        ids_done = sem("ids_done")
        sh_full = sem("sh_full")
        sh_act_done = sem("sh_act_done")
        sh_hid_done = sem("sh_hid_done")
        sh_down_full = sem("sh_down_full")
        sh_added = sem("sh_added")
        rows_in = [sem(f"rows_in{k}") for k in range(RING)]
        rows_t_full = sem("rows_t_full")
        rows_t_done = sem("rows_t_done")
        gu_full = sem("gu_full")
        gate_act_done = sem("gate_act_done")
        hid_done = sem("hid_done")
        hid_t_full = sem("hid_t_full")
        hid_t_done = sem("hid_t_done")
        y_full = sem("y_full")
        y_done = sem("y_done")
        carried = sem("carried")
        y_out = [sem(f"y_out{k}") for k in range(RING)]
        y_in_done = [sem(f"y_in_done{c}") for c in range(CHUNKS)]
        part_done = sem("part_done")
        out_done = sem("out_done")
        stored = sem("stored")

        BLOCKS, BT = 4, TOK // 4

        def tile_steps(eng, step):
            for i in range(PEEL):
                step(i, i % RING, i // RING)
            with eng.Fori(0, (TILES - 2 * PEEL) // RING) as r:
                for j in range(PEEL, PEEL + RING):
                    step(r * RING + j, j % RING, r + j // RING)
            for i in range(TILES - PEEL, TILES):
                step(i, i % RING, i // RING)

        def sp_experts(sp):
            for par in range(2):
                sp.wait_ge(h_free[par], 16 * (B // 2 + 1))
            for c in range(CHUNKS):
                tiles = slice(c * NT // CHUNKS, (c + 1) * NT // CHUNKS)
                sp.dma_start(h_all[:, tiles, :], h_out[:, tiles, :]).then_inc(h_in, 16)
            sp.wait_ge(rows_sorted, 16 * NT * TOPK)

            def load_rows(i, k):
                sp.dma_start(rows[k], sorted_out[:, bass.ds(i, 1), :].rearrange("p o d -> p (o d)")).then_inc(rows_in[k], 16)

            def step(i, k, r):
                if not (isinstance(i, int) and i + RING - 1 >= TILES):
                    if not (isinstance(i, int) and i == 0):
                        sp.wait_ge(rows_t_full, i)
                    load_rows(i + (RING - 1), (k + RING - 1) % RING)

            for i in range(RING - 1):
                load_rows(i, i)
            tile_steps(sp, step)
            for c in range(CHUNKS):
                if c == 0:
                    for k in range(RING):
                        sp.wait_ge(y_out[k], 16 * (TILES // RING))
                    sp.wait_ge(gu_full, TILES)
                tiles = slice(c * NT // CHUNKS, (c + 1) * NT // CHUNKS)
                for k in range(TOPK):
                    sp.dma_start(y_in[:, k, tiles, :], y_rows_in[:, k, tiles, :]).then_inc(y_in_done[c], 16)
            for c in range(CHUNKS):
                tiles = slice(c * NT // CHUNKS, (c + 1) * NT // CHUNKS)
                sp.wait_ge(out_done, (c + 1) * NT // CHUNKS)
                sp.dma_start(out_rows[:, tiles, :], x1[:, tiles, :]).then_inc(stored, 16)
            sp.wait_ge(stored, 16 * CHUNKS)

        def pool_experts(pool):
            pool.wait_ge(rows_cleared, 16 * TILES // 8)
            pool.wait_ge(pos_done, 1)
            for k in range(TOPK):
                for t in range(NT):
                    if k == 0 and t % (NT // CHUNKS) == 0:
                        pool.wait_ge(h_in, 16 * CHUNKS)
                    nc.gpsimd.indirect_dma_start(sorted_rows, bass.IndirectOffsetOnAxis(ap=pos_at[:, k, t:t + 1], axis=0),
                                                 h_all[:, t, :], None).then_inc(rows_sorted, 16)

            def step(i, k, r):
                pool.wait_ge(y_done, i * 2 + 2)
                nc.gpsimd.tensor_tensor(pool_carrier[:, k:k + 1], zeros[:, 0:1], zeros[:, 0:1], ALU.add).then_inc(carried, 1)
                nc.gpsimd.indirect_dma_start(y_dram, bass.IndirectOffsetOnAxis(ap=scatter_at[k][:, 0:1], axis=0),
                                             y_rows[k][:, :], None, bounds_check=PAIRS - 1, oob_is_err=False).then_inc(y_out[k], 16)

            tile_steps(pool, step)

        def dve_experts(dve):
            links = [0]

            def link(ins):
                ins.then_inc(route_link, 1)
                links[0] += 1
                dve.wait_ge(route_link, links[0])

            def choose():
                nc.vector.memset(ones_bf[:, :], 1.0)
                nc.vector.tensor_scalar(before[:, :], row_iota[:, :], row_number[:, 0:1], None, ALU.is_gt)
                dve.wait_ge(misc_read, END_USES + len(EPILOGUE))
                for t in range(NT):
                    last = nc.vector.max(top8[:, t, :], logits[:, t, :])
                link(last)
                for t in range(NT):
                    last = nc.vector.max_index(top8_at[:, t, :], top8[:, t, :], logits[:, t, :])
                link(last)
                nc.vector.tensor_tensor(gap[:, :], top8[:, :, 1], top8[:, :, 0], ALU.subtract).then_inc(gap_done, 1)
                link(nc.vector.tensor_copy(choice[:, :, :], top8_at[:, :, 0:TOPK]))
                for k in range(TOPK):
                    last = nc.vector.tensor_tensor(chosen[:, k], expert_iota[:, :].unsqueeze(1).to_broadcast([P, NT, E]),
                                                   choice[:, :, k].unsqueeze(2).to_broadcast([P, NT, E]), ALU.is_equal)
                link(last)
                nc.vector.tensor_tensor(chosen_any[:, :, :], chosen[:, 0], chosen[:, 1], ALU.add).then_inc(chosen_done, 1)

            def place():
                dve.wait_ge(rank_full, 1)
                counts = ps_misc[0][:, NT * E:NT * E + E]
                link(nc.vector.tensor_scalar(tiles_i[:, :], counts, float(P - 1), None, ALU.add))
                link(nc.vector.tensor_scalar(tiles_s[:, :], tiles_i[:, :], 7, None, ALU.arith_shift_right))
                link(nc.vector.tensor_copy(tiles_f[:, :], tiles_s[:, :]))
                link(nc.vector.tensor_tensor_scan(tiles_end[:, :], ones_f[:, :], tiles_f[:, :], 0.0, ALU.mult, ALU.add))
                link(nc.vector.tensor_tensor(row_start[:, :], tiles_end[:, :], tiles_f[:, :], ALU.subtract))
                link(nc.vector.tensor_scalar(row_start[:, :], row_start[:, :], float(P), None, ALU.mult))
                nc.vector.tensor_tensor(rank[:, :, :], ps_misc[0][:, 0:NT * E].rearrange("p (t e) -> p t e", e=E),
                                        row_start[:, :].unsqueeze(1).to_broadcast([P, NT, E]), ALU.add).then_inc(rank_read, 1)
                dve.wait_ge(rank_read, 1)
                for k in range(TOPK):
                    last = nc.vector.tensor_tensor(rank_of[:, k], chosen[:, k], rank[:, :, :], ALU.mult)
                link(last)
                link(nc.vector.tensor_reduce(pos_f[:, :, :].rearrange("p k t -> p (k t)"),
                                             rank_of[:, :, :, :].rearrange("p k t e -> p (k t) e"), AX.X, ALU.add))
                link(nc.vector.tensor_copy(pos_i[:, :, :], pos_f[:, :, :]))
                nc.vector.tensor_copy(pos_at[:, :, :], pos_f[:, :, :]).then_inc(pos_done, 1)
                nc.vector.tensor_scalar(pos_lo[:, :, :], pos_i[:, :, :], P - 1, None, ALU.bitwise_and)
                link(nc.vector.tensor_scalar(pos_hi[:, :, :], pos_i[:, :, :], 7, None, ALU.arith_shift_right))
                link(nc.vector.tensor_copy(pos_lof[:, :, :], pos_lo[:, :, :]))
                link(nc.vector.tensor_copy(pos_hif[:, :, :], pos_hi[:, :, :]))
                link(nc.vector.tensor_tensor(past[:, :, :], tile_iota[:, :].unsqueeze(2).to_broadcast([P, TILES, E]),
                                             tiles_end[:, :].unsqueeze(1).to_broadcast([P, TILES, E]), ALU.is_ge))
                link(nc.vector.tensor_reduce(tile_expert_f[:, :], past[:, :, :], AX.X, ALU.add))
                nc.vector.tensor_scalar(tile_expert[:, :], tile_expert_f[:, :], float(E - 1), None, ALU.min).then_inc(table_done, 1)
                dve.wait_ge(gap_exp_done, 1)
                link(nc.vector.tensor_scalar(gap_sum[:, :], gap_exp[:, :], 1.0, None, ALU.add))
                link(nc.vector.reciprocal(weight[:, 0, :], gap_sum[:, :]))
                link(nc.vector.tensor_tensor(weight[:, 1, :], weight[:, 0, :], gap_exp[:, :], ALU.mult))

            def invert():
                for n in range(TOPK * NT):
                    k, t = n // NT, n % NT
                    if n >= HOTS:
                        dve.wait_ge(hot_used, n - HOTS + 1)
                    nc.vector.tensor_scalar(hot_row[:, n % HOTS, :], row_iota[:, :], pos_lof[:, k, t:t + 1], None, ALU.is_equal)
                    nc.vector.tensor_scalar(hot_tile[:, n % HOTS, 0, :], tile_iota[:, :], pos_hif[:, k, t:t + 1], float(n),
                                            ALU.is_equal, ALU.mult)
                    nc.vector.tensor_scalar(hot_tile[:, n % HOTS, 1, :], tile_iota[:, :], pos_hif[:, k, t:t + 1],
                                            row_number[:, 0:1], ALU.is_equal, ALU.mult)
                    nc.vector.tensor_scalar(hot_tile[:, n % HOTS, 2, :], tile_iota[:, :], pos_hif[:, k, t:t + 1], None,
                                            ALU.is_equal).then_inc(hot_done, 1)

            def pair_numbers():
                sums = ps_misc[1][:, 0:3 * TILES].rearrange("p (c t) -> p c t", c=3)
                dve.wait_ge(hot_used, TOPK * NT)
                link(nc.vector.tensor_copy(id_sums[:, :, :], sums))
                link(nc.vector.scalar_tensor_tensor(id_sums[:, 0, :], id_sums[:, 0, :], float(P), id_sums[:, 1, :], ALU.mult, ALU.add))
                link(nc.vector.scalar_tensor_tensor(id_sums[:, 0, :], id_sums[:, 2, :], float(-PAIRS), id_sums[:, 0, :],
                                                    ALU.mult, ALU.add))
                nc.vector.tensor_scalar(ids[:, :], id_sums[:, 0, :], float(PAIRS), None, ALU.add).then_inc(ids_done, 1)

            def shared_hidden(bl):
                for m in range(KT):
                    dve.wait_ge(sh_act_done, bl * KT + m + 1)
                    dve.wait_ge(sh_full, bl * 2 * KT + KT + m + 1)
                    nc.vector.tensor_tensor(sh_hid[:, bl % 2, m, :], ps[:, KT + m, :], sh_act[:, bl % 2, m, :],
                                            ALU.mult).then_inc(sh_hid_done, 1)

            def shared_add(bl):
                for hf in range(2):
                    tiles = slice(bl * 4 + 2 * hf, bl * 4 + 2 * hf + 2)
                    dve.wait_ge(sh_down_full, bl * 2 + hf + 1)
                    nc.vector.tensor_tensor(x1[:, tiles, :], ps_probs[hf].rearrange("p (t d) -> p t d", t=2), x1[:, tiles, :],
                                            ALU.add).then_inc(sh_added, 1)

            dve.wait_ge(route_const_in, 64)
            choose()
            shared_hidden(0)
            place()
            shared_hidden(1)
            shared_add(0)
            invert()
            shared_hidden(2)
            shared_add(1)
            pair_numbers()
            shared_hidden(3)
            shared_add(2)
            shared_add(3)
            dve.wait_ge(ids_done, 1)

            def hidden(i, k):
                dve.wait_ge(gate_act_done, i + 1)
                if not (isinstance(i, int) and i < 2):
                    dve.wait_ge(hid_t_full, i - 1)
                nc.vector.tensor_tensor(hid[:, k % 2, :], ps[:, 2 + k % 2, EH:2 * EH], gate_act[:, k % 2, :],
                                        ALU.mult).then_inc(hid_done, 1)

            def hidden_t(i, k):
                dve.wait_ge(hid_t_full, i + 1)
                if not (isinstance(i, int) and i < 2):
                    dve.wait_ge(y_full, i - 1)
                nc.vector.tensor_copy(hid_t[:, k % 2, :], ps[:, 4 + k % 2, 0:P]).then_inc(hid_t_done, 1)

            def result(i, k, r):
                dve.wait_ge(y_full, i + 1)
                if not (isinstance(i, int) and i < RING):
                    dve.wait_ge(y_out[k], r * 16)
                    dve.wait_ge(carried, i + 1)
                nc.vector.tensor_copy(y_rows[k][:, :], ps[:, 6 + k % 2, 0:D]).then_inc(y_done, 1)
                nc.vector.tensor_copy(scatter_at[k][:, :], ids[:, bass.ds(i, 1)]).then_inc(y_done, 1)

            def step(i, k, r):
                static = isinstance(i, int)
                hidden(i, k)
                if not (static and i < 1):
                    hidden_t(i - 1, k - 1)
                if not (static and i < 2):
                    result(i - 2, (k - 2) % RING, r if k >= 2 else r - 1)

            tile_steps(dve, step)
            hidden_t(TILES - 1, TILES - 1)
            for i in (TILES - 2, TILES - 1):
                result(i, i % RING, i // RING)

            for t in range(NT):
                if t % (NT // CHUNKS) == 0:
                    dve.wait_ge(y_in_done[t // (NT // CHUNKS)], 16 * TOPK)
                if t >= 2:
                    dve.wait_ge(out_done, t - 1)
                nc.vector.scalar_tensor_tensor(part[:, t % 2, :], y_in[:, 0, t, :], weight[:, 0, t:t + 1], x1[:, t, :],
                                               ALU.mult, ALU.add).then_inc(part_done, 1)
                if t:
                    combine(dve, t - 1)
            combine(dve, NT - 1)

        def combine(dve, t):
            dve.wait_ge(part_done, t + 1)
            nc.vector.scalar_tensor_tensor(x1[:, t, :], y_in[:, 1, t, :], weight[:, 1, t:t + 1], part[:, t % 2, :],
                                           ALU.mult, ALU.add).then_inc(out_done, 1)

        def act_experts(act):
            act.wait_ge(gap_done, 1)
            nc.scalar.activation(gap_exp[:, :], gap[:, :], ACT.Exp).then_inc(gap_exp_done, 1)
            for bl in range(BLOCKS):
                for m in range(KT):
                    act.wait_ge(sh_full, bl * 2 * KT + m + 1)
                    if bl >= 2:
                        act.wait_ge(sh_hid_done, (bl - 2) * KT + m + 1)
                    nc.scalar.activation(sh_act[:, bl % 2, m, :], ps[:, m, :], ACT.Silu).then_inc(sh_act_done, 1)

            def rows_to_sbuf(i, k):
                act.wait_ge(rows_t_full, i + 1)
                if not (isinstance(i, int) and i < 2):
                    act.wait_ge(gu_full, i - 1)
                nc.scalar.activation(rows_t[:, k % 2].rearrange("p k n -> p (k n)"), ps[:, k % 2, 0:D], ACT.Copy).then_inc(rows_t_done, 1)

            def gate(i, k):
                act.wait_ge(gu_full, i + 1)
                if not (isinstance(i, int) and i < 2):
                    act.wait_ge(hid_done, i - 1)
                nc.scalar.activation(gate_act[:, k % 2, :], ps[:, 2 + k % 2, 0:EH], ACT.Silu).then_inc(gate_act_done, 1)

            rows_to_sbuf(0, 0)

            def step(i, k, r):
                gate(i, k)
                if not (isinstance(i, int) and i == TILES - 1):
                    rows_to_sbuf(i + 1, k + 1)

            tile_steps(act, step)

        def pe_experts(pe):
            def shared_gate_up(bl):
                if bl:
                    pe.wait_ge(sh_hid_done, bl * KT)
                for m in range(2 * KT):
                    for k in range(KT):
                        last = nc.tensor.matmul(ps[:, m, :], sh_gu[:, k, m * P:m * P + P], h_t[:, k, bl * BT:bl * BT + BT],
                                                start=(k == 0), stop=(k == KT - 1))
                    last.then_inc(sh_full, 1)

            def shared_down(bl):
                pe.wait_ge(sh_hid_done, (bl + 1) * KT)
                for hf in range(2):
                    if bl:
                        pe.wait_ge(sh_added, (bl - 1) * 2 + hf + 1)
                    for t in range(2):
                        at = (2 * hf + t) * P
                        for k in range(KT):
                            last = nc.tensor.matmul(ps_probs[hf][:, t * D:t * D + D], sh_hid[:, bl % 2, k, at:at + P],
                                                    sh_d[:, k, :], start=(k == 0), stop=(k == KT - 1))
                    last.then_inc(sh_down_full, 1)

            def ranks():
                pe.wait_ge(route_const_in, 64)
                pe.wait_ge(chosen_done, 1)
                dst = ps_misc[0]
                nc.tensor.matmul(dst[:, 0:NT * E], before[:, :], chosen_any[:, :, :].rearrange("p t e -> p (t e)"),
                                 start=True, stop=False, skip_group_check=True)
                for t in range(NT):
                    last = nc.tensor.matmul(dst[:, (t + 1) * E:(NT + 1) * E].rearrange("p (t e) -> p t e", e=E), ones_bf[:, :],
                                            chosen_any[:, t, :].unsqueeze(1).to_broadcast([P, NT - t, E]),
                                            start=False, stop=(t == NT - 1), skip_group_check=True)
                last.then_inc(rank_full, 1)

            pe.wait_ge(misc_read, END_USES + len(EPILOGUE))
            pe.wait_ge(expert_w_in, 96)
            def invert():
                pe.wait_ge(misc_read, END_USES + len(EPILOGUE))
                for n in range(TOPK * NT):
                    pe.wait_ge(hot_done, n + 1)
                    last = nc.tensor.matmul(ps_misc[1][:, 0:3 * TILES], hot_row[:, n % HOTS, :],
                                            hot_tile[:, n % HOTS].rearrange("p c t -> p (c t)"),
                                            start=(n == 0), stop=(n == TOPK * NT - 1))
                    last.then_inc(hot_used, 1)

            shared_gate_up(0)
            ranks()
            shared_gate_up(1)
            shared_down(0)
            shared_gate_up(2)
            invert()
            shared_down(1)
            shared_gate_up(3)
            shared_down(2)
            shared_down(3)

            def expert_of(i):
                return pe.value_load(tile_expert[0:1, bass.ds(i, 1)], min_val=0, max_val=E - 1)

            def rows_transpose(i, k, r):
                pe.wait_ge(rows_in[k], r * 16 + 16)
                if not (isinstance(i, int) and i < 2):
                    pe.wait_ge(rows_t_done, i - 1)
                for c in range(KT):
                    last = nc.tensor.transpose(ps[:, k % 2, c * P:c * P + P], rows[k][:, c * P:c * P + P], ident[:, :])
                last.then_inc(rows_t_full, 1)

            def gate_up(i, k):
                e = expert_of(i)
                pe.wait_ge(rows_t_done, i + 1)
                if not (isinstance(i, int) and i < 2):
                    pe.wait_ge(hid_done, i - 1)
                for c in range(KT):
                    last = nc.tensor.matmul(ps[:, 2 + k % 2, 0:2 * EH], rows_t[:, k % 2, c, :],
                                            w_gu[:, bass.ds(e, 1), c, :].rearrange("p o n -> p (o n)"),
                                            start=(c == 0), stop=(c == KT - 1))
                last.then_inc(gu_full, 1)

            def hidden_transpose(i, k):
                pe.wait_ge(hid_done, i + 1)
                if not (isinstance(i, int) and i < 2):
                    pe.wait_ge(hid_t_done, i - 1)
                nc.tensor.transpose(ps[:, 4 + k % 2, 0:P], hid[:, k % 2, :], ident[:, :]).then_inc(hid_t_full, 1)

            def down(i, k):
                e = expert_of(i)
                pe.wait_ge(hid_t_done, i + 1)
                if not (isinstance(i, int) and i < 2):
                    pe.wait_ge(y_done, i * 2 - 3)
                nc.tensor.matmul(ps[:, 6 + k % 2, 0:D], hid_t[:, k % 2, :],
                                 w_d[:, bass.ds(e, 1), :].rearrange("p o n -> p (o n)"), start=True, stop=True).then_inc(y_full, 1)

            pe.wait_ge(table_done, 1)
            pe.wait_ge(rank_read, 1)
            pe.wait_ge(sh_added, BLOCKS * 2)
            rows_transpose(0, 0, 0)

            def step(i, k, r):
                static = isinstance(i, int)
                gate_up(i, k)
                if not (static and i == TILES - 1):
                    rows_transpose(i + 1, (k + 1) % RING, r + (k + 1) // RING)
                if not (static and i < 1):
                    hidden_transpose(i - 1, k - 1)
                if not (static and i < 2):
                    down(i - 2, k - 2)

            tile_steps(pe, step)
            hidden_transpose(TILES - 1, TILES - 1)
            down(TILES - 2, TILES - 2)
            down(TILES - 1, TILES - 1)

        block = ctx.enter_context(nc.Block())

        @block.sync
        def _(sp):
            def load_entry(b, par):
                sp.dma_start(x_in[:, par], x_rows[bass.ds(b, 1)].rearrange("o p st d -> p (o st) d")).then_inc(entry_in[par], 16)
                sp.dma_start(ctx_t[:, par], ctx_rows[bass.ds(b, 1)].rearrange("o p kt t -> p (o kt) t")).then_inc(entry_in[par], 16)

            def load_entry_when_free(b, par):
                sp.wait_ge(xn_ready, b - 1)
                sp.wait_ge(x_bo_ready, b - 1)
                sp.wait_ge(scores_full, b * NU - 2 * NU + 2)
                load_entry(b, par)

            def store_h(b, par):
                sp.wait_ge(h_ready, b + 1)
                sp.dma_start(h_out[:, bass.ds(b * ST, ST), :], h[:, par]).then_inc(h_free[par], 16)

            split_rows = lambda name: a[name].rearrange("(kt p) n -> p kt n", p=P)
            load_entry(0, 0)
            sp.dma_start(ident[:, :], a["ident"]).then_inc(const_in, 16)
            for dst, name in ((wq, "wq"), (wk, "wk"), (wv, "wv")):
                sp.dma_start(dst[:, :, :], split_rows(name)).then_inc(attn_w_in, 16)
            sp.dma_start(bq[:, :], a["bq"]).then_inc(attn_w_in, 16)
            sp.dma_start(bk[:, :], a["bk"]).then_inc(attn_w_in, 16)
            sp.dma_start(bv[:, :], a["bv"].to_broadcast([P, D])).then_inc(attn_w_in, 16)
            sp.dma_start(head_mask[:, :], a["head_mask"]).then_inc(const_in, 16)
            sp.dma_start(part_mask[:, :], a["part_mask"]).then_inc(const_in, 16)
            sp.dma_start(bo[:, :], a["bo"].to_broadcast([P, D])).then_inc(out_w_in, 16)
            load_entry(1, 1)
            sp.dma_start(wo[:, :, :], split_rows("wo")).then_inc(out_w_in, 16)
            sp.dma_start(rw[:, :, :], split_rows("rw")).then_inc(out_w_in, 16)
            sp.dma_start(rb[:, :], a["rb"].to_broadcast([P, E])).then_inc(out_w_in, 16)
            sp.wait_ge(set_up, 10)
            for c in range(TILES // 8):
                sp.dma_start(sorted_out[:, 8 * c:8 * c + 8, :], zero_rows[:, :].unsqueeze(1).to_broadcast([P, 8, D])).then_inc(rows_cleared, 16)
            load_entry_when_free(2, 0)
            for dst, name in ((expert_iota, "expert_iota"), (tile_iota, "tile_iota"), (row_iota, "row_iota"), (row_number, "row_number")):
                sp.dma_start(dst[:, :], a[name]).then_inc(route_const_in, 16)
            sp.dma_start(sh_gu[:, :, 0:D], split_rows("sh_gate")).then_inc(expert_w_in, 16)
            sp.dma_start(sh_gu[:, :, D:2 * D], split_rows("sh_up")).then_inc(expert_w_in, 16)
            sp.dma_start(sh_d[:, :, :], split_rows("sh_down")).then_inc(expert_w_in, 16)
            load_entry_when_free(3, 1)
            for name, at in (("gate", 0), ("up", EH)):
                sp.dma_start(w_gu[:, :, :, at:at + EH].rearrange("p e k n -> p (e k) n"),
                             a[name].rearrange("e (kt p) n -> p (e kt) n", p=P)).then_inc(expert_w_in, 16)
            sp.dma_start(w_d[:, :, :], a["down"].rearrange("e p n -> p e n")).then_inc(expert_w_in, 16)
            with sp.Fori(0, B // 2 - 2) as i:
                for par in range(2):
                    store_h(i * 2 + par, par)
                    load_entry_when_free(i * 2 + (4 + par), par)
            for b in range(B - 4, B):
                store_h(b, b % 2)
            sp_experts(sp)

        @block.gpsimd
        def _(pool):
            nc.gpsimd.memset(minus_half[:, :], -0.5).then_inc(set_up, 1)
            nc.gpsimd.memset(eps_tile[:, :], EPS).then_inc(set_up, 1)
            nc.gpsimd.memset(zeros[:, :], 0.0).then_inc(set_up, 1)
            nc.gpsimd.memset(pool_carrier[:, :], 0.0).then_inc(carried, RING)
            nc.gpsimd.memset(zero_rows[:, :], 0.0).then_inc(set_up, 1)
            nc.gpsimd.memset(max_parts[:, :, :, :], 0.0).then_inc(set_up, 1)
            nc.gpsimd.memset(max_rows[:, :, :, :], 0.0).then_inc(set_up, 1)
            nc.gpsimd.memset(v_one[:, :, :, :, HD:SLOT].rearrange("p a t h n -> p (a t h) n"), 0.0).then_inc(set_up, 1)
            nc.gpsimd.memset(ones_f[:, :], 1.0).then_inc(set_up, 1)
            pool.wait_ge(set_up, 8)
            pool.wait_ge(carried, RING)
            nc.gpsimd.memset(v_one[:, :, :, :, HD:HD + 1].rearrange("p a t h n -> p (a t h) n"), 1.0).then_inc(set_up, 1)
            pool.wait_ge(const_in, 48)
            nc.gpsimd.tensor_copy(onehot[:, :, :], part_mask[:, :].unsqueeze(2).to_broadcast([P, 4, P])).then_inc(set_up, 1)
            nc.gpsimd.memset(start_marks[:, 0:1], 0.0).then_inc(h_free[0], 16)
            nc.gpsimd.memset(start_marks[:, 1:2], 0.0).then_inc(h_free[1], 16)
            pool.wait_ge(h_free[0], 16)
            pool.wait_ge(h_free[1], 16)

            def layernorm(ln, b, stats_sem, link, ready):
                pool.wait_ge(stats_sem, b + 1)
                nc.gpsimd.tensor_tensor(ln_var[:, ln], ln_mv[:, ln, :, 1], eps_tile[:, :], ALU.add).then_inc(link, 1)
                pool.wait_ge(link, b * 3 + 1)
                nc.gpsimd.tensor_tensor(ln_rstd[:, ln], ln_var[:, ln], minus_half[:, :], ALU.pow).then_inc(link, 1)
                pool.wait_ge(link, b * 3 + 2)
                nc.gpsimd.tensor_tensor(ln_var[:, ln], ln_mv[:, ln, :, 0], ln_rstd[:, ln], ALU.mult).then_inc(link, 1)
                pool.wait_ge(link, b * 3 + 3)
                nc.gpsimd.tensor_tensor(ln_shift[:, ln], zeros[:, 0:ST], ln_var[:, ln], ALU.subtract).then_inc(ready, 1)

            def layernorm_1(b):
                layernorm(0, b, ln1_stats, ln1_link, ln1_coeff)

            def layernorm_2(b):
                layernorm(1, b, ln2_stats, ln2_link, ln2_coeff)

            def add_bo(par):
                for t in range(ST):
                    last = nc.gpsimd.tensor_tensor(x_bo[:, par, t, :], x_in[:, par, t, :], bo[:, :], ALU.add)
                last.then_inc(x_bo_ready, 1)

            def split_max(n, par):
                in_cols = lambda k: max_parts[:, par, :, 4 * k:4 * k + 4].rearrange("p t j -> p j t")
                flat = lambda t: t[:, par, :].rearrange("p (j t) -> p j t", t=ST)
                zero = zeros[:, :].rearrange("p (j t) -> p j t", t=ST)
                pool.wait_ge(max_done, n + 1)
                nc.gpsimd.tensor_tensor(in_cols(0), flat(neg_max), zero, ALU.add).then_inc(split_link, 1)
                pool.wait_ge(split_link, n * 3 + 1)
                nc.gpsimd.tensor_tensor(flat(rest1), flat(neg_max), in_cols(0), ALU.subtract).then_inc(split_link, 1)
                pool.wait_ge(split_link, n * 3 + 2)
                nc.gpsimd.tensor_tensor(in_cols(1), flat(rest1), zero, ALU.add).then_inc(split_link, 1)
                pool.wait_ge(split_link, n * 3 + 3)
                nc.gpsimd.tensor_tensor(in_cols(2), flat(rest1), in_cols(1), ALU.subtract).then_inc(parts_done, 1)

            layernorm_1(0)
            pool.wait_ge(out_w_in, 64)
            add_bo(0)
            split_max(0, 0)

            def step(s):
                nxt = 1 - s.par
                for u in range(NU):
                    if u == 0 and not s.last:
                        layernorm_1(s.b + 1)
                    if not (s.last and u == NU - 1):
                        split_max(s.b * NU + (u + 1), (u + 1) % 2)
                    if u == 1 and not s.first:
                        layernorm_2(s.b - 1)
                    if u == NU - 1 and not s.last:
                        if not s.first:
                            pool.wait_ge(h_ready, s.b)
                        add_bo(nxt)

            in_steps(pool, step)
            layernorm_2(B - 1)
            pool_experts(pool)

        @block.vector
        def _(dve):
            def stats(b, ln, src, bn_done, done):
                for t in range(ST):
                    nc.vector.bn_stats(ln_stats[:, ln, t, :], src[:, t, :]).then_inc(bn_done, 1)
                dve.wait_ge(bn_done, b * ST + ST)
                nc.vector.memset(dve_carrier[:, :], 0.0)
                for t in range(ST):
                    last = nc.vector.bn_aggr(ln_mv[:, ln, t, :], ln_stats[:, ln, t, :])
                last.then_inc(done, 1)

            def stats_1(b, par, half):
                dve.wait_ge(entry_in[par], half * 32 + 32)
                stats(b, 0, x_in[:, par], ln1_bn, ln1_stats)

            def row_max(n, par):
                dve.wait_ge(scores_abs, n + 1)
                nc.vector.tensor_reduce(neg_max[:, par, :], scores[:, par].rearrange("p j t k -> p (j t) k"),
                                        AX.X, ALU.max, negate=True).then_inc(max_done, 1)

            def max_to_rows(n, par):
                dve.wait_ge(parts_done, n + 1)
                for q in range(4):
                    for t in range(ST):
                        last = nc.vector.transpose(max_rows[32 * q:32 * q + 32, par, t, 32 * q:32 * q + 32],
                                                   max_parts[32 * q:32 * q + 32, par, t, :])
                last.then_inc(max_rows_done, 1)

            def unit_out(number, bank, u):
                dve.wait_ge(misc_full, number + 1)
                nc.vector.tensor_copy(o_slots[:, u, :], ps_misc[bank][:, 0:S]).then_inc(misc_read, 1)

            def evacuate(name, number, bank, b, par, half):
                src = ps_misc[bank]
                dve.wait_ge(misc_full, number + 1)
                if name == "p_x":
                    nc.vector.tensor_copy(xn_t[:, par].rearrange("p k s -> p (k s)"), src).then_inc(misc_read, 1)
                elif name == "p_q":
                    for g in range(2):
                        last = nc.vector.tensor_scalar(q_t[:, par, g, :], src[:, g * S:g * S + S], bq[:, g:g + 1],
                                                       None, ALU.add)
                    last.then_inc(misc_read, 1)
                elif name == "p_k":
                    for g in range(2):
                        for r in range(2):
                            last = nc.vector.tensor_scalar(k_t[:, par, g, r, :], src[:, g * S:g * S + S], bk[:, g:g + 1],
                                                           head_mask[:, r:r + 1], ALU.add, ALU.mult)
                    last.then_inc(misc_read, 1)
                elif name == "p_v":
                    for t in range(ST):
                        last = nc.vector.tensor_tensor(v_one[:, par, t, :, 0:HD],
                                                       src[:, t * D:t * D + D].rearrange("p (h n) -> p h n", h=H),
                                                       bv[:, :].rearrange("p (h n) -> p h n", h=H), ALU.add)
                    last.then_inc(misc_read, 1)
                elif name in ("f_slots0", "f_slots1"):
                    t = int(name[-1])
                    heads = src.rearrange("p (h n) -> p h n", h=H)
                    nc.vector.reciprocal(inv_sum[:, t, :], heads[:, :, HD]).then_inc(inv_sum_done, 1)
                    dve.wait_ge(inv_sum_done, b * ST + (t + 1))
                    nc.vector.tensor_tensor(o_norm[:, t, :].rearrange("p (h n) -> p h n", h=H), heads[:, :, 0:HD],
                                            inv_sum[:, t, :].unsqueeze(2).to_broadcast([P, H, HD]),
                                            ALU.mult).then_inc(misc_read, 1)
                elif name == "f_heads":
                    nc.vector.tensor_copy(o_t[:, :, :].rearrange("p k s -> p (k s)"), src).then_inc(misc_read, 1)
                elif name == "f_out":
                    dve.wait_ge(x_bo_ready, b + 1)
                    nc.vector.tensor_tensor(x_bo[:, par], src.rearrange("p (t d) -> p t d", t=ST), x_bo[:, par],
                                            ALU.add).then_inc(x1_sum, 1)
                    dve.wait_ge(x1_sum, b + 1)
                    nc.vector.tensor_copy(x1[:, bass.ds(b * ST, ST), :], x_bo[:, par]).then_inc(misc_read, 1)
                    stats(b, 1, x_bo[:, par], ln2_bn, ln2_stats)
                elif name == "f_h":
                    nc.vector.tensor_copy(h_tp[:, par].rearrange("p k s -> p (k s)"), src)
                    nc.vector.tensor_copy(h_t[:, :, bass.ds(b * S, S)], src.rearrange("p (k s) -> p k s", k=KT)).then_inc(misc_read, 1)
                elif name == "f_router":
                    nc.vector.tensor_tensor(logits[:, bass.ds(b * ST, ST), :],
                                            src[:, 0:ST * E].rearrange("p (t e) -> p t e", t=ST),
                                            rb[:, :].unsqueeze(1).to_broadcast([P, ST, E]), ALU.add).then_inc(misc_read, 1)

            dve.wait_ge(const_in, 48)
            dve.wait_ge(attn_w_in, 96)
            dve.wait_ge(set_up, 10)
            stats_1(0, 0, 0)
            for k, name in enumerate(PROLOGUE):
                evacuate(name, k, k % MISC, 0, 0, 0)
            row_max(0, 0)
            max_to_rows(0, 0)

            def step(s):
                nxt = 1 - s.par
                for u, (before_t, between_t) in enumerate(PLAN):
                    n = s.b * NU + u
                    if u > 0:
                        unit_out(s.number(f"o{u - 1}"), s.bank(f"o{u - 1}"), u - 1)
                    elif not s.first:
                        unit_out(s.number(s.uses[0]) - 1, (s.bank(s.uses[0]) + 1) % MISC, NU - 1)
                    for name in before_t:
                        do(s, name, nxt)
                    if u == 0 and not s.last:
                        stats_1(s.b + 1, nxt, entry_half(s))
                    if not (s.last and u == NU - 1):
                        row_max(n + 1, (u + 1) % 2)
                    for name in between_t:
                        do(s, name, nxt)
                    if s.first and u == 0:
                        dve.wait_ge(out_w_in, 64)
                    if not (s.last and u == NU - 1):
                        max_to_rows(n + 1, (u + 1) % 2)

            def do(s, name, nxt):
                if s.has(name):
                    b = s.b + 1 if name[0] == "p" else s.b - 1
                    evacuate(name, s.number(name), s.bank(name), b, nxt, None)

            in_steps(dve, step)
            unit_out(END_USES - 1, (END_USES - 1) % MISC, NU - 1)
            for k, name in enumerate(EPILOGUE):
                evacuate(name, END_USES + k, k % MISC, B - 1, 1, None)
            dve_experts(dve)

        @block.scalar
        def _(act):
            def take_abs(n, par):
                act.wait_ge(scores_full, n + 1)
                nc.scalar.activation(scores[:, par].rearrange("p j t k -> p (j t k)"),
                                     ps_scores.rearrange("p j n -> p (j n)"), ACT.Abs).then_inc(scores_abs, 1)

            def take_exp(n, s):
                act.wait_ge(probs_full, n * 4 + (s + 1))
                nc.scalar.activation(probs[:, s].rearrange("p j q -> p (j q)"), ps_probs[s % 2], ACT.Exp,
                                     scale=SCALE).then_inc(probs_done, 1)

            def normalise(ln, b, coeff, src, dst, ready):
                act.wait_ge(coeff, b + 1)
                for t in range(ST):
                    last = nc.scalar.activation(dst[:, t, :], src[:, t, :], ACT.Identity, scale=ln_rstd[:, ln, t:t + 1],
                                                bias=ln_shift[:, ln, t:t + 1])
                last.then_inc(ready, 1)

            def normalise_2(b, par, half):
                act.wait_ge(h_free[par], half * 16 + 16)
                normalise(1, b, ln2_coeff, x_bo[:, par], h[:, par], h_ready)

            act.wait_ge(entry_in[0], 32)
            normalise(0, 0, ln1_coeff, x_in[:, 0], xn[:, 0], xn_ready)
            take_abs(0, 0)

            def step(s):
                nxt = 1 - s.par
                for u in range(NU):
                    n = s.b * NU + u
                    if u == 1 and not s.last:
                        act.wait_ge(entry_in[nxt], entry_half(s) * 32 + 32)
                        normalise(0, s.b + 1, ln1_coeff, x_in[:, nxt], xn[:, nxt], xn_ready)
                    if not (s.last and u == NU - 1):
                        take_abs(n + 1, (u + 1) % 2)
                    for k in range(4):
                        take_exp(n, k)
                    if u == 2 and not s.first:
                        normalise_2(s.b - 1, nxt, entry_half(s) - 1)

            in_steps(act, step)
            normalise_2(B - 1, 1, (B - 1) // 2)
            act_experts(act)

        @block.tensor
        def _(pe):
            def transposes(dst, sources):
                for i, src in enumerate(sources):
                    last = nc.tensor.transpose(dst[:, i * P:i * P + P], src, ident[:, :])
                return last

            def shared_use(name, number, bank, b, par):
                dst = ps_misc[bank]
                if not (isinstance(number, int) and number < MISC):
                    pe.wait_ge(misc_read, number + (1 - MISC))
                if name == "p_x":
                    pe.wait_ge(xn_ready, b + 1)
                    last = transposes(dst, [xn[:, par, t, k * P:k * P + P] for k in range(KT) for t in range(ST)])
                elif name in ("p_q", "p_k"):
                    w, src = (wq, xn_t) if name == "p_q" else (wk, ctx_t)
                    for g in range(2):
                        for k in range(KT):
                            last = nc.tensor.matmul(dst[:, g * S:g * S + S], w[:, k, g * P:g * P + P], src[:, par, k, :],
                                                    start=(k == 0), stop=(k == KT - 1))
                elif name == "p_v":
                    for t in range(ST):
                        for k in range(KT):
                            last = nc.tensor.matmul(dst[:, t * D:t * D + D], ctx_t[:, par, k, t * P:t * P + P], wv[:, k, :],
                                                    start=(k == 0), stop=(k == KT - 1))
                elif name in ("f_slots0", "f_slots1"):
                    t = int(name[-1])
                    if t == 0:
                        pe.wait_ge(misc_read, number)
                    last = transposes(dst, [o_slots[:, u, t * P:t * P + P] for u in range(NU)])
                elif name == "f_heads":
                    last = transposes(dst, [o_norm[:, t, k * P:k * P + P] for k in range(KT) for t in range(ST)])
                elif name == "f_out":
                    pe.wait_ge(misc_read, number)
                    for t in range(ST):
                        for k in range(KT):
                            last = nc.tensor.matmul(dst[:, t * D:t * D + D], o_t[:, k, t * P:t * P + P], wo[:, k, :],
                                                    start=(k == 0), stop=(k == KT - 1))
                elif name == "f_h":
                    pe.wait_ge(h_ready, b + 1)
                    last = transposes(dst, [h[:, par, t, k * P:k * P + P] for k in range(KT) for t in range(ST)])
                elif name == "f_router":
                    pe.wait_ge(misc_read, number)
                    for t in range(ST):
                        for k in range(KT):
                            last = nc.tensor.matmul(dst[:, t * E:t * E + E], h_tp[:, par, k, t * P:t * P + P], rw[:, k, :],
                                                    start=(k == 0), stop=(k == KT - 1))
                last.then_inc(misc_full, 1)

            def unit_scores(n, u, par):
                if not (isinstance(n, int) and n == 0):
                    pe.wait_ge(scores_abs, n)
                for t in range(ST):
                    for j in range(4):
                        rows32 = slice(SLOT * j, SLOT * j + SLOT)
                        last = nc.tensor.matmul(ps_scores[:, j, t * S:t * S + S],
                                                q_t[rows32, par, u // 2, t * P:t * P + P],
                                                k_t[rows32, par, u // 2, u % 2, :], start=True, stop=True)
                last.then_inc(scores_full, 1)

            def unit_transposes(n, u, s):
                key_tile, pair = s // 2, s % 2
                dst = ps_probs[s % 2]
                if s == 0:
                    pe.wait_ge(scores_abs, n + 1)
                if isinstance(n, int) and n * 4 + s < 2:
                    pass
                else:
                    pe.wait_ge(probs_done, n * 4 + (s - 1))
                for jj in range(2):
                    for t in range(ST):
                        at = jj * S + t * P
                        nc.tensor.matmul(dst[:, at:at + P], scores[:, u % 2, 2 * pair + jj, t, key_tile * P:key_tile * P + P],
                                         ident[:, :], start=(at == 0), stop=False, is_transpose=True, skip_group_check=True)
                if s == 0:
                    pe.wait_ge(max_rows_done, n + 1)
                for jj in range(2):
                    j = 2 * pair + jj
                    last = nc.tensor.matmul(dst[:, jj * S:jj * S + S], onehot[:, j, :],
                                            max_rows[:, u % 2].rearrange("p t q -> p (t q)"), start=False, stop=True,
                                            skip_group_check=True)
                last.then_inc(probs_full, 1)

            def unit_values(n, u, par, key_tile, number, bank):
                if key_tile == 0:
                    pe.wait_ge(misc_read, number + (1 - MISC) if not (isinstance(n, int) and n == 0) else len(PROLOGUE))
                pe.wait_ge(probs_done, n * 4 + (2 * key_tile + 2))
                for j in range(4):
                    last = nc.tensor.matmul(ps_misc[bank][SLOT * j:SLOT * j + SLOT, 0:S], v_one[:, par, key_tile, 4 * u + j, :],
                                            probs[:, 2 * key_tile + j // 2, j % 2, :],
                                            start=(key_tile == 0), stop=(key_tile == 1), skip_group_check=True)
                if key_tile == 1:
                    last.then_inc(misc_full, 1)

            pe.wait_ge(const_in, 48)
            pe.wait_ge(attn_w_in, 96)
            for k, name in enumerate(PROLOGUE):
                if name == "p_x":
                    pe.wait_ge(entry_in[0], 32)
                if k:
                    pe.wait_ge(misc_read, k)
                shared_use(name, k, k % MISC, 0, 0)
            pe.wait_ge(misc_read, 3)
            unit_scores(0, 0, 0)

            def step(s):
                nxt = 1 - s.par

                def do(name):
                    if s.has(name):
                        if name == "p_x":
                            pe.wait_ge(entry_in[nxt], entry_half(s) * 32 + 32)
                        shared_use(name, s.number(name), s.bank(name), s.b + 1 if name[0] == "p" else s.b - 1, nxt)

                for u, (before_t, between_t) in enumerate(PLAN):
                    n = s.b * NU + u
                    if not (s.last and u == NU - 1):
                        if u == NU - 1:
                            pe.wait_ge(misc_read, s.number("p_k") + 1)
                            unit_scores(n + 1, 0, nxt)
                        else:
                            unit_scores(n + 1, u + 1, s.par)
                    if u > 0:
                        unit_values(n - 1, u - 1, s.par, 1, s.number(f"o{u - 1}"), s.bank(f"o{u - 1}"))
                    elif not s.first:
                        unit_values(n - 1, NU - 1, nxt, 1, None, (s.bank(s.uses[0]) + 1) % MISC)
                    for name in before_t:
                        do(name)
                    unit_transposes(n, u, 0)
                    unit_transposes(n, u, 1)
                    for name in between_t:
                        do(name)
                    if s.first and u == 0:
                        pe.wait_ge(out_w_in, 64)
                    unit_transposes(n, u, 2)
                    unit_values(n, u, s.par, 0, s.number(f"o{u}"), s.bank(f"o{u}"))
                    unit_transposes(n, u, 3)

            in_steps(pe, step)
            unit_values(B * NU - 1, NU - 1, 1, 1, None, (END_USES - 1) % MISC)
            for k, name in enumerate(EPILOGUE):
                pe.wait_ge(misc_read, END_USES + k)
                shared_use(name, END_USES + k, k % MISC, B - 1, 1)
            pe_experts(pe)


_OUT_SHAPE = (B, S, D)


def _lay_out(inputs):
    arr = lambda name: np.asarray(inputs[name])
    rows = np.arange(P)
    flipped = (np.arange(H)[:, None] * HD + (-np.arange(HD)) % HD).reshape(-1)
    heads = np.array([8 * g + 2 * j + r for g in range(2) for r in range(2) for j in range(4)])
    unit_order = (heads[:, None] * HD + np.arange(HD)).reshape(-1)
    by_column = lambda v: v.reshape(KT, P).T
    a = {
        "x": arr("x"),
        "ctx_t": arr("ctx_1024").transpose(0, 2, 1),
        "wq": arr("L0_xattn_Wq").T,
        "bq": by_column(arr("L0_xattn_bq")),
        "wk": arr("L0_xattn_Wk")[flipped].T,
        "bk": by_column(arr("L0_xattn_bk")[flipped]),
        "wv": arr("L0_xattn_Wv")[unit_order].T,
        "bv": arr("L0_xattn_bv")[unit_order][None, :],
        "wo": arr("L0_xattn_Wo").T[unit_order],
        "bo": arr("L0_xattn_bo")[None, :],
        "rw": arr("L0_ffn_router_w").T,
        "rb": arr("L0_ffn_router_bias")[None, :],
        "gate": arr("L0_ffn_gate_proj"),
        "up": arr("L0_ffn_up_proj"),
        "down": arr("L0_ffn_down_proj"),
        "sh_gate": arr("L0_ffn_sh_gate").T,
        "sh_up": arr("L0_ffn_sh_up").T,
        "sh_down": arr("L0_ffn_sh_down").T,
        "ident": np.eye(P, dtype=np.float32),
        "head_mask": np.stack([(rows // HD) % 2 == r for r in range(2)], 1).astype(np.float32),
        "part_mask": np.stack([(rows % SLOT % 4 == j) & (rows % SLOT < 12) for j in range(4)], 1).astype(np.float32),
        "expert_iota": np.tile(np.arange(E, dtype=np.float32), (P, 1)),
        "tile_iota": np.tile(np.arange(TILES, dtype=np.float32), (P, 1)),
        "row_iota": np.tile(rows.astype(np.float32), (P, 1)),
        "row_number": rows.astype(np.float32)[:, None],
    }
    return {name: np.ascontiguousarray(v) for name, v in a.items()}


def kernel(**inputs):
    import concourse.bacc as bacc
    from concourse.bass_utils import run_bass_kernel_spmd

    arrays = _lay_out(inputs)
    nc = bacc.Bacc("TRN2", target_bir_lowering=False, num_devices=1)
    aps = {name: nc.dram_tensor(f"in_{name}", v.shape, mybir.dt.from_np(v.dtype), kind="ExternalInput").ap()
           for name, v in arrays.items()}
    out = nc.dram_tensor("out_0", _OUT_SHAPE, F32, kind="ExternalOutput").ap()
    program(nc, aps, out)
    r = run_bass_kernel_spmd(nc, [{f"in_{name}": v for name, v in arrays.items()}], core_ids=[0])
    return r.results[0]["out_0"]
```

```python
from contextlib import ExitStack

import numpy as np

import concourse.bass as bass
from concourse import mybir

F32 = mybir.dt.float32
BF16 = mybir.dt.bfloat16
I32 = mybir.dt.int32
U32 = mybir.dt.uint32
ALU = mybir.AluOpType
ACT = mybir.ActivationFunctionType
AX = mybir.AxisListType

P = 128
B, S, D = 8, 256, 256
H, HD = 16, 16
KT = D // P
ST = S // P
NT = B * ST
TOK = B * S
NU = 4
SLOT = 32
E, EH, TOPK = 16, 128, 2
PAIRS = TOPK * TOK
TILES = 48
SCALE = float(HD) ** 0.5
EPS = 1e-5
RING = 4
PEEL = RING + 2
PRODUCTS = [(0, 0), (0, 1), (0, 2), (1, 0), (1, 1), (1, 2), (2, 0), (2, 1)]
WORD = RING + 2
HOTS = 4
CHUNKS = 4
MISC = 2
assert PAIRS // P + E - 1 <= TILES and (TILES - 2 * PEEL) % RING == 0

PLAN = [
    (["p_q", "p_k"], ["f_slots0", "f_slots1"]),
    (["f_heads"], ["f_out"]),
    (["p_v"], []),
    (["f_h"], ["p_x", "f_router"]),
]
READS = {"p_q": "p_x_next", "f_slots0": f"o{NU - 1}", "f_out": "f_heads", "f_router": "f_h"}
PROLOGUE = ["p_x", "p_q", "p_k", "p_v", "p_x_next"]
EPILOGUE = ["f_slots0", "f_slots1", "f_heads", "f_out", "f_h", "f_router"]


class Step:

    def __init__(self, b, par, half, first=False, last=False, tail=False):
        self.b, self.par, self.half, self.first, self.last = b, par, half, first, last
        self.loads = not (last or tail)
        self.uses = []
        for u, (before, between) in enumerate(PLAN):
            self.uses += [n for n in before + between if self.has(n)] + [f"o{u}"]

    def has(self, name):
        if name == "p_x":
            return self.loads
        return not ((self.first and name[0] == "f") or (self.last and name[0] == "p"))

    def entry(self, name):
        if name == "p_x":
            return self.b + 2, self.par
        return (self.b + 1 if name[0] == "p" else self.b - 1), 1 - self.par

    def before(self, name):
        at = self.uses.index(name)
        return self.uses[at - 1] if at else PROLOGUE[-1] if self.first else f"o{NU - 1}"

    def _after_first(self, name):
        missing = 1 if self.last else 0
        return FIRST_USES - USES - missing + self.uses.index(name)

    def number(self, name):
        if self.first:
            return len(PROLOGUE) + self.uses.index(name)
        return self.b * USES + self._after_first(name)

    def bank(self, name):
        return (self.number(name) if self.first else self._after_first(name)) % MISC


USES = len(Step(1, 1, 0).uses)
FIRST_USES = len(PROLOGUE) + len(Step(0, 0, 0, first=True).uses)
LAST_STEP = Step(B - 1, 1, B // 2 - 1, last=True)
END_USES = LAST_STEP.number("o3") + 1
assert USES % MISC == 0


def program(nc, a, out):
    with ExitStack() as ctx:
        def sb(name, shape, dt=F32):
            return ctx.enter_context(nc.sbuf_tensor(name, shape, dt))

        def sem(name):
            return ctx.enter_context(nc.semaphore(name))

        ps = ctx.enter_context(nc.psum_tensor("ps", [P, 8, 512], F32))
        ps_scores = ps[:, 0:4, :]
        ps_probs = [ps[:, 4 + i, :] for i in range(2)]
        ps_misc = [ps[:, 6 + i, :] for i in range(MISC)]

        ident = sb("ident", [P, P])
        part_mask = sb("part_mask", [P, 4])
        onehot = sb("onehot", [P, 4, P], BF16)
        before = sb("before", [P, P], BF16)
        ones_bf = sb("ones_bf", [P, P], BF16)
        expert_iota = sb("expert_iota", [P, E])
        tile_iota = sb("tile_iota", [P, TILES])
        row_iota = sb("row_iota", [P, P])
        row_number = sb("row_number", [P, 1])
        minus_half = sb("minus_half", [P, ST])
        eps_tile = sb("eps_tile", [P, ST])
        zeros = sb("zeros", [P, 4 * ST])
        dve_carrier = sb("dve_carrier", [P, 1])
        pool_carrier = sb("pool_carrier", [P, RING])

        wq = sb("wq", [P, KT, D])
        wk = sb("wk", [P, KT, D])
        wv = sb("wv", [P, KT, D])
        wo = sb("wo", [P, KT, D])
        bq = sb("bq", [P, KT])
        bk = sb("bk", [P, KT])
        bv = sb("bv", [P, D])
        bo = sb("bo", [P, D])
        rw = sb("rw", [P, KT, E])
        rb = sb("rb", [P, E])
        sh_gu = sb("sh_gu", [P, KT, 2 * D])
        sh_d = sb("sh_d", [P, KT, D])
        w_gu = sb("w_gu", [P, E, KT, 2 * EH])

        x_in = sb("x_in", [P, 2, ST, D])
        ctx_t = sb("ctx_t", [P, 2, KT, S])
        x_bo = sb("x_bo", [P, 2, ST, D])
        ln_stats = sb("ln_stats", [P, 2, ST, 6])
        ln_mv = sb("ln_mv", [P, 2, ST, 2])
        ln_var = sb("ln_var", [P, 2, ST])
        ln_rstd = sb("ln_rstd", [P, 2, ST])
        ln_shift = sb("ln_shift", [P, 2, ST])
        xn = sb("xn", [P, 2, ST, D])
        xn_t = sb("xn_t", [P, 2, KT, S])
        qk = sb("qk", [P, 2, 2 * S])
        qk_parts = sb("qk_parts", [P, 2, 3, 2 * S], BF16)
        both_rows = sb("both_rows", [P, 2 * 2 * H * S // 2])
        q_rows, k_rows = [both_rows[:, i * H * S:(i + 1) * H * S].bitcast(BF16).rearrange("p (a h s) -> p a h s", a=2, h=H)
                          for i in range(2)]
        w_d = both_rows[:, 0:E * D].rearrange("p (e d) -> p e d", e=E)
        v_one = sb("v_one", [P, 2, ST, H, SLOT])
        scores = sb("scores", [P, 2, 4, ST, S])
        neg_max = sb("neg_max", [P, 2, 4 * ST])
        rest1 = sb("rest1", [P, 2, 4 * ST])
        start_marks = sb("start_marks", [P, 2])
        max_parts = sb("max_parts", [P, 2, ST, SLOT], BF16)
        max_rows = sb("max_rows", [P, 2, ST, P], BF16)
        attn = sb("attn", [P, NT * D])
        h_all = attn[:, :].rearrange("p (t d) -> p t d", d=D)
        probs = attn[:, 0:8 * S].rearrange("p (s j q) -> p s j q", s=4, j=2)
        o_slots = attn[:, 8 * S:12 * S].rearrange("p (u q) -> p u q", u=NU)
        inv_sum = sb("inv_sum", [P, ST, H])
        o_norm = attn[:, 12 * S:14 * S].rearrange("p (t d) -> p t d", t=ST)
        o_t = attn[:, 14 * S:16 * S].rearrange("p (k s) -> p k s", k=KT)
        h = sb("h", [P, 2, ST, D])
        h_tp = sb("h_tp", [P, KT, S])

        x1 = sb("x1", [P, NT, D])
        h_t = sb("h_t", [P, KT, TOK])
        logits = sb("logits", [P, NT, E])

        top8 = sb("top8", [P, NT, 8])
        top8_at = sb("top8_at", [P, NT, 8], U32)
        choice = sb("choice", [P, NT, TOPK])
        v_flat = v_one[:, :, :, :, :].rearrange("p a t h n -> p (a t h n)")
        NE = NT * E
        chosen, rank_of = [v_flat[:, i * TOPK * NE:(i + 1) * TOPK * NE].rearrange("p (k t e) -> p k t e", k=TOPK, t=NT)
                           for i in range(2)]
        rank = v_flat[:, 4 * NE:5 * NE].rearrange("p (t e) -> p t e", t=NT)
        past = v_flat[:, 5 * NE:5 * NE + TILES * E].rearrange("p (t e) -> p t e", e=E)
        chosen_any = sb("chosen_any", [P, NT, E], BF16)
        tiles_i = sb("tiles_i", [P, E], I32)
        tiles_s = sb("tiles_s", [P, E], I32)
        tiles_f = sb("tiles_f", [P, E])
        tiles_end = sb("tiles_end", [P, E])
        row_start = sb("row_start", [P, E])
        ones_f = sb("ones_f", [P, E])
        pos_f = sb("pos_f", [P, TOPK, NT])
        pos_i = sb("pos_i", [P, TOPK, NT], I32)
        pos_lo = sb("pos_lo", [P, TOPK, NT], I32)
        pos_hi = sb("pos_hi", [P, TOPK, NT], I32)
        pos_lof = sb("pos_lof", [P, TOPK, NT])
        pos_hif = sb("pos_hif", [P, TOPK, NT])
        pos_at = sb("pos_at", [P, TOPK, NT], U32)
        tile_expert_f = sb("tile_expert_f", [P, TILES])
        words = sb("words", [P, TILES])
        tile_expert = sb("tile_expert", [P, TILES], I32)
        gap = sb("gap", [P, NT])
        gap_exp = sb("gap_exp", [P, NT])
        gap_sum = sb("gap_sum", [P, NT])
        weight = sb("weight", [P, TOPK, NT])
        ids = sb("ids", [P, TILES], U32)
        id_sums = sb("id_sums", [P, 3, TILES])
        hot_row = sb("hot_row", [P, HOTS, P], BF16)
        hot_tile = sb("hot_tile", [P, HOTS, 3, TILES], BF16)

        sh_act, sh_hid = [scores[:, i].rearrange("p j t k -> p (j t k)").rearrange("p (a m n) -> p a m n", a=2, m=KT)
                          for i in range(2)]
        scatter_at = [sb(f"scatter_at{i}", [P, 1], U32) for i in range(RING)]
        rows = [x_in[:, i // ST, i % ST, :] for i in range(RING)]
        rows_t = xn_t[:, 0].rearrange("p a (k n) -> p a k n", k=KT)
        gate_act, hid = [xn_t[:, 1, i].rearrange("p (a n) -> p a n", a=2) for i in range(2)]
        hid_t = sb("hid_t", [P, 2, P])
        y_rows = [x_bo[:, i // ST, i % ST, :] for i in range(RING)]
        zero_rows = sb("zero_rows", [P, D])
        y_in = w_gu[:, :, :, :].rearrange("p e k n -> p (e k n)").rearrange("p (c t d) -> p c t d", c=TOPK, t=NT)
        part = xn[:, 0]

        h_rows = nc.dram_tensor("h_rows", (TOK, D), F32).ap()
        sorted_rows = nc.dram_tensor("sorted_rows", (TILES * P, D), F32).ap()
        y_dram = nc.dram_tensor("y_dram", (PAIRS, D), F32).ap()
        x_rows = a["x"].rearrange("b (st p) d -> b p st d", p=P)
        ctx_rows = a["ctx_t"].rearrange("b (kt p) t -> b p kt t", p=P)
        sorted_out = sorted_rows.rearrange("(t p) d -> p t d", p=P)
        parts_dram = nc.dram_tensor("parts_dram", (2, B, 3, P, 2 * S), BF16).ap()
        h_out = h_rows.rearrange("(t p) d -> p t d", p=P)
        out_rows = out.rearrange("b (st p) d -> p (b st) d", p=P)
        y_rows_in = y_dram.rearrange("(c t p) d -> p c t d", c=TOPK, p=P)

        const_in = sem("const_in")
        attn_w_in = sem("attn_w_in")
        out_w_in = sem("out_w_in")
        route_const_in = sem("route_const_in")
        expert_w_in = sem("expert_w_in")
        entry_in = [sem("entry_in0"), sem("entry_in1")]
        set_up = sem("set_up")
        misc_full = sem("misc_full")
        misc_read = sem("misc_read")
        ln1_stats = sem("ln1_stats")
        ln2_stats = sem("ln2_stats")
        ln1_coeff = sem("ln1_coeff")
        ln2_coeff = sem("ln2_coeff")
        xn_ready = sem("xn_ready")
        h_ready = sem("h_ready")
        x_bo_ready = sem("x_bo_ready")
        h_free = [sem("h_free0"), sem("h_free1")]
        split_q_link = sem("split_q_link")
        split_k_link = sem("split_k_link")
        q_split = sem("q_split")
        k_split = sem("k_split")
        parts_out = sem("parts_out")
        qk_in = [[sem(f"qk_in{half}{par}") for par in range(2)] for half in range(2)]
        down_w_in = sem("down_w_in")
        scores_full = sem("scores_full")
        scores_abs = sem("scores_abs")
        max_done = sem("max_done")
        parts_done = sem("parts_done")
        max_rows_done = sem("max_rows_done")
        probs_full = sem("probs_full")
        probs_done = sem("probs_done")
        x1_sum = sem("x1_sum")
        ln1_bn = sem("ln1_bn")
        ln2_bn = sem("ln2_bn")
        inv_sum_done = sem("inv_sum_done")
        ln1_link = sem("ln1_link")
        ln2_link = sem("ln2_link")
        split_link = sem("split_link")

        def in_steps(eng, step):
            step(Step(0, 0, 0, first=True))
            with eng.Fori(0, B // 2 - 2) as i:
                step(Step(i * 2 + 1, 1, i))
                step(Step(i * 2 + 2, 0, i + 1))
            step(Step(B - 3, 1, B // 2 - 2))
            step(Step(B - 2, 0, B // 2 - 1, tail=True))
            step(LAST_STEP)

        def entry_half(s):
            return s.half + s.par

        rows_cleared = sem("rows_cleared")
        gap_done = sem("gap_done")
        gap_exp_done = sem("gap_exp_done")
        chosen_done = sem("chosen_done")
        rank_full = sem("rank_full")
        rank_read = sem("rank_read")
        pos_done = sem("pos_done")
        table_done = sem("table_done")
        route_link = sem("route_link")
        h_in = sem("h_in")
        rows_sorted = sem("rows_sorted")
        hot_done = sem("hot_done")
        hot_used = sem("hot_used")
        ids_done = sem("ids_done")
        sh_full = sem("sh_full")
        sh_act_done = sem("sh_act_done")
        sh_hid_done = sem("sh_hid_done")
        sh_down_full = sem("sh_down_full")
        sh_added = sem("sh_added")
        rows_in = [sem(f"rows_in{k}") for k in range(RING)]
        rows_t_full = sem("rows_t_full")
        rows_t_done = sem("rows_t_done")
        gu_full = sem("gu_full")
        gate_act_done = sem("gate_act_done")
        hid_done = sem("hid_done")
        hid_t_full = sem("hid_t_full")
        hid_t_done = sem("hid_t_done")
        y_full = sem("y_full")
        y_done = sem("y_done")
        carried = sem("carried")
        y_out = [sem(f"y_out{k}") for k in range(RING)]
        y_in_done = [sem(f"y_in_done{c}") for c in range(CHUNKS)]
        part_done = sem("part_done")
        out_done = sem("out_done")
        stored = sem("stored")

        BLOCKS, BT = 4, TOK // 4

        def tile_steps(eng, step):
            for i in range(PEEL):
                step(i, i % RING, i // RING)
            with eng.Fori(0, (TILES - 2 * PEEL) // RING) as r:
                for j in range(PEEL, PEEL + RING):
                    step(r * RING + j, j % RING, r + j // RING)
            for i in range(TILES - PEEL, TILES):
                step(i, i % RING, i // RING)

        def sp_experts(sp):
            for par in range(2):
                sp.wait_ge(h_free[par], 16 * (B // 2 + 1))
            for c in range(CHUNKS):
                tiles = slice(c * NT // CHUNKS, (c + 1) * NT // CHUNKS)
                sp.dma_start(h_all[:, tiles, :], h_out[:, tiles, :]).then_inc(h_in, 16)
            sp.wait_ge(rows_sorted, 16 * NT * TOPK)

            def load_rows(i, k):
                sp.dma_start(rows[k], sorted_out[:, bass.ds(i, 1), :].rearrange("p o d -> p (o d)")).then_inc(rows_in[k], 16)

            def step(i, k, r):
                if not (isinstance(i, int) and i + RING - 1 >= TILES):
                    if not (isinstance(i, int) and i == 0):
                        sp.wait_ge(rows_t_full, i)
                    load_rows(i + (RING - 1), (k + RING - 1) % RING)

            for i in range(RING - 1):
                load_rows(i, i)
            tile_steps(sp, step)
            for c in range(CHUNKS):
                if c == 0:
                    for k in range(RING):
                        sp.wait_ge(y_out[k], 16 * (TILES // RING))
                    sp.wait_ge(gu_full, TILES)
                tiles = slice(c * NT // CHUNKS, (c + 1) * NT // CHUNKS)
                for k in range(TOPK):
                    sp.dma_start(y_in[:, k, tiles, :], y_rows_in[:, k, tiles, :]).then_inc(y_in_done[c], 16)
            for c in range(CHUNKS):
                tiles = slice(c * NT // CHUNKS, (c + 1) * NT // CHUNKS)
                sp.wait_ge(out_done, (c + 1) * NT // CHUNKS)
                sp.dma_start(out_rows[:, tiles, :], x1[:, tiles, :]).then_inc(stored, 16)
            sp.wait_ge(stored, 16 * CHUNKS)

        def pool_experts(pool):
            pool.wait_ge(rows_cleared, 16 * TILES // 8)
            pool.wait_ge(pos_done, 1)
            for k in range(TOPK):
                for t in range(NT):
                    if k == 0 and t % (NT // CHUNKS) == 0:
                        pool.wait_ge(h_in, 16 * CHUNKS)
                    nc.gpsimd.indirect_dma_start(sorted_rows, bass.IndirectOffsetOnAxis(ap=pos_at[:, k, t:t + 1], axis=0),
                                                 h_all[:, t, :], None).then_inc(rows_sorted, 16)

            def step(i, k, r):
                pool.wait_ge(y_done, i * 2 + 2)
                nc.gpsimd.tensor_tensor(pool_carrier[:, k:k + 1], zeros[:, 0:1], zeros[:, 0:1], ALU.add).then_inc(carried, 1)
                nc.gpsimd.indirect_dma_start(y_dram, bass.IndirectOffsetOnAxis(ap=scatter_at[k][:, 0:1], axis=0),
                                             y_rows[k], None, bounds_check=PAIRS - 1, oob_is_err=False).then_inc(y_out[k], 16)

            tile_steps(pool, step)

        def dve_experts(dve):
            links = [0]

            def link(ins):
                ins.then_inc(route_link, 1)
                links[0] += 1
                dve.wait_ge(route_link, links[0])

            def choose():
                nc.vector.memset(ones_bf[:, :], 1.0)
                nc.vector.tensor_scalar(before[:, :], row_iota[:, :], row_number[:, 0:1], None, ALU.is_gt)
                dve.wait_ge(misc_read, END_USES + len(EPILOGUE))
                for t in range(NT):
                    last = nc.vector.max(top8[:, t, :], logits[:, t, :])
                link(last)
                for t in range(NT):
                    last = nc.vector.max_index(top8_at[:, t, :], top8[:, t, :], logits[:, t, :])
                link(last)
                nc.vector.tensor_tensor(gap[:, :], top8[:, :, 1], top8[:, :, 0], ALU.subtract).then_inc(gap_done, 1)
                link(nc.vector.tensor_copy(choice[:, :, :], top8_at[:, :, 0:TOPK]))
                for k in range(TOPK):
                    last = nc.vector.tensor_tensor(chosen[:, k], expert_iota[:, :].unsqueeze(1).to_broadcast([P, NT, E]),
                                                   choice[:, :, k].unsqueeze(2).to_broadcast([P, NT, E]), ALU.is_equal)
                link(last)
                nc.vector.tensor_tensor(chosen_any[:, :, :], chosen[:, 0], chosen[:, 1], ALU.add).then_inc(chosen_done, 1)

            def place():
                dve.wait_ge(rank_full, 1)
                counts = ps_misc[0][:, NT * E:NT * E + E]
                link(nc.vector.tensor_scalar(tiles_i[:, :], counts, float(P - 1), None, ALU.add))
                link(nc.vector.tensor_scalar(tiles_s[:, :], tiles_i[:, :], 7, None, ALU.arith_shift_right))
                link(nc.vector.tensor_copy(tiles_f[:, :], tiles_s[:, :]))
                link(nc.vector.tensor_tensor_scan(tiles_end[:, :], ones_f[:, :], tiles_f[:, :], 0.0, ALU.mult, ALU.add))
                link(nc.vector.tensor_tensor(row_start[:, :], tiles_end[:, :], tiles_f[:, :], ALU.subtract))
                link(nc.vector.tensor_scalar(row_start[:, :], row_start[:, :], float(P), None, ALU.mult))
                nc.vector.tensor_tensor(rank[:, :, :], ps_misc[0][:, 0:NT * E].rearrange("p (t e) -> p t e", e=E),
                                        row_start[:, :].unsqueeze(1).to_broadcast([P, NT, E]), ALU.add).then_inc(rank_read, 1)
                dve.wait_ge(rank_read, 1)
                for k in range(TOPK):
                    last = nc.vector.tensor_tensor(rank_of[:, k], chosen[:, k], rank[:, :, :], ALU.mult)
                link(last)
                link(nc.vector.tensor_reduce(pos_f[:, :, :].rearrange("p k t -> p (k t)"),
                                             rank_of[:, :, :, :].rearrange("p k t e -> p (k t) e"), AX.X, ALU.add))
                link(nc.vector.tensor_copy(pos_i[:, :, :], pos_f[:, :, :]))
                nc.vector.tensor_copy(pos_at[:, :, :], pos_f[:, :, :]).then_inc(pos_done, 1)
                nc.vector.tensor_scalar(pos_lo[:, :, :], pos_i[:, :, :], P - 1, None, ALU.bitwise_and)
                link(nc.vector.tensor_scalar(pos_hi[:, :, :], pos_i[:, :, :], 7, None, ALU.arith_shift_right))
                link(nc.vector.tensor_copy(pos_lof[:, :, :], pos_lo[:, :, :]))
                link(nc.vector.tensor_copy(pos_hif[:, :, :], pos_hi[:, :, :]))
                link(nc.vector.tensor_tensor(past[:, :, :], tile_iota[:, :].unsqueeze(2).to_broadcast([P, TILES, E]),
                                             tiles_end[:, :].unsqueeze(1).to_broadcast([P, TILES, E]), ALU.is_ge))
                link(nc.vector.tensor_reduce(tile_expert_f[:, :], past[:, :, :], AX.X, ALU.add))
                link(nc.vector.tensor_scalar(tile_expert_f[:, :], tile_expert_f[:, :], float(E - 1), None, ALU.min))
                link(nc.vector.tensor_copy(words[:, 2:TILES], tile_expert_f[:, 0:TILES - 2]))
                for j in range(1, WORD):
                    n = min(TILES - 2, TILES - j)
                    link(nc.vector.scalar_tensor_tensor(words[:, 2:2 + n], tile_expert_f[:, j:j + n], float(E ** j), words[:, 2:2 + n],
                                                        ALU.mult, ALU.add))
                nc.vector.tensor_copy(tile_expert[:, 2:TILES], words[:, 2:TILES]).then_inc(table_done, 1)
                dve.wait_ge(gap_exp_done, 1)
                link(nc.vector.tensor_scalar(gap_sum[:, :], gap_exp[:, :], 1.0, None, ALU.add))
                link(nc.vector.reciprocal(weight[:, 0, :], gap_sum[:, :]))
                link(nc.vector.tensor_tensor(weight[:, 1, :], weight[:, 0, :], gap_exp[:, :], ALU.mult))

            def invert():
                for n in range(TOPK * NT):
                    k, t = n // NT, n % NT
                    if n >= HOTS:
                        dve.wait_ge(hot_used, n - HOTS + 1)
                    nc.vector.tensor_scalar(hot_row[:, n % HOTS, :], row_iota[:, :], pos_lof[:, k, t:t + 1], None, ALU.is_equal)
                    nc.vector.tensor_scalar(hot_tile[:, n % HOTS, 0, :], tile_iota[:, :], pos_hif[:, k, t:t + 1], float(n),
                                            ALU.is_equal, ALU.mult)
                    nc.vector.tensor_scalar(hot_tile[:, n % HOTS, 1, :], tile_iota[:, :], pos_hif[:, k, t:t + 1],
                                            row_number[:, 0:1], ALU.is_equal, ALU.mult)
                    nc.vector.tensor_scalar(hot_tile[:, n % HOTS, 2, :], tile_iota[:, :], pos_hif[:, k, t:t + 1], None,
                                            ALU.is_equal).then_inc(hot_done, 1)

            def pair_numbers():
                sums = ps_misc[1][:, 0:3 * TILES].rearrange("p (c t) -> p c t", c=3)
                dve.wait_ge(hot_used, TOPK * NT)
                link(nc.vector.tensor_copy(id_sums[:, :, :], sums))
                link(nc.vector.scalar_tensor_tensor(id_sums[:, 0, :], id_sums[:, 0, :], float(P), id_sums[:, 1, :], ALU.mult, ALU.add))
                link(nc.vector.scalar_tensor_tensor(id_sums[:, 0, :], id_sums[:, 2, :], float(-PAIRS), id_sums[:, 0, :],
                                                    ALU.mult, ALU.add))
                nc.vector.tensor_scalar(ids[:, :], id_sums[:, 0, :], float(PAIRS), None, ALU.add).then_inc(ids_done, 1)

            def shared_hidden(bl):
                for m in range(KT):
                    dve.wait_ge(sh_act_done, bl * KT + m + 1)
                    dve.wait_ge(sh_full, bl * 2 * KT + KT + m + 1)
                    nc.vector.tensor_tensor(sh_hid[:, bl % 2, m, :], ps[:, KT + m, :], sh_act[:, bl % 2, m, :],
                                            ALU.mult).then_inc(sh_hid_done, 1)

            def shared_add(bl):
                for hf in range(2):
                    tiles = slice(bl * 4 + 2 * hf, bl * 4 + 2 * hf + 2)
                    dve.wait_ge(sh_down_full, bl * 2 + hf + 1)
                    nc.vector.tensor_tensor(x1[:, tiles, :], ps_probs[hf].rearrange("p (t d) -> p t d", t=2), x1[:, tiles, :],
                                            ALU.add).then_inc(sh_added, 1)

            dve.wait_ge(route_const_in, 64)
            choose()
            shared_hidden(0)
            place()
            shared_hidden(1)
            shared_add(0)
            invert()
            shared_hidden(2)
            shared_add(1)
            pair_numbers()
            shared_hidden(3)
            shared_add(2)
            shared_add(3)
            dve.wait_ge(ids_done, 1)

            def hidden(i, k):
                dve.wait_ge(gate_act_done, i + 1)
                nc.vector.tensor_tensor(hid[:, k % 2, :], ps[:, 2 + k % 2, EH:2 * EH], gate_act[:, k % 2, :],
                                        ALU.mult).then_inc(hid_done, 1)

            def hidden_t(i, k):
                dve.wait_ge(hid_t_full, i + 1)
                nc.vector.tensor_copy(hid_t[:, k % 2, :], ps[:, 4 + k % 2, 0:P]).then_inc(hid_t_done, 1)

            def result(i, k, r):
                dve.wait_ge(y_full, i + 1)
                if not (isinstance(i, int) and i < RING):
                    dve.wait_ge(y_out[k], r * 16)
                    dve.wait_ge(carried, i + 1)
                nc.vector.tensor_copy(y_rows[k], ps[:, 6 + k % 2, 0:D]).then_inc(y_done, 1)
                nc.vector.tensor_copy(scatter_at[k][:, :], ids[:, bass.ds(i, 1)]).then_inc(y_done, 1)

            def step(i, k, r):
                static = isinstance(i, int)
                hidden(i, k)
                if not (static and i < 1):
                    hidden_t(i - 1, k - 1)
                if not (static and i < 2):
                    result(i - 2, (k - 2) % RING, r if k >= 2 else r - 1)

            tile_steps(dve, step)
            hidden_t(TILES - 1, TILES - 1)
            for i in (TILES - 2, TILES - 1):
                result(i, i % RING, i // RING)

            for t in range(NT):
                if t % (NT // CHUNKS) == 0:
                    dve.wait_ge(y_in_done[t // (NT // CHUNKS)], 16 * TOPK)
                if t >= 2:
                    dve.wait_ge(out_done, t - 1)
                nc.vector.scalar_tensor_tensor(part[:, t % 2, :], y_in[:, 0, t, :], weight[:, 0, t:t + 1], x1[:, t, :],
                                               ALU.mult, ALU.add).then_inc(part_done, 1)
                if t:
                    combine(dve, t - 1)
            combine(dve, NT - 1)

        def combine(dve, t):
            dve.wait_ge(part_done, t + 1)
            nc.vector.scalar_tensor_tensor(x1[:, t, :], y_in[:, 1, t, :], weight[:, 1, t:t + 1], part[:, t % 2, :],
                                           ALU.mult, ALU.add).then_inc(out_done, 1)

        def act_experts(act):
            act.wait_ge(gap_done, 1)
            nc.scalar.activation(gap_exp[:, :], gap[:, :], ACT.Exp).then_inc(gap_exp_done, 1)
            for bl in range(BLOCKS):
                for m in range(KT):
                    act.wait_ge(sh_full, bl * 2 * KT + m + 1)
                    if bl >= 2:
                        act.wait_ge(sh_hid_done, (bl - 2) * KT + m + 1)
                    nc.scalar.activation(sh_act[:, bl % 2, m, :], ps[:, m, :], ACT.Silu).then_inc(sh_act_done, 1)

            def rows_to_sbuf(i, k):
                act.wait_ge(rows_t_full, i + 1)
                nc.scalar.activation(rows_t[:, k % 2].rearrange("p k n -> p (k n)"), ps[:, k % 2, 0:D], ACT.Copy).then_inc(rows_t_done, 1)

            def gate(i, k):
                act.wait_ge(gu_full, i + 1)
                nc.scalar.activation(gate_act[:, k % 2, :], ps[:, 2 + k % 2, 0:EH], ACT.Silu).then_inc(gate_act_done, 1)

            rows_to_sbuf(0, 0)

            def step(i, k, r):
                gate(i, k)
                if not (isinstance(i, int) and i == TILES - 1):
                    rows_to_sbuf(i + 1, k + 1)

            tile_steps(act, step)

        def pe_experts(pe):
            def shared_gate_up(bl):
                if bl:
                    pe.wait_ge(sh_hid_done, bl * KT)
                for m in range(2 * KT):
                    for k in range(KT):
                        last = nc.tensor.matmul(ps[:, m, :], sh_gu[:, k, m * P:m * P + P], h_t[:, k, bl * BT:bl * BT + BT],
                                                start=(k == 0), stop=(k == KT - 1))
                    last.then_inc(sh_full, 1)

            def shared_down(bl):
                pe.wait_ge(sh_hid_done, (bl + 1) * KT)
                for hf in range(2):
                    if bl:
                        pe.wait_ge(sh_added, (bl - 1) * 2 + hf + 1)
                    for t in range(2):
                        at = (2 * hf + t) * P
                        for k in range(KT):
                            last = nc.tensor.matmul(ps_probs[hf][:, t * D:t * D + D], sh_hid[:, bl % 2, k, at:at + P],
                                                    sh_d[:, k, :], start=(k == 0), stop=(k == KT - 1))
                    last.then_inc(sh_down_full, 1)

            def ranks():
                pe.wait_ge(route_const_in, 64)
                pe.wait_ge(chosen_done, 1)
                dst = ps_misc[0]
                nc.tensor.matmul(dst[:, 0:NT * E], before[:, :], chosen_any[:, :, :].rearrange("p t e -> p (t e)"),
                                 start=True, stop=False, skip_group_check=True)
                for t in range(NT):
                    last = nc.tensor.matmul(dst[:, (t + 1) * E:(NT + 1) * E].rearrange("p (t e) -> p t e", e=E), ones_bf[:, :],
                                            chosen_any[:, t, :].unsqueeze(1).to_broadcast([P, NT - t, E]),
                                            start=False, stop=(t == NT - 1), skip_group_check=True)
                last.then_inc(rank_full, 1)

            pe.wait_ge(misc_read, END_USES + len(EPILOGUE))
            pe.wait_ge(expert_w_in, 16 * (3 + 2 * 4))
            def invert():
                pe.wait_ge(misc_read, END_USES + len(EPILOGUE))
                for n in range(TOPK * NT):
                    pe.wait_ge(hot_done, n + 1)
                    last = nc.tensor.matmul(ps_misc[1][:, 0:3 * TILES], hot_row[:, n % HOTS, :],
                                            hot_tile[:, n % HOTS].rearrange("p c t -> p (c t)"),
                                            start=(n == 0), stop=(n == TOPK * NT - 1))
                    last.then_inc(hot_used, 1)

            shared_gate_up(0)
            ranks()
            shared_gate_up(1)
            shared_down(0)
            shared_gate_up(2)
            invert()
            shared_down(1)
            shared_gate_up(3)
            shared_down(2)
            shared_down(3)

            def experts_from(i):
                word = pe.value_load(tile_expert[0:1, bass.ds(i, 1)], min_val=0, max_val=E ** WORD - 1)
                return [(word // E ** j) % E for j in range(WORD)]

            def rows_transpose(i, k, r):
                pe.wait_ge(rows_in[k], r * 16 + 16)
                for c in range(KT):
                    last = nc.tensor.transpose(ps[:, k % 2, c * P:c * P + P], rows[k][:, c * P:c * P + P], ident[:, :])
                last.then_inc(rows_t_full, 1)

            def gate_up(i, k, e):
                pe.wait_ge(rows_t_done, i + 1)
                for c in range(KT):
                    last = nc.tensor.matmul(ps[:, 2 + k % 2, 0:2 * EH], rows_t[:, k % 2, c, :],
                                            w_gu[:, bass.ds(e, 1), c, :].rearrange("p o n -> p (o n)"),
                                            start=(c == 0), stop=(c == KT - 1))
                last.then_inc(gu_full, 1)

            def hidden_transpose(i, k):
                pe.wait_ge(hid_done, i + 1)
                nc.tensor.transpose(ps[:, 4 + k % 2, 0:P], hid[:, k % 2, :], ident[:, :]).then_inc(hid_t_full, 1)

            def down(i, k, e):
                pe.wait_ge(hid_t_done, i + 1)
                if not (isinstance(i, int) and i < 2):
                    pe.wait_ge(y_done, i * 2 - 3)
                nc.tensor.matmul(ps[:, 6 + k % 2, 0:D], hid_t[:, k % 2, :],
                                 w_d[:, bass.ds(e, 1), :].rearrange("p o n -> p (o n)"), start=True, stop=True).then_inc(y_full, 1)

            pe.wait_ge(down_w_in, 16)
            pe.wait_ge(table_done, 1)
            pe.wait_ge(rank_read, 1)
            pe.wait_ge(sh_added, BLOCKS * 2)
            rows_transpose(0, 0, 0)
            experts = []

            def step(i, k, r):
                static = isinstance(i, int)
                j = (k - PEEL) % RING
                if static and i == 0:
                    experts[:] = experts_from(2)
                elif j == 0 and not (static and i < PEEL):
                    experts[:] = experts_from(i)
                at = i if static and i < PEEL else j + 2
                gate_up(i, k, experts[at])
                if not (static and i == TILES - 1):
                    rows_transpose(i + 1, (k + 1) % RING, r + (k + 1) // RING)
                if not (static and i < 1):
                    hidden_transpose(i - 1, k - 1)
                if not (static and i < 2):
                    down(i - 2, k - 2, experts[at - 2])

            tile_steps(pe, step)
            hidden_transpose(TILES - 1, TILES - 1)
            for i in (TILES - 2, TILES - 1):
                down(i, i, experts[i - (TILES - 4)])

        block = ctx.enter_context(nc.Block())

        @block.sync
        def _(sp):
            def load_entry(b, par):
                sp.dma_start(x_in[:, par], x_rows[bass.ds(b, 1)].rearrange("o p st d -> p (o st) d")).then_inc(entry_in[par], 16)
                sp.dma_start(ctx_t[:, par], ctx_rows[bass.ds(b, 1)].rearrange("o p kt t -> p (o kt) t")).then_inc(entry_in[par], 16)

            def load_entry_when_free(b, par):
                sp.wait_ge(xn_ready, b - 1)
                sp.wait_ge(x_bo_ready, b - 1)
                sp.wait_ge(scores_full, b * NU - 2 * NU + 2)
                load_entry(b, par)

            def spread_parts(b, par, first=False):
                for w, split in ((1, k_split), (0, q_split)):
                    sp.wait_ge(split, b + 1)
                    sp.dma_start(parts_dram[w, bass.ds(b, 1)].rearrange("o c p n -> p (o c) n"), qk_parts[:, w]).then_inc(parts_out, 16)
                if not first:
                    sp.wait_ge(scores_full, b * NU - NU)
                sp.wait_ge(parts_out, b * 32 + 32)
                for half in range(2):
                    cols = slice(half * H * S // 2, (half + 1) * H * S // 2)
                    for w, rows_of in ((0, q_rows), (1, k_rows)):
                        for at in range(0, len(PRODUCTS), 3):
                            parts = [pair[w] for pair in PRODUCTS[at:at + 3]]
                            dst = rows_of[at * HD:(at + len(parts)) * HD, par].rearrange("p h s -> p (h s)")[:, cols]
                            if w == 0:
                                src = parts_dram[w, bass.ds(b, 1), parts[0]].rearrange("o (r j) n -> (o r) (j n)", r=HD)[:, cols]
                                src = src.unsqueeze(0).to_broadcast([len(parts), HD, H * S // 2])
                            else:
                                src = parts_dram[w, bass.ds(b, 1), 0:len(parts)].rearrange("o c (r j) n -> (o c r) (j n)",
                                                                                           r=HD)[:, cols]
                            sp.dma_start(dst, src).then_inc(qk_in[half][par], 16)

            def store_h(b, par):
                sp.wait_ge(h_ready, b + 1)
                sp.dma_start(h_out[:, bass.ds(b * ST, ST), :], h[:, par]).then_inc(h_free[par], 16)

            def clear_rows(c):
                if c == 0:
                    sp.wait_ge(set_up, 10)
                for at in range(16 * c, 16 * c + 16, 8):
                    sp.dma_start(sorted_out[:, at:at + 8, :],
                                 zero_rows[:, :].unsqueeze(1).to_broadcast([P, 8, D])).then_inc(rows_cleared, 16)

            split_rows = lambda name: a[name].rearrange("(kt p) n -> p kt n", p=P)

            def load_experts(e, n):
                for name, at in (("gate", 0), ("up", EH)):
                    sp.dma_start(w_gu[:, bass.ds(e, n), :, at:at + EH].rearrange("p e k n -> p (e k) n"),
                                 a[name][bass.ds(e, n)].rearrange("e (kt p) n -> p (e kt) n", p=P)).then_inc(expert_w_in, 16)

            load_entry(0, 0)
            sp.dma_start(ident[:, :], a["ident"]).then_inc(const_in, 16)
            for dst, name in ((wq, "wq"), (wk, "wk"), (wv, "wv")):
                sp.dma_start(dst[:, :, :], split_rows(name)).then_inc(attn_w_in, 16)
            sp.dma_start(bq[:, :], a["bq"]).then_inc(attn_w_in, 16)
            sp.dma_start(bk[:, :], a["bk"]).then_inc(attn_w_in, 16)
            sp.dma_start(bv[:, :], a["bv"].to_broadcast([P, D])).then_inc(attn_w_in, 16)
            sp.dma_start(part_mask[:, :], a["part_mask"]).then_inc(const_in, 16)
            load_entry(1, 1)
            sp.dma_start(bo[:, :], a["bo"].to_broadcast([P, D])).then_inc(out_w_in, 16)
            spread_parts(0, 0, first=True)
            sp.dma_start(wo[:, :, :], split_rows("wo")).then_inc(out_w_in, 16)
            sp.dma_start(rw[:, :, :], split_rows("rw")).then_inc(out_w_in, 16)
            sp.dma_start(rb[:, :], a["rb"].to_broadcast([P, E])).then_inc(out_w_in, 16)
            load_entry_when_free(2, 0)
            spread_parts(1, 1, first=True)
            for dst, name in ((expert_iota, "expert_iota"), (tile_iota, "tile_iota"), (row_iota, "row_iota"), (row_number, "row_number")):
                sp.dma_start(dst[:, :], a[name]).then_inc(route_const_in, 16)
            for dst, name in ((sh_gu[:, :, 0:D], "sh_gate"), (sh_gu[:, :, D:2 * D], "sh_up"), (sh_d[:, :, :], "sh_down")):
                sp.dma_start(dst, split_rows(name)).then_inc(expert_w_in, 16)
            for b in range(1, B):
                if b + 2 < B:
                    load_entry_when_free(b + 2, b % 2)
                if b + 1 < B:
                    spread_parts(b + 1, (b + 1) % 2)
                if b + 1 == B:
                    sp.wait_ge(scores_full, B * NU)
                    sp.dma_start(w_d, a["down"].rearrange("e p n -> p e n")).then_inc(down_w_in, 16)
                store_h(b - 1, (b - 1) % 2)
                if b <= 4:
                    load_experts((b - 1) * 4, 4)
                else:
                    clear_rows(b - 5)
            store_h(B - 1, (B - 1) % 2)
            sp_experts(sp)

        @block.gpsimd
        def _(pool):
            nc.gpsimd.memset(minus_half[:, :], -0.5).then_inc(set_up, 1)
            nc.gpsimd.memset(eps_tile[:, :], EPS).then_inc(set_up, 1)
            nc.gpsimd.memset(zeros[:, :], 0.0).then_inc(set_up, 1)
            nc.gpsimd.memset(pool_carrier[:, :], 0.0).then_inc(carried, RING)
            nc.gpsimd.memset(zero_rows[:, :], 0.0).then_inc(set_up, 1)
            nc.gpsimd.memset(max_parts[:, :, :, :], 0.0).then_inc(set_up, 1)
            nc.gpsimd.memset(max_rows[:, :, :, :], 0.0).then_inc(set_up, 1)
            nc.gpsimd.memset(v_one[:, :, :, :, HD:SLOT].rearrange("p a t h n -> p (a t h) n"), 0.0).then_inc(set_up, 1)
            nc.gpsimd.memset(ones_f[:, :], 1.0).then_inc(set_up, 1)
            pool.wait_ge(set_up, 8)
            pool.wait_ge(carried, RING)
            nc.gpsimd.memset(v_one[:, :, :, :, HD:HD + 1].rearrange("p a t h n -> p (a t h) n"), 1.0).then_inc(set_up, 1)
            pool.wait_ge(const_in, 32)
            nc.gpsimd.tensor_copy(onehot[:, :, :], part_mask[:, :].unsqueeze(2).to_broadcast([P, 4, P])).then_inc(set_up, 1)
            nc.gpsimd.memset(start_marks[:, 0:1], 0.0).then_inc(h_free[0], 16)
            nc.gpsimd.memset(start_marks[:, 1:2], 0.0).then_inc(h_free[1], 16)
            pool.wait_ge(h_free[0], 16)
            pool.wait_ge(h_free[1], 16)

            def layernorm(ln, b, stats_sem, link, ready):
                pool.wait_ge(stats_sem, b + 1)
                nc.gpsimd.tensor_tensor(ln_var[:, ln], ln_mv[:, ln, :, 1], eps_tile[:, :], ALU.add).then_inc(link, 1)
                pool.wait_ge(link, b * 3 + 1)
                nc.gpsimd.tensor_tensor(ln_rstd[:, ln], ln_var[:, ln], minus_half[:, :], ALU.pow).then_inc(link, 1)
                pool.wait_ge(link, b * 3 + 2)
                nc.gpsimd.tensor_tensor(ln_var[:, ln], ln_mv[:, ln, :, 0], ln_rstd[:, ln], ALU.mult).then_inc(link, 1)
                pool.wait_ge(link, b * 3 + 3)
                nc.gpsimd.tensor_tensor(ln_shift[:, ln], zeros[:, 0:ST], ln_var[:, ln], ALU.subtract).then_inc(ready, 1)

            def layernorm_1(b):
                layernorm(0, b, ln1_stats, ln1_link, ln1_coeff)

            def layernorm_2(b):
                layernorm(1, b, ln2_stats, ln2_link, ln2_coeff)

            def add_bo(par):
                for t in range(ST):
                    last = nc.gpsimd.tensor_tensor(x_bo[:, par, t, :], x_in[:, par, t, :], bo[:, :], ALU.add)
                last.then_inc(x_bo_ready, 1)

            def split_max(n, par):
                in_cols = lambda k: max_parts[:, par, :, 4 * k:4 * k + 4].rearrange("p t j -> p j t")
                flat = lambda t: t[:, par, :].rearrange("p (j t) -> p j t", t=ST)
                zero = zeros[:, :].rearrange("p (j t) -> p j t", t=ST)
                pool.wait_ge(max_done, n + 1)
                nc.gpsimd.tensor_tensor(in_cols(0), flat(neg_max), zero, ALU.add).then_inc(split_link, 1)
                pool.wait_ge(split_link, n * 3 + 1)
                nc.gpsimd.tensor_tensor(flat(rest1), flat(neg_max), in_cols(0), ALU.subtract).then_inc(split_link, 1)
                pool.wait_ge(split_link, n * 3 + 2)
                nc.gpsimd.tensor_tensor(in_cols(1), flat(rest1), zero, ALU.add).then_inc(split_link, 1)
                pool.wait_ge(split_link, n * 3 + 3)
                nc.gpsimd.tensor_tensor(in_cols(2), flat(rest1), in_cols(1), ALU.subtract).then_inc(parts_done, 1)

            def split_q(number, b):
                part_of = lambda c: qk_parts[:, 0, c, :]
                q = qk[:, 0, :]
                zero = zeros[:, 0:1].to_broadcast([P, 2 * S])
                if not (isinstance(b, int) and b == 0):
                    pool.wait_ge(parts_out, b * 32)
                pool.wait_ge(misc_read, number + 1)
                nc.gpsimd.tensor_tensor(part_of(0), q, zero, ALU.add).then_inc(split_q_link, 1)
                pool.wait_ge(split_q_link, b * 3 + 1)
                nc.gpsimd.tensor_tensor(q, q, part_of(0), ALU.subtract).then_inc(split_q_link, 1)
                pool.wait_ge(split_q_link, b * 3 + 2)
                nc.gpsimd.tensor_tensor(part_of(1), q, zero, ALU.add).then_inc(split_q_link, 1)
                pool.wait_ge(split_q_link, b * 3 + 3)
                nc.gpsimd.tensor_tensor(part_of(2), q, part_of(1), ALU.subtract).then_inc(q_split, 1)

            layernorm_1(0)
            split_q(1, 0)
            layernorm_1(1)
            pool.wait_ge(out_w_in, 64)
            add_bo(0)
            split_max(0, 0)

            def step(s):
                nxt = 1 - s.par
                for u in range(NU):
                    if not (s.last and u == NU - 1):
                        split_max(s.b * NU + (u + 1), (u + 1) % 2)
                    if u == 0 and not s.last:
                        split_q(s.number("p_q"), s.b + 1)
                    if u == NU - 1 and not s.last:
                        if not s.first:
                            pool.wait_ge(h_ready, s.b)
                        add_bo(nxt)
                    if u == 1 and s.loads:
                        layernorm_1(s.b + 2)
                    if u == 1 and not s.first:
                        layernorm_2(s.b - 1)

            in_steps(pool, step)
            layernorm_2(B - 1)
            pool_experts(pool)

        @block.vector
        def _(dve):
            def stats(b, ln, src, bn_done, done):
                for t in range(ST):
                    nc.vector.bn_stats(ln_stats[:, ln, t, :], src[:, t, :]).then_inc(bn_done, 1)
                dve.wait_ge(bn_done, b * ST + ST)
                nc.vector.memset(dve_carrier[:, :], 0.0)
                for t in range(ST):
                    last = nc.vector.bn_aggr(ln_mv[:, ln, t, :], ln_stats[:, ln, t, :])
                last.then_inc(done, 1)

            def stats_1(b, par, half):
                dve.wait_ge(entry_in[par], half * 32 + 32)
                stats(b, 0, x_in[:, par], ln1_bn, ln1_stats)

            def row_max(n, par):
                dve.wait_ge(scores_abs, n + 1)
                nc.vector.tensor_reduce(neg_max[:, par, :], scores[:, par].rearrange("p j t k -> p (j t) k"),
                                        AX.X, ALU.max, negate=True).then_inc(max_done, 1)

            def max_to_rows(n, par):
                dve.wait_ge(parts_done, n + 1)
                for q in range(4):
                    for t in range(ST):
                        last = nc.vector.transpose(max_rows[32 * q:32 * q + 32, par, t, 32 * q:32 * q + 32],
                                                   max_parts[32 * q:32 * q + 32, par, t, :])
                last.then_inc(max_rows_done, 1)

            def unit_out(number, bank, u):
                dve.wait_ge(misc_full, number + 1)
                nc.vector.tensor_copy(o_slots[:, u, :], ps_misc[bank][:, 0:S]).then_inc(misc_read, 1)

            def split_k(number, b):
                part_of = lambda c: qk_parts[:, 1, c, :]
                k = qk[:, 1, :]
                if not (isinstance(b, int) and b == 0):
                    dve.wait_ge(parts_out, b * 32)
                dve.wait_ge(misc_read, number + 1)
                nc.vector.tensor_copy(part_of(0), k).then_inc(split_k_link, 1)
                dve.wait_ge(split_k_link, b * 3 + 1)
                nc.vector.tensor_tensor(k, k, part_of(0), ALU.subtract).then_inc(split_k_link, 1)
                dve.wait_ge(split_k_link, b * 3 + 2)
                nc.vector.tensor_copy(part_of(1), k).then_inc(split_k_link, 1)
                dve.wait_ge(split_k_link, b * 3 + 3)
                nc.vector.tensor_tensor(part_of(2), k, part_of(1), ALU.subtract).then_inc(k_split, 1)

            def evacuate(name, number, bank, b, par):
                src = ps_misc[bank]
                dve.wait_ge(misc_full, number + 1)
                if name in ("p_x", "p_x_next"):
                    nc.vector.tensor_copy(xn_t[:, par].rearrange("p k s -> p (k s)"), src).then_inc(misc_read, 1)
                elif name in ("p_q", "p_k"):
                    w, bias = (0, bq) if name == "p_q" else (1, bk)
                    if name == "p_q" and not (isinstance(b, int) and b == 0):
                        dve.wait_ge(q_split, b)
                    for g in range(2):
                        last = nc.vector.tensor_scalar(qk[:, w, g * S:g * S + S], src[:, g * S:g * S + S], bias[:, g:g + 1],
                                                       None, ALU.add)
                    last.then_inc(misc_read, 1)
                elif name == "p_v":
                    for t in range(ST):
                        last = nc.vector.tensor_tensor(v_one[:, par, t, :, 0:HD],
                                                       src[:, t * D:t * D + D].rearrange("p (h n) -> p h n", h=H),
                                                       bv[:, :].rearrange("p (h n) -> p h n", h=H), ALU.add)
                    last.then_inc(misc_read, 1)
                elif name in ("f_slots0", "f_slots1"):
                    t = int(name[-1])
                    heads = src.rearrange("p (h n) -> p h n", h=H)
                    nc.vector.reciprocal(inv_sum[:, t, :], heads[:, :, HD]).then_inc(inv_sum_done, 1)
                    dve.wait_ge(inv_sum_done, b * ST + (t + 1))
                    nc.vector.tensor_tensor(o_norm[:, t, :].rearrange("p (h n) -> p h n", h=H), heads[:, :, 0:HD],
                                            inv_sum[:, t, :].unsqueeze(2).to_broadcast([P, H, HD]),
                                            ALU.mult).then_inc(misc_read, 1)
                elif name == "f_heads":
                    nc.vector.tensor_copy(o_t[:, :, :].rearrange("p k s -> p (k s)"), src).then_inc(misc_read, 1)
                elif name == "f_out":
                    dve.wait_ge(x_bo_ready, b + 1)
                    nc.vector.tensor_tensor(x_bo[:, par], src.rearrange("p (t d) -> p t d", t=ST), x_bo[:, par],
                                            ALU.add).then_inc(x1_sum, 1)
                    dve.wait_ge(x1_sum, b + 1)
                    nc.vector.tensor_copy(x1[:, bass.ds(b * ST, ST), :], x_bo[:, par]).then_inc(misc_read, 1)
                    stats(b, 1, x_bo[:, par], ln2_bn, ln2_stats)
                elif name == "f_h":
                    nc.vector.tensor_copy(h_tp[:, :, :].rearrange("p k s -> p (k s)"), src)
                    nc.vector.tensor_copy(h_t[:, :, bass.ds(b * S, S)], src.rearrange("p (k s) -> p k s", k=KT)).then_inc(misc_read, 1)
                elif name == "f_router":
                    nc.vector.tensor_tensor(logits[:, bass.ds(b * ST, ST), :],
                                            src[:, 0:ST * E].rearrange("p (t e) -> p t e", t=ST),
                                            rb[:, :].unsqueeze(1).to_broadcast([P, ST, E]), ALU.add).then_inc(misc_read, 1)

            dve.wait_ge(const_in, 32)
            dve.wait_ge(attn_w_in, 96)
            dve.wait_ge(set_up, 10)
            stats_1(0, 0, 0)
            for k, name in enumerate(PROLOGUE):
                if name == "p_x_next":
                    stats_1(1, 1, 0)
                evacuate(name, k, k % MISC, int(name == "p_x_next"), int(name == "p_x_next"))
                if name == "p_k":
                    split_k(k, 0)
            row_max(0, 0)
            max_to_rows(0, 0)

            def step(s):
                nxt = 1 - s.par
                for u, (before_t, between_t) in enumerate(PLAN):
                    n = s.b * NU + u
                    if u > 0:
                        unit_out(s.number(f"o{u - 1}"), s.bank(f"o{u - 1}"), u - 1)
                    elif not s.first:
                        unit_out(s.number(s.uses[0]) - 1, (s.bank(s.uses[0]) + 1) % MISC, NU - 1)
                    if u > 0:
                        for name in before_t:
                            do(s, name)
                    if not (s.last and u == NU - 1):
                        row_max(n + 1, (u + 1) % 2)
                    for name in between_t if u > 0 else before_t + between_t:
                        do(s, name)
                    if u == 1 and s.loads:
                        stats_1(s.b + 2, s.par, s.half + 1)
                    if s.first and u == 0:
                        dve.wait_ge(out_w_in, 64)
                    if not (s.last and u == NU - 1):
                        max_to_rows(n + 1, (u + 1) % 2)
                    if u == 0 and not s.last:
                        split_k(s.number("p_k"), s.b + 1)

            def do(s, name):
                if s.has(name):
                    evacuate(name, s.number(name), s.bank(name), *s.entry(name))

            in_steps(dve, step)
            unit_out(END_USES - 1, (END_USES - 1) % MISC, NU - 1)
            for k, name in enumerate(EPILOGUE):
                evacuate(name, END_USES + k, (END_USES + k) % MISC, B - 1, 1)
            dve_experts(dve)

        @block.scalar
        def _(act):
            def take_abs(n, par):
                act.wait_ge(scores_full, n + 1)
                nc.scalar.activation(scores[:, par].rearrange("p j t k -> p (j t k)"),
                                     ps_scores.rearrange("p j n -> p (j n)"), ACT.Abs).then_inc(scores_abs, 1)

            def take_exp(n, s):
                act.wait_ge(probs_full, n * 4 + (s + 1))
                nc.scalar.activation(probs[:, s].rearrange("p j q -> p (j q)"), ps_probs[s % 2], ACT.Exp,
                                     scale=SCALE).then_inc(probs_done, 1)

            def normalise(ln, b, coeff, src, dst, ready):
                act.wait_ge(coeff, b + 1)
                for t in range(ST):
                    last = nc.scalar.activation(dst[:, t, :], src[:, t, :], ACT.Identity, scale=ln_rstd[:, ln, t:t + 1],
                                                bias=ln_shift[:, ln, t:t + 1])
                last.then_inc(ready, 1)

            def normalise_2(b, par, half):
                act.wait_ge(h_free[par], half * 16 + 16)
                normalise(1, b, ln2_coeff, x_bo[:, par], h[:, par], h_ready)

            act.wait_ge(entry_in[0], 32)
            normalise(0, 0, ln1_coeff, x_in[:, 0], xn[:, 0], xn_ready)
            act.wait_ge(entry_in[1], 32)
            normalise(0, 1, ln1_coeff, x_in[:, 1], xn[:, 1], xn_ready)
            take_abs(0, 0)

            def step(s):
                nxt = 1 - s.par
                for u in range(NU):
                    n = s.b * NU + u
                    if not (s.last and u == NU - 1):
                        take_abs(n + 1, (u + 1) % 2)
                    for k in range(4):
                        take_exp(n, k)
                        if u == 2 and k == 1 and not s.first:
                            normalise_2(s.b - 1, nxt, entry_half(s) - 1)
                        if u == 2 and k == 2 and s.loads:
                            act.wait_ge(entry_in[s.par], s.half * 32 + 64)
                            normalise(0, s.b + 2, ln1_coeff, x_in[:, s.par], xn[:, s.par], xn_ready)

            in_steps(act, step)
            normalise_2(B - 1, 1, (B - 1) // 2)
            act_experts(act)

        @block.tensor
        def _(pe):
            def transposes(dst, sources):
                for i, src in enumerate(sources):
                    last = nc.tensor.transpose(dst[:, i * P:i * P + P], src, ident[:, :])
                return last

            def shared_use(name, number, bank, b, par):
                dst = ps_misc[bank]
                if not (isinstance(number, int) and number < MISC):
                    pe.wait_ge(misc_read, number + (1 - MISC))
                if name in ("p_x", "p_x_next"):
                    pe.wait_ge(xn_ready, b + 1)
                    last = transposes(dst, [xn[:, par, t, k * P:k * P + P] for k in range(KT) for t in range(ST)])
                elif name in ("p_q", "p_k"):
                    w, src = (wq, xn_t) if name == "p_q" else (wk, ctx_t)
                    for g in range(2):
                        for k in range(KT):
                            last = nc.tensor.matmul(dst[:, g * S:g * S + S], w[:, k, g * P:g * P + P], src[:, par, k, :],
                                                    start=(k == 0), stop=(k == KT - 1))
                elif name == "p_v":
                    for t in range(ST):
                        for k in range(KT):
                            last = nc.tensor.matmul(dst[:, t * D:t * D + D], ctx_t[:, par, k, t * P:t * P + P], wv[:, k, :],
                                                    start=(k == 0), stop=(k == KT - 1))
                elif name in ("f_slots0", "f_slots1"):
                    t = int(name[-1])
                    last = transposes(dst, [o_slots[:, u, t * P:t * P + P] for u in range(NU)])
                elif name == "f_heads":
                    last = transposes(dst, [o_norm[:, t, k * P:k * P + P] for k in range(KT) for t in range(ST)])
                elif name == "f_out":
                    for t in range(ST):
                        for k in range(KT):
                            last = nc.tensor.matmul(dst[:, t * D:t * D + D], o_t[:, k, t * P:t * P + P], wo[:, k, :],
                                                    start=(k == 0), stop=(k == KT - 1))
                elif name == "f_h":
                    pe.wait_ge(h_ready, b + 1)
                    last = transposes(dst, [h[:, par, t, k * P:k * P + P] for k in range(KT) for t in range(ST)])
                elif name == "f_router":
                    for t in range(ST):
                        for k in range(KT):
                            last = nc.tensor.matmul(dst[:, t * E:t * E + E], h_tp[:, k, t * P:t * P + P], rw[:, k, :],
                                                    start=(k == 0), stop=(k == KT - 1))
                last.then_inc(misc_full, 1)

            def unit_scores(n, u, par):
                if not (isinstance(n, int) and n == 0):
                    pe.wait_ge(scores_abs, n)
                for t in range(ST):
                    for j in range(4):
                        last = nc.tensor.matmul(ps_scores[:, j, t * S:t * S + S], q_rows[:, par, 4 * u + j, t * P:t * P + P],
                                                k_rows[:, par, 4 * u + j, :], start=True, stop=True)
                last.then_inc(scores_full, 1)

            def unit_transposes(n, u, s):
                key_tile, pair = s // 2, s % 2
                dst = ps_probs[s % 2]
                if s == 0:
                    pe.wait_ge(scores_abs, n + 1)
                if isinstance(n, int) and n * 4 + s < 2:
                    pass
                else:
                    pe.wait_ge(probs_done, n * 4 + (s - 1))
                for jj in range(2):
                    for t in range(ST):
                        at = jj * S + t * P
                        nc.tensor.matmul(dst[:, at:at + P], scores[:, u % 2, 2 * pair + jj, t, key_tile * P:key_tile * P + P],
                                         ident[:, :], start=(at == 0), stop=False, is_transpose=True, skip_group_check=True)
                if s == 0:
                    pe.wait_ge(max_rows_done, n + 1)
                for jj in range(2):
                    j = 2 * pair + jj
                    last = nc.tensor.matmul(dst[:, jj * S:jj * S + S], onehot[:, j, :],
                                            max_rows[:, u % 2].rearrange("p t q -> p (t q)"), start=False, stop=True,
                                            skip_group_check=True)
                last.then_inc(probs_full, 1)

            def unit_values(n, u, par, key_tile, number, bank):
                if key_tile == 0:
                    pe.wait_ge(misc_read, number + (1 - MISC))
                pe.wait_ge(probs_done, n * 4 + (2 * key_tile + 2))
                for j in range(4):
                    last = nc.tensor.matmul(ps_misc[bank][SLOT * j:SLOT * j + SLOT, 0:S], v_one[:, par, key_tile, 4 * u + j, :],
                                            probs[:, 2 * key_tile + j // 2, j % 2, :],
                                            start=(key_tile == 0), stop=(key_tile == 1), skip_group_check=True)
                if key_tile == 1:
                    last.then_inc(misc_full, 1)

            pe.wait_ge(const_in, 32)
            pe.wait_ge(attn_w_in, 96)
            pe.wait_ge(entry_in[0], 32)
            for k, name in enumerate(PROLOGUE):
                if name == "p_q":
                    pe.wait_ge(misc_read, 1)
                shared_use(name, k, k % MISC, int(name == "p_x_next"), int(name == "p_x_next"))
            pe.wait_ge(qk_in[0][0], 96)
            unit_scores(0, 0, 0)

            def step(s):
                nxt = 1 - s.par

                def do(name):
                    if s.has(name):
                        if name == "p_q":
                            pe.wait_ge(entry_in[nxt], entry_half(s) * 32 + 32)
                        if READS.get(name) == s.before(name):
                            pe.wait_ge(misc_read, s.number(name))
                        shared_use(name, s.number(name), s.bank(name), *s.entry(name))

                for u, (before_t, between_t) in enumerate(PLAN):
                    n = s.b * NU + u
                    if not (s.last and u == NU - 1):
                        if u == NU - 1:
                            pe.wait_ge(qk_in[0][nxt], entry_half(s) * 96 + 96)
                            unit_scores(n + 1, 0, nxt)
                        else:
                            if u == 1:
                                pe.wait_ge(qk_in[1][s.par], s.half * 96 + 96)
                            unit_scores(n + 1, u + 1, s.par)
                    if u > 0:
                        unit_values(n - 1, u - 1, s.par, 1, s.number(f"o{u - 1}"), s.bank(f"o{u - 1}"))
                    elif not s.first:
                        unit_values(n - 1, NU - 1, nxt, 1, None, (s.bank(s.uses[0]) + 1) % MISC)
                    for name in before_t:
                        do(name)
                    unit_transposes(n, u, 0)
                    unit_transposes(n, u, 1)
                    for name in between_t:
                        do(name)
                    if s.first and u == 0:
                        pe.wait_ge(out_w_in, 64)
                    unit_transposes(n, u, 2)
                    unit_values(n, u, s.par, 0, s.number(f"o{u}"), s.bank(f"o{u}"))
                    unit_transposes(n, u, 3)

            in_steps(pe, step)
            unit_values(B * NU - 1, NU - 1, 1, 1, None, (END_USES - 1) % MISC)
            for k, name in enumerate(EPILOGUE):
                pe.wait_ge(misc_read, END_USES + k)
                shared_use(name, END_USES + k, (END_USES + k) % MISC, B - 1, 1)
            pe_experts(pe)


_OUT_SHAPE = (B, S, D)


def _lay_out(inputs):
    arr = lambda name: np.asarray(inputs[name])
    rows = np.arange(P)
    g, r, j = np.meshgrid(np.arange(KT), np.arange(HD), np.arange(H // 2), indexing="ij")
    q_order = ((2 * j + g) * HD + r).reshape(-1)
    k_order = ((2 * j + g) * HD + (-r) % HD).reshape(-1)
    by_column = lambda v: v.reshape(KT, P).T
    a = {
        "x": arr("x"),
        "ctx_t": arr("ctx_1024").transpose(0, 2, 1),
        "wq": arr("L0_xattn_Wq")[q_order].T,
        "bq": by_column(arr("L0_xattn_bq")[q_order]),
        "wk": arr("L0_xattn_Wk")[k_order].T,
        "bk": by_column(arr("L0_xattn_bk")[k_order]),
        "wv": arr("L0_xattn_Wv").T,
        "bv": arr("L0_xattn_bv")[None, :],
        "wo": arr("L0_xattn_Wo").T,
        "bo": arr("L0_xattn_bo")[None, :],
        "rw": arr("L0_ffn_router_w").T,
        "rb": arr("L0_ffn_router_bias")[None, :],
        "gate": arr("L0_ffn_gate_proj"),
        "up": arr("L0_ffn_up_proj"),
        "down": arr("L0_ffn_down_proj"),
        "sh_gate": arr("L0_ffn_sh_gate").T,
        "sh_up": arr("L0_ffn_sh_up").T,
        "sh_down": arr("L0_ffn_sh_down").T,
        "ident": np.eye(P, dtype=np.float32),
        "part_mask": np.stack([(rows % SLOT % 4 == j) & (rows % SLOT < 12) for j in range(4)], 1).astype(np.float32),
        "expert_iota": np.tile(np.arange(E, dtype=np.float32), (P, 1)),
        "tile_iota": np.tile(np.arange(TILES, dtype=np.float32), (P, 1)),
        "row_iota": np.tile(rows.astype(np.float32), (P, 1)),
        "row_number": rows.astype(np.float32)[:, None],
    }
    return {name: np.ascontiguousarray(v) for name, v in a.items()}


def kernel(**inputs):
    import concourse.bacc as bacc
    from concourse.bass_utils import run_bass_kernel_spmd

    arrays = _lay_out(inputs)
    nc = bacc.Bacc("TRN2", target_bir_lowering=False, num_devices=1)
    aps = {name: nc.dram_tensor(f"in_{name}", v.shape, mybir.dt.from_np(v.dtype), kind="ExternalInput").ap()
           for name, v in arrays.items()}
    out = nc.dram_tensor("out_0", _OUT_SHAPE, F32, kind="ExternalOutput").ap()
    program(nc, aps, out)
    r = run_bass_kernel_spmd(nc, [{f"in_{name}": v for name, v in arrays.items()}], core_ids=[0])
    return r.results[0]["out_0"]
```

```python
from contextlib import ExitStack

import numpy as np

import concourse.bass as bass
from concourse import mybir

F32 = mybir.dt.float32
BF16 = mybir.dt.bfloat16
I32 = mybir.dt.int32
U32 = mybir.dt.uint32
ALU = mybir.AluOpType
ACT = mybir.ActivationFunctionType
AX = mybir.AxisListType

P = 128
B, S, D = 8, 256, 256
H, HD = 16, 16
KT = D // P
ST = S // P
NT = B * ST
TOK = B * S
NU = 4
SLOT = 32
E, EH, TOPK = 16, 128, 2
PAIRS = TOPK * TOK
TILES = 48
SCALE = float(HD) ** 0.5
EPS = 1e-5
RING = 4
PEEL = RING + 2
PRODUCTS = [(0, 0), (0, 1), (0, 2), (1, 0), (1, 1), (1, 2), (2, 0), (2, 1)]
WORD = RING + 2
MAX_DVE, MAX_ACT = 4, 1
COEFF_2_UNIT = 2
NORMALISE_2_AT, NORMALISE_1_AT, KEEP_X1_AT, KEEP_H_T_AT = (2, 1), (3, 0), (3, 1), (3, 3)
SUBTRACT_AFTER = 2
CHUNKS = 8
COMBINE_POOL = (3, 7, 11)
COMBINE_DVE = tuple(t for t in range(NT) if t not in COMBINE_POOL)
MISC = 2
assert PAIRS // P + E - 1 <= TILES and (TILES - 2 * PEEL) % RING == 0

PLAN = [
    (["p_q", "p_k"], ["f_slots0", "f_slots1"], []),
    (["f_heads"], ["f_out"], []),
    (["p_v"], [], []),
    (["f_h"], ["f_router"], ["p_x"]),
]
READS = {"p_q": "p_x_next", "f_slots0": f"o{NU - 1}", "f_out": "f_heads", "f_router": "f_h"}
PROLOGUE = ["p_k", "p_x", "p_q", "p_v", "p_x_next"]
EPILOGUE = ["f_slots0", "f_slots1", "f_heads", "f_out", "f_h", "f_router"]


class Step:

    def __init__(self, b, par, half, first=False, last=False, tail=False):
        self.b, self.par, self.half, self.first, self.last = b, par, half, first, last
        self.loads = not (last or tail)
        self.uses = []
        for u, (before, between, after) in enumerate(PLAN):
            self.uses += [n for n in before + between + after if self.has(n)] + [f"o{u}"]

    def has(self, name):
        if name == "p_x":
            return self.loads
        return not ((self.first and name[0] == "f") or (self.last and name[0] == "p"))

    def entry(self, name):
        if name == "p_x":
            return self.b + 2, self.par
        return (self.b + 1 if name[0] == "p" else self.b - 1), 1 - self.par

    def before(self, name):
        at = self.uses.index(name)
        return self.uses[at - 1] if at else PROLOGUE[-1] if self.first else f"o{NU - 1}"

    def _after_first(self, name):
        missing = 1 if self.last else 0
        return FIRST_USES - USES - missing + self.uses.index(name)

    def number(self, name):
        if self.first:
            return len(PROLOGUE) + self.uses.index(name)
        return self.b * USES + self._after_first(name)

    def bank(self, name):
        return (self.number(name) if self.first else self._after_first(name)) % MISC


USES = len(Step(1, 1, 0).uses)
FIRST_USES = len(PROLOGUE) + len(Step(0, 0, 0, first=True).uses)
LAST_STEP = Step(B - 1, 1, B // 2 - 1, last=True)
END_USES = LAST_STEP.number("o3") + 1
assert USES % MISC == 0


def program(nc, a, out):
    with ExitStack() as ctx:
        def sb(name, shape, dt=F32):
            return ctx.enter_context(nc.sbuf_tensor(name, shape, dt))

        def sem(name):
            return ctx.enter_context(nc.semaphore(name))

        ps = ctx.enter_context(nc.psum_tensor("ps", [P, 8, 512], F32))
        ps_scores = ps[:, 0:4, :]
        ps_probs = [ps[:, 4 + i, :] for i in range(2)]
        ps_misc = [ps[:, 6 + i, :] for i in range(MISC)]

        ident = sb("ident", [P, P])
        before = sb("before", [P, P], BF16)
        ones_bf = sb("ones_bf", [P, P], BF16)
        expert_iota = sb("expert_iota", [P, E])
        tile_iota = sb("tile_iota", [P, TILES])
        row_iota = sb("row_iota", [P, P])
        row_number = sb("row_number", [P, 1])
        minus_half = sb("minus_half", [P, ST])
        eps_tile = sb("eps_tile", [P, ST])
        zeros = sb("zeros", [P, 4 * ST])
        dve_carrier = sb("dve_carrier", [P, 1])
        pool_carrier = sb("pool_carrier", [P, RING])

        wq = sb("wq", [P, KT, D])
        wk = sb("wk", [P, KT, D])
        wv = sb("wv", [P, KT, D])
        wo = sb("wo", [P, KT, D])
        bq = sb("bq", [P, KT])
        bk = sb("bk", [P, KT])
        bv = sb("bv", [P, D])
        bo = sb("bo", [P, D])
        rw = sb("rw", [P, KT, E])
        rb = sb("rb", [P, E])
        sh_gu = sb("sh_gu", [P, KT, 2 * D])
        sh_d = sb("sh_d", [P, KT, D])
        w_gu = sb("w_gu", [P, E, KT, 2 * EH])

        x_in = sb("x_in", [P, 2, ST, D])
        ctx_t = sb("ctx_t", [P, 2, KT, S])
        x_bo = sb("x_bo", [P, 2, ST, D])
        ln_stats = sb("ln_stats", [P, 2, ST, 6])
        ln_mv = sb("ln_mv", [P, 2, ST, 2])
        ln_var = sb("ln_var", [P, 2, ST])
        ln_rstd = sb("ln_rstd", [P, 2, ST])
        ln_shift = sb("ln_shift", [P, 2, ST])
        xn = sb("xn", [P, 2, ST, D])
        xn_t = sb("xn_t", [P, 2, KT, S])
        qk = sb("qk", [P, 2, 2 * S])
        qk_parts = sb("qk_parts", [P, 2, 3, 2 * S], BF16)
        both_rows = sb("both_rows", [P, 2 * 2 * H * S // 2])
        q_rows, k_rows = [both_rows[:, i * H * S:(i + 1) * H * S].bitcast(BF16).rearrange("p (a h s) -> p a h s", a=2, h=H)
                          for i in range(2)]
        w_d = both_rows[:, 0:E * D].rearrange("p (e d) -> p e d", e=E)
        v_one = sb("v_one", [P, 2, ST, H, SLOT])
        scores = sb("scores", [P, 2, 4, ST, S])
        neg_max = sb("neg_max", [P, 2, 4 * ST])
        start_marks = sb("start_marks", [P, 2])
        table_mark = sb("table_mark", [P, 1])
        attn = sb("attn", [P, NT * D])
        h_all = attn[:, :].rearrange("p (t d) -> p t d", d=D)
        probs = attn[:, 0:8 * S].rearrange("p (s j q) -> p s j q", s=4, j=2)
        o_slots = attn[:, 8 * S:12 * S].rearrange("p (u q) -> p u q", u=NU)
        inv_sum = sb("inv_sum", [P, ST, H])
        o_norm = attn[:, 12 * S:14 * S].rearrange("p (t d) -> p t d", t=ST)
        o_t = attn[:, 14 * S:16 * S].rearrange("p (k s) -> p k s", k=KT)
        h = sb("h", [P, 2, ST, D])
        h_tp = sb("h_tp", [P, KT, S])

        x1 = sb("x1", [P, NT, D])
        h_t = sb("h_t", [P, KT, TOK])
        logits = sb("logits", [P, NT, E])

        top8 = sb("top8", [P, NT, 8])
        top8_at = sb("top8_at", [P, NT, 8], U32)
        choice = sb("choice", [P, NT, TOPK])
        v_flat = v_one[:, :, :, :, :].rearrange("p a t h n -> p (a t h n)")
        NE = NT * E
        chosen, rank_of = [v_flat[:, i * TOPK * NE:(i + 1) * TOPK * NE].rearrange("p (k t e) -> p k t e", k=TOPK, t=NT)
                           for i in range(2)]
        rank = v_flat[:, 4 * NE:5 * NE].rearrange("p (t e) -> p t e", t=NT)
        past = v_flat[:, 5 * NE:5 * NE + TILES * E].rearrange("p (t e) -> p t e", e=E)
        chosen_any = sb("chosen_any", [P, NT, E], BF16)
        tiles_i = sb("tiles_i", [P, E], I32)
        tiles_s = sb("tiles_s", [P, E], I32)
        tiles_f = sb("tiles_f", [P, E])
        tiles_end = sb("tiles_end", [P, E])
        row_start = sb("row_start", [P, E])
        ones_f = sb("ones_f", [P, E])
        pos_f = sb("pos_f", [P, TOPK, NT])
        pos_i = sb("pos_i", [P, TOPK, NT], I32)
        pos_lo = sb("pos_lo", [P, TOPK, NT], I32)
        pos_hi = sb("pos_hi", [P, TOPK, NT], I32)
        pos_lof = sb("pos_lof", [P, TOPK, NT])
        pos_hif = sb("pos_hif", [P, TOPK, NT])
        pos_at = sb("pos_at", [P, TOPK, NT], U32)
        tile_expert_f = sb("tile_expert_f", [P, TILES])
        words = sb("words", [P, TILES])
        tile_expert = sb("tile_expert", [P, TILES], I32)
        gap = sb("gap", [P, NT])
        gap_exp = sb("gap_exp", [P, NT])
        gap_sum = sb("gap_sum", [P, NT])
        weight = sb("weight", [P, TOPK, NT])
        ids = sb("ids", [P, TILES], U32)
        id_sums = sb("id_sums", [P, 3, TILES])
        hots = both_rows[:, H * S:2 * H * S].bitcast(BF16)
        HOT = TOPK * NT
        hot_row = hots[:, 0:HOT * P].rearrange("p (n r) -> p n r", n=HOT)
        hot_tile = hots[:, HOT * P:HOT * (P + 2 * TILES)].rearrange("p (n c t) -> p n c t", n=HOT, c=2)
        hot_at = sb("hot_at", [P, HOT // 4, TILES], BF16)

        sh_act, sh_hid = [scores[:, i].rearrange("p j t k -> p (j t k)").rearrange("p (a m n) -> p a m n", a=2, m=KT)
                          for i in range(2)]
        scatter_at = [sb(f"scatter_at{i}", [P, 1], U32) for i in range(RING)]
        rows = [x_in[:, i // ST, i % ST, :] for i in range(RING)]
        rows_t = xn_t[:, 0].rearrange("p a (k n) -> p a k n", k=KT)
        gate_act, hid = [xn_t[:, 1, i].rearrange("p (a n) -> p a n", a=2) for i in range(2)]
        hid_t = sb("hid_t", [P, 2, P])
        y_rows = [x_bo[:, i // ST, i % ST, :] for i in range(RING)]
        zero_rows = sb("zero_rows", [P, D])
        y_in = w_gu[:, :, :, :].rearrange("p e k n -> p (e k n)").rearrange("p (c t d) -> p c t d", c=TOPK, t=NT)

        h_rows = nc.dram_tensor("h_rows", (TOK, D), F32).ap()
        sorted_rows = nc.dram_tensor("sorted_rows", (TILES * P, D), F32).ap()
        y_dram = nc.dram_tensor("y_dram", (PAIRS, D), F32).ap()
        x_rows = a["x"].rearrange("b (st p) d -> b p st d", p=P)
        ctx_rows = a["ctx_t"].rearrange("b (kt p) t -> b p kt t", p=P)
        sorted_out = sorted_rows.rearrange("(t p) d -> p t d", p=P)
        parts_dram = nc.dram_tensor("parts_dram", (2, B, 3, P, 2 * S), BF16).ap()
        h_out = h_rows.rearrange("(t p) d -> p t d", p=P)
        out_rows = out.rearrange("b (st p) d -> p (b st) d", p=P)
        y_rows_in = y_dram.rearrange("(c t p) d -> p c t d", c=TOPK, p=P)

        const_in = sem("const_in")
        table_in = sem("table_in")
        k_w_in = sem("k_w_in")
        attn_w_in = sem("attn_w_in")
        out_w_in = sem("out_w_in")
        route_const_in = sem("route_const_in")
        expert_w_in = sem("expert_w_in")
        entry_in = [sem("entry_in0"), sem("entry_in1")]
        set_up = sem("set_up")
        misc_full = sem("misc_full")
        misc_read = sem("misc_read")
        ln1_stats = sem("ln1_stats")
        ln2_stats = sem("ln2_stats")
        ln1_coeff = sem("ln1_coeff")
        ln2_coeff = sem("ln2_coeff")
        xn_ready = sem("xn_ready")
        x1_done = sem("x1_done")
        h_t_done = sem("h_t_done")
        h_ready = sem("h_ready")
        x_bo_ready = sem("x_bo_ready")
        h_free = [sem("h_free0"), sem("h_free1")]
        split_q_link = sem("split_q_link")
        split_k_link = sem("split_k_link")
        q_split = sem("q_split")
        k_split = sem("k_split")
        parts_out = sem("parts_out")
        qk_in = [[sem(f"qk_in{half}{par}") for par in range(2)] for half in range(2)]
        down_w_in = sem("down_w_in")
        scores_full = sem("scores_full")
        scores_abs = sem("scores_abs")
        max_done = sem("max_done")
        less_max = [sem(f"less_max_{name}") for name in ("dve", "act", "pool")]
        probs_full = sem("probs_full")
        probs_done = sem("probs_done")
        ln1_bn = sem("ln1_bn")
        ln2_bn = sem("ln2_bn")
        inv_sum_done = sem("inv_sum_done")
        ln1_link = sem("ln1_link")
        ln2_link = sem("ln2_link")

        def in_steps(eng, step):
            step(Step(0, 0, 0, first=True))
            with eng.Fori(0, B // 2 - 2) as i:
                step(Step(i * 2 + 1, 1, i))
                step(Step(i * 2 + 2, 0, i + 1))
            step(Step(B - 3, 1, B // 2 - 2))
            step(Step(B - 2, 0, B // 2 - 1, tail=True))
            step(LAST_STEP)

        def entry_half(s):
            return s.half + s.par

        rows_cleared = sem("rows_cleared")
        gap_done = sem("gap_done")
        gap_exp_done = sem("gap_exp_done")
        top8_done = sem("top8_done")
        chosen_done = sem("chosen_done")
        rank_full = sem("rank_full")
        rank_read = sem("rank_read")
        pos_done = sem("pos_done")
        table_done = sem("table_done")
        route_link = sem("route_link")
        h_in = sem("h_in")
        rows_sorted = sem("rows_sorted")
        hot_done = sem("hot_done")
        hot_used = sem("hot_used")
        ids_done = sem("ids_done")
        sh_full = sem("sh_full")
        sh_act_done = sem("sh_act_done")
        sh_hid_done = sem("sh_hid_done")
        sh_down_full = sem("sh_down_full")
        sh_added = sem("sh_added")
        rows_in = [sem(f"rows_in{k}") for k in range(RING)]
        rows_t_full = sem("rows_t_full")
        rows_t_done = sem("rows_t_done")
        gu_full = sem("gu_full")
        gate_act_done = sem("gate_act_done")
        hid_done = sem("hid_done")
        hid_t_full = sem("hid_t_full")
        hid_t_done = sem("hid_t_done")
        y_full = sem("y_full")
        y_done = sem("y_done")
        carried = sem("carried")
        y_out = [sem(f"y_out{k}") for k in range(RING)]
        y_in_done = [sem(f"y_in_done{c}") for c in range(CHUNKS)]
        part_done = sem("part_done")
        out_done = sem("out_done")
        combine_link = sem("combine_link")
        out_done_pool = sem("out_done_pool")
        weight_done = sem("weight_done")
        stored = sem("stored")

        BLOCKS, BT = 4, TOK // 4

        def tile_steps(eng, step):
            for i in range(PEEL):
                step(i, i % RING, i // RING)
            with eng.Fori(0, (TILES - 2 * PEEL) // RING) as r:
                for j in range(PEEL, PEEL + RING):
                    step(r * RING + j, j % RING, r + j // RING)
            for i in range(TILES - PEEL, TILES):
                step(i, i % RING, i // RING)

        def sp_experts(sp):
            for par in range(2):
                sp.wait_ge(h_free[par], 16 * (B // 2 + 1))
            for c in range(CHUNKS):
                tiles = slice(c * NT // CHUNKS, (c + 1) * NT // CHUNKS)
                sp.dma_start(h_all[:, tiles, :], h_out[:, tiles, :]).then_inc(h_in, 16)
            sp.wait_ge(rows_sorted, 16 * NT * TOPK)

            def load_rows(i, k):
                sp.dma_start(rows[k], sorted_out[:, bass.ds(i, 1), :].rearrange("p o d -> p (o d)")).then_inc(rows_in[k], 16)

            def step(i, k, r):
                if not (isinstance(i, int) and i + RING - 1 >= TILES):
                    if not (isinstance(i, int) and i == 0):
                        sp.wait_ge(rows_t_full, i)
                    load_rows(i + (RING - 1), (k + RING - 1) % RING)

            for i in range(RING - 1):
                load_rows(i, i)
            tile_steps(sp, step)
            for c in range(CHUNKS):
                if c == 0:
                    for k in range(RING):
                        sp.wait_ge(y_out[k], 16 * (TILES // RING))
                    sp.wait_ge(gu_full, TILES)
                tiles = slice(c * NT // CHUNKS, (c + 1) * NT // CHUNKS)
                for k in range(TOPK):
                    sp.dma_start(y_in[:, k, tiles, :], y_rows_in[:, k, tiles, :]).then_inc(y_in_done[c], 16)
            for c in range(CHUNKS):
                tiles = slice(c * NT // CHUNKS, (c + 1) * NT // CHUNKS)
                done = (c + 1) * NT // CHUNKS
                sp.wait_ge(out_done, sum(t < done for t in COMBINE_DVE))
                if any(t in COMBINE_POOL for t in range(done - NT // CHUNKS, done)):
                    sp.wait_ge(out_done_pool, sum(t < done for t in COMBINE_POOL))
                sp.dma_start(out_rows[:, tiles, :], x1[:, tiles, :]).then_inc(stored, 16)
            sp.wait_ge(stored, 16 * CHUNKS)

        def pool_experts(pool):
            pool.wait_ge(rows_cleared, 16 * TILES // 8)
            pool.wait_ge(pos_done, 1)
            for k in range(TOPK):
                for t in range(NT):
                    if k == 0 and t % (NT // CHUNKS) == 0:
                        pool.wait_ge(h_in, 16 * CHUNKS)
                    nc.gpsimd.indirect_dma_start(sorted_rows, bass.IndirectOffsetOnAxis(ap=pos_at[:, k, t:t + 1], axis=0),
                                                 h_all[:, t, :], None).then_inc(rows_sorted, 16)

            def step(i, k, r):
                pool.wait_ge(y_done, i * 2 + 2)
                nc.gpsimd.tensor_tensor(pool_carrier[:, k:k + 1], zeros[:, 0:1], zeros[:, 0:1], ALU.add).then_inc(carried, 1)
                nc.gpsimd.indirect_dma_start(y_dram, bass.IndirectOffsetOnAxis(ap=scatter_at[k][:, 0:1], axis=0),
                                             y_rows[k], None, bounds_check=PAIRS - 1, oob_is_err=False).then_inc(y_out[k], 16)

            tile_steps(pool, step)
            pool_combine(pool)

        def dve_experts(dve):
            links = [0]

            def link(ins):
                ins.then_inc(route_link, 1)
                links[0] += 1
                dve.wait_ge(route_link, links[0])

            def largest(tiles):
                for t in tiles:
                    last = nc.vector.max(top8[:, t, :], logits[:, t, :])
                link(last)
                for t in tiles:
                    last = nc.vector.max_index(top8_at[:, t, :], top8[:, t, :], logits[:, t, :])
                link(last)
                dve.wait_ge(top8_done, 2)

            def choose():
                dve.wait_ge(misc_read, END_USES + len(EPILOGUE))
                largest(range(NT - ST, NT))
                nc.vector.tensor_tensor(gap[:, :], top8[:, :, 1], top8[:, :, 0], ALU.subtract).then_inc(gap_done, 1)
                link(nc.vector.tensor_copy(choice[:, :, :], top8_at[:, :, 0:TOPK]))
                for k in range(TOPK):
                    last = nc.vector.tensor_tensor(chosen[:, k], expert_iota[:, :].unsqueeze(1).to_broadcast([P, NT, E]),
                                                   choice[:, :, k].unsqueeze(2).to_broadcast([P, NT, E]), ALU.is_equal)
                link(last)
                nc.vector.tensor_tensor(chosen_any[:, :, :], chosen[:, 0], chosen[:, 1], ALU.add).then_inc(chosen_done, 1)

            def place():
                dve.wait_ge(rank_full, 1)
                counts = ps_misc[0][:, NT * E:NT * E + E]
                link(nc.vector.tensor_scalar(tiles_i[:, :], counts, float(P - 1), None, ALU.add))
                link(nc.vector.tensor_scalar(tiles_s[:, :], tiles_i[:, :], 7, None, ALU.arith_shift_right))
                link(nc.vector.tensor_copy(tiles_f[:, :], tiles_s[:, :]))
                link(nc.vector.tensor_tensor_scan(tiles_end[:, :], ones_f[:, :], tiles_f[:, :], 0.0, ALU.mult, ALU.add))
                link(nc.vector.tensor_tensor(row_start[:, :], tiles_end[:, :], tiles_f[:, :], ALU.subtract))
                link(nc.vector.tensor_scalar(row_start[:, :], row_start[:, :], float(P), None, ALU.mult))
                nc.vector.tensor_tensor(rank[:, :, :], ps_misc[0][:, 0:NT * E].rearrange("p (t e) -> p t e", e=E),
                                        row_start[:, :].unsqueeze(1).to_broadcast([P, NT, E]), ALU.add).then_inc(rank_read, 1)
                dve.wait_ge(rank_read, 1)
                for k in range(TOPK):
                    last = nc.vector.tensor_tensor(rank_of[:, k], chosen[:, k], rank[:, :, :], ALU.mult)
                link(last)
                link(nc.vector.tensor_reduce(pos_f[:, :, :].rearrange("p k t -> p (k t)"),
                                             rank_of[:, :, :, :].rearrange("p k t e -> p (k t) e"), AX.X, ALU.add))
                link(nc.vector.tensor_copy(pos_i[:, :, :], pos_f[:, :, :]))
                nc.vector.tensor_copy(pos_at[:, :, :], pos_f[:, :, :]).then_inc(pos_done, 1)
                nc.vector.tensor_scalar(pos_lo[:, :, :], pos_i[:, :, :], P - 1, None, ALU.bitwise_and)
                link(nc.vector.tensor_scalar(pos_hi[:, :, :], pos_i[:, :, :], 7, None, ALU.arith_shift_right))
                link(nc.vector.tensor_copy(pos_lof[:, :, :], pos_lo[:, :, :]))
                link(nc.vector.tensor_copy(pos_hif[:, :, :], pos_hi[:, :, :]))
                link(nc.vector.tensor_tensor(past[:, :, :], tile_iota[:, :].unsqueeze(2).to_broadcast([P, TILES, E]),
                                             tiles_end[:, :].unsqueeze(1).to_broadcast([P, TILES, E]), ALU.is_ge))
                link(nc.vector.tensor_reduce(tile_expert_f[:, :], past[:, :, :], AX.X, ALU.add))
                link(nc.vector.tensor_scalar(tile_expert_f[:, :], tile_expert_f[:, :], float(E - 1), None, ALU.min))
                link(nc.vector.tensor_copy(words[:, 2:TILES], tile_expert_f[:, 0:TILES - 2]))
                for j in range(1, WORD):
                    n = min(TILES - 2, TILES - j)
                    link(nc.vector.scalar_tensor_tensor(words[:, 2:2 + n], tile_expert_f[:, j:j + n], float(E ** j), words[:, 2:2 + n],
                                                        ALU.mult, ALU.add))
                nc.vector.tensor_copy(tile_expert[:, 2:TILES], words[:, 2:TILES]).then_inc(table_done, 1)
                dve.wait_ge(gap_exp_done, 1)
                link(nc.vector.tensor_scalar(gap_sum[:, :], gap_exp[:, :], 1.0, None, ALU.add))
                link(nc.vector.reciprocal(weight[:, 0, :], gap_sum[:, :]))
                nc.vector.tensor_tensor(weight[:, 1, :], weight[:, 0, :], gap_exp[:, :], ALU.mult).then_inc(weight_done, 1)
                dve.wait_ge(weight_done, 1)

            def invert(parts):
                for n in parts:
                    group = slice(n * HOT // 4, (n + 1) * HOT // 4)
                    wide = lambda v, width: v.unsqueeze(2).to_broadcast([P, HOT // 4, width])
                    every = lambda v, width: v.unsqueeze(1).to_broadcast([P, HOT // 4, width])
                    flat = lambda v: v[:, :, :].rearrange("p k t -> p (k t)")[:, group]
                    nc.vector.tensor_tensor(hot_row[:, group, :], every(row_iota[:, :], P), wide(flat(pos_lof), P), ALU.is_equal)
                    link(nc.vector.tensor_tensor(hot_at[:, :, :], every(tile_iota[:, :], TILES),
                                                 wide(flat(pos_hif), TILES), ALU.is_equal))
                    nc.vector.tensor_tensor(hot_tile[:, group, 0, :], hot_at[:, :, :], wide(tile_iota[:, group], TILES), ALU.mult)
                    nc.vector.scalar_tensor_tensor(hot_tile[:, group, 1, :], hot_at[:, :, :], row_number[:, 0:1], hot_at[:, :, :],
                                                   ALU.mult, ALU.add).then_inc(hot_done, 1)
                    dve.wait_ge(hot_done, n + 1)

            def pair_numbers():
                sums = ps_misc[1][:, 0:2 * TILES].rearrange("p (c t) -> p c t", c=2)
                dve.wait_ge(hot_used, 1)
                link(nc.vector.tensor_copy(id_sums[:, 0:2, :], sums))
                link(nc.vector.scalar_tensor_tensor(id_sums[:, 0, :], id_sums[:, 0, :], float(P), id_sums[:, 1, :], ALU.mult, ALU.add))
                link(nc.vector.tensor_scalar(id_sums[:, 2, :], id_sums[:, 0, :], 0.0, float(PAIRS + 1), ALU.is_equal, ALU.mult))
                nc.vector.scalar_tensor_tensor(ids[:, :], id_sums[:, 0, :], -1.0, id_sums[:, 2, :], ALU.add, ALU.add).then_inc(ids_done, 1)

            def shared_hidden(bl):
                for m in range(KT):
                    dve.wait_ge(sh_act_done, bl * KT + m + 1)
                    dve.wait_ge(sh_full, bl * 2 * KT + KT + m + 1)
                    nc.vector.tensor_tensor(sh_hid[:, bl % 2, m, :], ps[:, KT + m, :], sh_act[:, bl % 2, m, :],
                                            ALU.mult).then_inc(sh_hid_done, 1)

            def shared_add(bl):
                for hf in range(2):
                    tiles = slice(bl * 4 + 2 * hf, bl * 4 + 2 * hf + 2)
                    if bl == 0 and hf == 0:
                        dve.wait_ge(x1_done, B)
                    dve.wait_ge(sh_down_full, bl * 2 + hf + 1)
                    nc.vector.tensor_tensor(x1[:, tiles, :], ps_probs[hf].rearrange("p (t d) -> p t d", t=2), x1[:, tiles, :],
                                            ALU.add).then_inc(sh_added, 1)

            choose()
            shared_hidden(0)
            place()
            shared_hidden(1)
            shared_add(0)
            invert(range(2))
            shared_hidden(2)
            invert(range(2, 4))
            shared_add(1)
            shared_hidden(3)
            pair_numbers()
            shared_add(2)
            shared_add(3)
            dve.wait_ge(ids_done, 1)

            def hidden(i, k):
                dve.wait_ge(gate_act_done, i + 1)
                nc.vector.tensor_tensor(hid[:, k % 2, :], ps[:, 2 + k % 2, EH:2 * EH], gate_act[:, k % 2, :],
                                        ALU.mult).then_inc(hid_done, 1)

            def hidden_t(i, k):
                dve.wait_ge(hid_t_full, i + 1)
                nc.vector.tensor_copy(hid_t[:, k % 2, :], ps[:, 4 + k % 2, 0:P]).then_inc(hid_t_done, 1)

            def result(i, k, r):
                dve.wait_ge(y_full, i + 1)
                if not (isinstance(i, int) and i < RING):
                    dve.wait_ge(y_out[k], r * 16)
                    dve.wait_ge(carried, i + 1)
                nc.vector.tensor_copy(y_rows[k], ps[:, 6 + k % 2, 0:D]).then_inc(y_done, 1)
                nc.vector.tensor_copy(scatter_at[k][:, :], ids[:, bass.ds(i, 1)]).then_inc(y_done, 1)

            def step(i, k, r):
                static = isinstance(i, int)
                hidden(i, k)
                if not (static and i < 1):
                    hidden_t(i - 1, k - 1)
                if not (static and i < 2):
                    result(i - 2, (k - 2) % RING, r if k >= 2 else r - 1)

            tile_steps(dve, step)
            hidden_t(TILES - 1, TILES - 1)
            for i in (TILES - 2, TILES - 1):
                result(i, i % RING, i // RING)

            for t in COMBINE_DVE:
                dve.wait_ge(y_in_done[t // (NT // CHUNKS)], 16 * TOPK)
                nc.vector.scalar_tensor_tensor(y_in[:, 0, t, :], y_in[:, 0, t, :], weight[:, 0, t:t + 1], x1[:, t, :],
                                               ALU.mult, ALU.add).then_inc(part_done, 1)
                if t != COMBINE_DVE[0]:
                    combine(dve, COMBINE_DVE.index(t) - 1)
            combine(dve, len(COMBINE_DVE) - 1)

        def combine(dve, n):
            t = COMBINE_DVE[n]
            dve.wait_ge(part_done, n + 1)
            nc.vector.scalar_tensor_tensor(x1[:, t, :], y_in[:, 1, t, :], weight[:, 1, t:t + 1], y_in[:, 0, t, :],
                                           ALU.mult, ALU.add).then_inc(out_done, 1)

        def pool_combine(pool):
            links = 0
            pool.wait_ge(weight_done, 1)
            for t in COMBINE_POOL:
                pool.wait_ge(y_in_done[t // (NT // CHUNKS)], 16 * TOPK)
                for k in range(TOPK):
                    last = nc.gpsimd.tensor_tensor(y_in[:, k, t, :], y_in[:, k, t, :], weight[:, k, t:t + 1].to_broadcast([P, D]),
                                                   ALU.mult)
                last.then_inc(combine_link, 1)
                links += 1
                pool.wait_ge(combine_link, links)
                nc.gpsimd.tensor_tensor(y_in[:, 0, t, :], y_in[:, 0, t, :], x1[:, t, :], ALU.add).then_inc(combine_link, 1)
                links += 1
                pool.wait_ge(combine_link, links)
                nc.gpsimd.tensor_tensor(x1[:, t, :], y_in[:, 1, t, :], y_in[:, 0, t, :], ALU.add).then_inc(out_done_pool, 1)

        def dve_largest(dve):
            dve.wait_ge(route_const_in, 64)
            nc.vector.memset(ones_bf[:, :], 1.0)
            nc.vector.tensor_scalar(before[:, :], row_iota[:, :], row_number[:, 0:1], None, ALU.is_gt)
            for t in range(NT - ST):
                last = nc.vector.max(top8[:, t, :], logits[:, t, :])
            last.then_inc(top8_done, 1)
            dve.wait_ge(top8_done, 1)
            for t in range(NT - ST):
                last = nc.vector.max_index(top8_at[:, t, :], top8[:, t, :], logits[:, t, :])
            last.then_inc(top8_done, 1)

        def act_experts(act):
            act.wait_ge(gap_done, 1)
            nc.scalar.activation(gap_exp[:, :], gap[:, :], ACT.Exp).then_inc(gap_exp_done, 1)
            for bl in range(BLOCKS):
                for m in range(KT):
                    act.wait_ge(sh_full, bl * 2 * KT + m + 1)
                    if bl >= 2:
                        act.wait_ge(sh_hid_done, (bl - 2) * KT + m + 1)
                    nc.scalar.activation(sh_act[:, bl % 2, m, :], ps[:, m, :], ACT.Silu).then_inc(sh_act_done, 1)

            def rows_to_sbuf(i, k):
                act.wait_ge(rows_t_full, i + 1)
                nc.scalar.activation(rows_t[:, k % 2].rearrange("p k n -> p (k n)"), ps[:, k % 2, 0:D], ACT.Copy).then_inc(rows_t_done, 1)

            def gate(i, k):
                act.wait_ge(gu_full, i + 1)
                nc.scalar.activation(gate_act[:, k % 2, :], ps[:, 2 + k % 2, 0:EH], ACT.Silu).then_inc(gate_act_done, 1)

            rows_to_sbuf(0, 0)

            def step(i, k, r):
                if not (isinstance(i, int) and i == TILES - 1):
                    rows_to_sbuf(i + 1, k + 1)
                gate(i, k)

            tile_steps(act, step)

        def pe_shared_gate_up(pe, bl, columns):
            if bl:
                pe.wait_ge(sh_hid_done, bl * KT)
            for m in columns:
                for k in range(KT):
                    last = nc.tensor.matmul(ps[:, m, :], sh_gu[:, k, m * P:m * P + P], h_t[:, k, bl * BT:bl * BT + BT],
                                            start=(k == 0), stop=(k == KT - 1))
                last.then_inc(sh_full, 1)

        def pe_experts(pe):
            def shared_gate_up(bl):
                pe_shared_gate_up(pe, bl, range(2 * KT))

            def shared_down(bl):
                pe.wait_ge(sh_hid_done, (bl + 1) * KT)
                for hf in range(2):
                    if bl:
                        pe.wait_ge(sh_added, (bl - 1) * 2 + hf + 1)
                    for t in range(2):
                        at = (2 * hf + t) * P
                        for k in range(KT):
                            last = nc.tensor.matmul(ps_probs[hf][:, t * D:t * D + D], sh_hid[:, bl % 2, k, at:at + P],
                                                    sh_d[:, k, :], start=(k == 0), stop=(k == KT - 1))
                    last.then_inc(sh_down_full, 1)

            def ranks():
                pe.wait_ge(route_const_in, 64)
                pe.wait_ge(chosen_done, 1)
                dst = ps_misc[0]
                nc.tensor.matmul(dst[:, 0:NT * E], before[:, :], chosen_any[:, :, :].rearrange("p t e -> p (t e)"),
                                 start=True, stop=False, skip_group_check=True)
                for t in range(NT):
                    last = nc.tensor.matmul(dst[:, (t + 1) * E:(NT + 1) * E].rearrange("p (t e) -> p t e", e=E), ones_bf[:, :],
                                            chosen_any[:, t, :].unsqueeze(1).to_broadcast([P, NT - t, E]),
                                            start=False, stop=(t == NT - 1), skip_group_check=True)
                last.then_inc(rank_full, 1)

            def invert():
                pe.wait_ge(hot_done, 4)
                for n in range(HOT):
                    last = nc.tensor.matmul(ps_misc[1][:, 0:2 * TILES], hot_row[:, n, :],
                                            hot_tile[:, n].rearrange("p c t -> p (c t)"), start=(n == 0), stop=(n == HOT - 1))
                last.then_inc(hot_used, 1)

            pe.wait_ge(misc_read, END_USES + len(EPILOGUE))
            ranks()
            pe.wait_ge(h_t_done, B)
            shared_gate_up(1)
            shared_down(0)
            shared_gate_up(2)
            shared_down(1)
            shared_gate_up(3)
            invert()
            shared_down(2)
            shared_down(3)

            def experts_from(i):
                word = pe.value_load(tile_expert[0:1, bass.ds(i, 1)], min_val=0, max_val=E ** WORD - 1)
                return [(word // E ** j) % E for j in range(WORD)]

            def rows_transpose(i, k, r):
                pe.wait_ge(rows_in[k], r * 16 + 16)
                for c in range(KT):
                    last = nc.tensor.transpose(ps[:, k % 2, c * P:c * P + P], rows[k][:, c * P:c * P + P], ident[:, :])
                last.then_inc(rows_t_full, 1)

            def gate_up(i, k, e):
                pe.wait_ge(rows_t_done, i + 1)
                for c in range(KT):
                    last = nc.tensor.matmul(ps[:, 2 + k % 2, 0:2 * EH], rows_t[:, k % 2, c, :],
                                            w_gu[:, bass.ds(e, 1), c, :].rearrange("p o n -> p (o n)"),
                                            start=(c == 0), stop=(c == KT - 1))
                last.then_inc(gu_full, 1)

            def hidden_transpose(i, k):
                pe.wait_ge(hid_done, i + 1)
                nc.tensor.transpose(ps[:, 4 + k % 2, 0:P], hid[:, k % 2, :], ident[:, :]).then_inc(hid_t_full, 1)

            def down(i, k, e):
                pe.wait_ge(hid_t_done, i + 1)
                if not (isinstance(i, int) and i < 2):
                    pe.wait_ge(y_done, i * 2 - 3)
                nc.tensor.matmul(ps[:, 6 + k % 2, 0:D], hid_t[:, k % 2, :],
                                 w_d[:, bass.ds(e, 1), :].rearrange("p o n -> p (o n)"), start=True, stop=True).then_inc(y_full, 1)

            pe.wait_ge(down_w_in, 16)
            pe.wait_ge(table_done, 1)
            pe.wait_ge(rank_read, 1)
            pe.wait_ge(sh_added, BLOCKS * 2)
            rows_transpose(0, 0, 0)
            experts = []

            def step(i, k, r):
                static = isinstance(i, int)
                j = (k - PEEL) % RING
                if static and i == 0:
                    experts[:] = experts_from(2)
                elif j == 0 and not (static and i < PEEL):
                    experts[:] = experts_from(i)
                at = i if static and i < PEEL else j + 2
                if not (static and i == TILES - 1):
                    rows_transpose(i + 1, (k + 1) % RING, r + (k + 1) // RING)
                gate_up(i, k, experts[at])
                if not (static and i < 1):
                    hidden_transpose(i - 1, k - 1)
                if not (static and i < 2):
                    down(i - 2, k - 2, experts[at - 2])

            tile_steps(pe, step)
            hidden_transpose(TILES - 1, TILES - 1)
            for i in (TILES - 2, TILES - 1):
                down(i, i, experts[i - (TILES - 4)])

        block = ctx.enter_context(nc.Block())

        @block.sync
        def _(sp):
            def load_entry(b, par):
                sp.dma_start(x_in[:, par], x_rows[bass.ds(b, 1)].rearrange("o p st d -> p (o st) d")).then_inc(entry_in[par], 16)
                sp.dma_start(ctx_t[:, par], ctx_rows[bass.ds(b, 1)].rearrange("o p kt t -> p (o kt) t")).then_inc(entry_in[par], 16)

            def load_entry_when_free(b, par):
                sp.wait_ge(xn_ready, b - 1)
                sp.wait_ge(x_bo_ready, b - 1)
                sp.wait_ge(scores_full, b * NU - 2 * NU + 2)
                load_entry(b, par)

            def write_parts(b, w, split):
                sp.wait_ge(split, b + 1)
                sp.dma_start(parts_dram[w, bass.ds(b, 1)].rearrange("o c p n -> p (o c) n"), qk_parts[:, w]).then_inc(parts_out, 16)

            def read_rows(b, par, w, half):
                cols = slice(half * H * S // 2, (half + 1) * H * S // 2)
                for at in range(0, len(PRODUCTS), 3):
                    parts = [pair[w] for pair in PRODUCTS[at:at + 3]]
                    dst = (q_rows, k_rows)[w][at * HD:(at + len(parts)) * HD, par].rearrange("p h s -> p (h s)")[:, cols]
                    if w == 0:
                        src = parts_dram[w, bass.ds(b, 1), parts[0]].rearrange("o (r j) n -> (o r) (j n)", r=HD)[:, cols]
                        src = src.unsqueeze(0).to_broadcast([len(parts), HD, H * S // 2])
                    else:
                        src = parts_dram[w, bass.ds(b, 1), 0:len(parts)].rearrange("o c (r j) n -> (o c r) (j n)", r=HD)[:, cols]
                    sp.dma_start(dst, src).then_inc(qk_in[half][par], 16)

            def spread_parts(b, par):
                write_parts(b, 1, k_split)
                write_parts(b, 0, q_split)
                if not (isinstance(b, int) and b < 2):
                    sp.wait_ge(scores_full, b * NU - NU)
                sp.wait_ge(parts_out, b * 32 + 32)
                for half in range(2):
                    for w in range(2):
                        read_rows(b, par, w, half)

            def store_h(b, par):
                sp.wait_ge(h_ready, b + 1)
                sp.dma_start(h_out[:, bass.ds(b * ST, ST), :], h[:, par]).then_inc(h_free[par], 16)

            def clear_rows(c):
                if c == 0:
                    sp.wait_ge(set_up, 7)
                for at in range(16 * c, 16 * c + 16, 8):
                    sp.dma_start(sorted_out[:, at:at + 8, :],
                                 zero_rows[:, :].unsqueeze(1).to_broadcast([P, 8, D])).then_inc(rows_cleared, 16)

            split_rows = lambda name: a[name].rearrange("(kt p) n -> p kt n", p=P)

            def load_experts(e, n):
                for name, at in (("gate", 0), ("up", EH)):
                    sp.dma_start(w_gu[:, bass.ds(e, n), :, at:at + EH].rearrange("p e k n -> p (e k) n"),
                                 a[name][bass.ds(e, n)].rearrange("e (kt p) n -> p (e kt) n", p=P)).then_inc(expert_w_in, 16)

            load_entry(0, 0)
            sp.dma_start(wk[:, :, :], split_rows("wk")).then_inc(k_w_in, 16)
            sp.dma_start(bk[:, :], a["bk"]).then_inc(k_w_in, 16)
            sp.dma_start(ident[:, :], a["ident"]).then_inc(const_in, 16)
            for dst, name in ((wq, "wq"), (wv, "wv")):
                sp.dma_start(dst[:, :, :], split_rows(name)).then_inc(attn_w_in, 16)
            sp.dma_start(bq[:, :], a["bq"]).then_inc(attn_w_in, 16)
            sp.dma_start(bv[:, :], a["bv"].to_broadcast([P, D])).then_inc(attn_w_in, 16)
            load_entry(1, 1)
            sp.dma_start(bo[:, :], a["bo"].to_broadcast([P, D])).then_inc(out_w_in, 16)
            for w, split in ((1, k_split), (0, q_split)):
                write_parts(0, w, split)
                sp.wait_ge(parts_out, 32 - 16 * w)
                for half in range(2):
                    read_rows(0, 0, w, half)
            sp.dma_start(wo[:, :, :], split_rows("wo")).then_inc(out_w_in, 16)
            sp.dma_start(rw[:, :, :], split_rows("rw")).then_inc(out_w_in, 16)
            sp.dma_start(rb[:, :], a["rb"].to_broadcast([P, E])).then_inc(out_w_in, 16)
            load_entry_when_free(2, 0)
            spread_parts(1, 1)
            for dst, name in ((expert_iota, "expert_iota"), (tile_iota, "tile_iota"), (row_iota, "row_iota"), (row_number, "row_number")):
                sp.dma_start(dst[:, :], a[name]).then_inc(route_const_in, 16)
            for dst, name in ((sh_gu[:, :, 0:D], "sh_gate"), (sh_gu[:, :, D:2 * D], "sh_up"), (sh_d[:, :, :], "sh_down")):
                sp.dma_start(dst, split_rows(name)).then_inc(expert_w_in, 16)
            for b in range(1, B):
                if b + 2 < B:
                    load_entry_when_free(b + 2, b % 2)
                if b + 1 < B:
                    spread_parts(b + 1, (b + 1) % 2)
                if b + 1 == B:
                    sp.wait_ge(scores_full, B * NU)
                    sp.dma_start(w_d, a["down"].rearrange("e p n -> p e n")).then_inc(down_w_in, 16)
                store_h(b - 1, (b - 1) % 2)
                if b <= 4:
                    load_experts((b - 1) * 4, 4)
                else:
                    clear_rows(b - 5)
            store_h(B - 1, (B - 1) % 2)
            sp_experts(sp)

        @block.gpsimd
        def _(pool):
            nc.gpsimd.memset(minus_half[:, :], -0.5).then_inc(set_up, 1)
            nc.gpsimd.memset(eps_tile[:, :], EPS).then_inc(set_up, 1)
            nc.gpsimd.memset(zeros[:, :], 0.0).then_inc(set_up, 1)
            nc.gpsimd.memset(pool_carrier[:, :], 0.0).then_inc(carried, RING)
            nc.gpsimd.memset(zero_rows[:, :], 0.0).then_inc(set_up, 1)
            nc.gpsimd.memset(v_one[:, :, :, :, HD:SLOT].rearrange("p a t h n -> p (a t h) n"), 0.0).then_inc(set_up, 1)
            nc.gpsimd.memset(ones_f[:, :], 1.0).then_inc(set_up, 1)
            pool.wait_ge(set_up, 6)
            pool.wait_ge(carried, RING)
            nc.gpsimd.memset(v_one[:, :, :, :, HD:HD + 1].rearrange("p a t h n -> p (a t h) n"), 1.0).then_inc(set_up, 1)
            nc.gpsimd.memset(start_marks[:, 0:1], 0.0).then_inc(h_free[0], 16)
            nc.gpsimd.memset(start_marks[:, 1:2], 0.0).then_inc(h_free[1], 16)
            pool.wait_ge(h_free[0], 16)
            pool.wait_ge(h_free[1], 16)

            def layernorm(ln, b, stats_sem, link, ready):
                pool.wait_ge(stats_sem, b + 1)
                nc.gpsimd.tensor_tensor(ln_var[:, ln], ln_mv[:, ln, :, 1], eps_tile[:, :], ALU.add).then_inc(link, 1)
                pool.wait_ge(link, b * 3 + 1)
                nc.gpsimd.tensor_tensor(ln_rstd[:, ln], ln_var[:, ln], minus_half[:, :], ALU.pow).then_inc(link, 1)
                pool.wait_ge(link, b * 3 + 2)
                nc.gpsimd.tensor_tensor(ln_var[:, ln], ln_mv[:, ln, :, 0], ln_rstd[:, ln], ALU.mult).then_inc(link, 1)
                pool.wait_ge(link, b * 3 + 3)
                nc.gpsimd.tensor_tensor(ln_shift[:, ln], zeros[:, 0:ST], ln_var[:, ln], ALU.subtract).then_inc(ready, 1)

            def layernorm_1(b):
                layernorm(0, b, ln1_stats, ln1_link, ln1_coeff)

            def layernorm_2(b):
                layernorm(1, b, ln2_stats, ln2_link, ln2_coeff)

            def add_bo(par):
                for t in range(ST):
                    last = nc.gpsimd.tensor_tensor(x_bo[:, par, t, :], x_in[:, par, t, :], bo[:, :], ALU.add)
                last.then_inc(x_bo_ready, 1)

            def subtract_max(n, par):
                mine = slice(MAX_DVE + MAX_ACT, 4 * ST)
                rest = scores[:, par].rearrange("p j t k -> p (j t) k")[:, mine, :]
                pool.wait_ge(max_done, n + 1)
                nc.gpsimd.tensor_tensor(rest, rest, neg_max[:, par, mine].unsqueeze(2).to_broadcast([P, 4 * ST - MAX_DVE - MAX_ACT, S]),
                                        ALU.add).then_inc(less_max[2], 1)

            def split_q(number, b):
                part_of = lambda c: qk_parts[:, 0, c, :]
                q = qk[:, 0, :]
                zero = zeros[:, 0:1].to_broadcast([P, 2 * S])
                if not (isinstance(b, int) and b == 0):
                    pool.wait_ge(parts_out, b * 32)
                pool.wait_ge(misc_read, number + 1)
                nc.gpsimd.tensor_tensor(part_of(0), q, zero, ALU.add).then_inc(split_q_link, 1)
                pool.wait_ge(split_q_link, b * 3 + 1)
                nc.gpsimd.tensor_tensor(q, q, part_of(0), ALU.subtract).then_inc(split_q_link, 1)
                pool.wait_ge(split_q_link, b * 3 + 2)
                nc.gpsimd.tensor_tensor(part_of(1), q, zero, ALU.add).then_inc(split_q_link, 1)
                pool.wait_ge(split_q_link, b * 3 + 3)
                nc.gpsimd.tensor_tensor(part_of(2), q, part_of(1), ALU.subtract).then_inc(q_split, 1)

            layernorm_1(0)
            layernorm_1(1)
            pool.wait_ge(out_w_in, 64)
            add_bo(0)
            subtract_max(0, 0)

            def step(s):
                nxt = 1 - s.par
                for u in range(NU):
                    if u == COEFF_2_UNIT and not s.first:
                        layernorm_2(s.b - 1)
                    if not (s.last and u == NU - 1):
                        subtract_max(s.b * NU + (u + 1), (u + 1) % 2)
                    if u == 0 and not s.last:
                        split_q(s.number("p_q"), s.b + 1)
                    if u == NU - 1 and not s.last:
                        if not s.first:
                            pool.wait_ge(h_ready, s.b)
                            pool.wait_ge(x1_done, s.b)
                        add_bo(nxt)
                    if u == 1 and s.loads:
                        layernorm_1(s.b + 2)

            in_steps(pool, step)
            layernorm_2(B - 1)
            pool_experts(pool)

        @block.vector
        def _(dve):
            def stats(b, ln, src, bn_done, done):
                for t in range(ST):
                    nc.vector.bn_stats(ln_stats[:, ln, t, :], src[:, t, :]).then_inc(bn_done, 1)
                dve.wait_ge(bn_done, b * ST + ST)
                nc.vector.memset(dve_carrier[:, :], 0.0)
                for t in range(ST):
                    last = nc.vector.bn_aggr(ln_mv[:, ln, t, :], ln_stats[:, ln, t, :])
                last.then_inc(done, 1)

            def stats_1(b, par, half):
                dve.wait_ge(entry_in[par], half * 32 + 32)
                stats(b, 0, x_in[:, par], ln1_bn, ln1_stats)

            def take_max(n, par):
                dve.wait_ge(scores_abs, n + 1)
                nc.vector.tensor_reduce(neg_max[:, par, :], scores[:, par].rearrange("p j t k -> p (j t) k"),
                                        AX.X, ALU.max, negate=True).then_inc(max_done, 1)

            def subtract_max(n, par):
                dve.wait_ge(max_done, n + 1)
                for i in range(MAX_DVE):
                    last = nc.vector.tensor_scalar(scores[:, par, i // ST, i % ST, :], scores[:, par, i // ST, i % ST, :],
                                                   neg_max[:, par, i:i + 1], None, ALU.add)
                last.then_inc(less_max[0], 1)

            def unit_out(number, bank, u):
                dve.wait_ge(misc_full, number + 1)
                nc.vector.tensor_copy(o_slots[:, u, :], ps_misc[bank][:, 0:S]).then_inc(misc_read, 1)

            def split(number, b, w, link, done):
                part_of = lambda c: qk_parts[:, w, c, :]
                whole = qk[:, w, :]
                if not (isinstance(b, int) and b == 0):
                    dve.wait_ge(parts_out, b * 32)
                dve.wait_ge(misc_read, number + 1)
                nc.vector.tensor_copy(part_of(0), whole).then_inc(link, 1)
                dve.wait_ge(link, b * 3 + 1)
                nc.vector.tensor_tensor(whole, whole, part_of(0), ALU.subtract).then_inc(link, 1)
                dve.wait_ge(link, b * 3 + 2)
                nc.vector.tensor_copy(part_of(1), whole).then_inc(link, 1)
                dve.wait_ge(link, b * 3 + 3)
                nc.vector.tensor_tensor(part_of(2), whole, part_of(1), ALU.subtract).then_inc(done, 1)

            def evacuate(name, number, bank, b, par):
                src = ps_misc[bank]
                dve.wait_ge(misc_full, number + 1)
                if name in ("p_x", "p_x_next"):
                    nc.vector.tensor_copy(xn_t[:, par].rearrange("p k s -> p (k s)"), src).then_inc(misc_read, 1)
                elif name in ("p_q", "p_k"):
                    w, bias = (0, bq) if name == "p_q" else (1, bk)
                    if name == "p_q" and not (isinstance(b, int) and b == 0):
                        dve.wait_ge(q_split, b)
                    for g in range(2):
                        last = nc.vector.tensor_scalar(qk[:, w, g * S:g * S + S], src[:, g * S:g * S + S], bias[:, g:g + 1],
                                                       None, ALU.add)
                    last.then_inc(misc_read, 1)
                elif name == "p_v":
                    for t in range(ST):
                        last = nc.vector.tensor_tensor(v_one[:, par, t, :, 0:HD],
                                                       src[:, t * D:t * D + D].rearrange("p (h n) -> p h n", h=H),
                                                       bv[:, :].rearrange("p (h n) -> p h n", h=H), ALU.add)
                    last.then_inc(misc_read, 1)
                elif name in ("f_slots0", "f_slots1"):
                    t = int(name[-1])
                    heads = src.rearrange("p (h n) -> p h n", h=H)
                    nc.vector.reciprocal(inv_sum[:, t, :], heads[:, :, HD]).then_inc(inv_sum_done, 1)
                    dve.wait_ge(inv_sum_done, b * ST + (t + 1))
                    nc.vector.tensor_tensor(o_norm[:, t, :].rearrange("p (h n) -> p h n", h=H), heads[:, :, 0:HD],
                                            inv_sum[:, t, :].unsqueeze(2).to_broadcast([P, H, HD]),
                                            ALU.mult).then_inc(misc_read, 1)
                elif name == "f_heads":
                    nc.vector.tensor_copy(o_t[:, :, :].rearrange("p k s -> p (k s)"), src).then_inc(misc_read, 1)
                elif name == "f_out":
                    dve.wait_ge(x_bo_ready, b + 1)
                    nc.vector.tensor_tensor(x_bo[:, par], src.rearrange("p (t d) -> p t d", t=ST), x_bo[:, par],
                                            ALU.add).then_inc(misc_read, 1)
                    dve.wait_ge(misc_read, number + 1)
                    stats(b, 1, x_bo[:, par], ln2_bn, ln2_stats)
                elif name == "f_h":
                    if not (isinstance(b, int) and b == 0):
                        dve.wait_ge(h_t_done, b)
                    nc.vector.tensor_copy(h_tp[:, :, :].rearrange("p k s -> p (k s)"), src).then_inc(misc_read, 1)
                elif name == "f_router":
                    nc.vector.tensor_tensor(logits[:, bass.ds(b * ST, ST), :],
                                            src[:, 0:ST * E].rearrange("p (t e) -> p t e", t=ST),
                                            rb[:, :].unsqueeze(1).to_broadcast([P, ST, E]), ALU.add).then_inc(misc_read, 1)

            stats_1(0, 0, 0)
            dve.wait_ge(k_w_in, 32)
            for k, name in enumerate(PROLOGUE):
                if name == "p_q":
                    dve.wait_ge(attn_w_in, 64)
                if name == "p_v":
                    dve.wait_ge(set_up, 7)
                if name == "p_x_next":
                    stats_1(1, 1, 0)
                evacuate(name, k, k % MISC, int(name == "p_x_next"), int(name == "p_x_next"))
                if name == "p_x":
                    split(PROLOGUE.index("p_k"), 0, 1, split_k_link, k_split)
                if name == "p_q":
                    split(k, 0, 0, split_q_link, q_split)
            take_max(0, 0)
            subtract_max(0, 0)

            def step(s):
                nxt = 1 - s.par
                for u, (before_t, between_t, after_t) in enumerate(PLAN):
                    n = s.b * NU + u
                    if u > 0:
                        unit_out(s.number(f"o{u - 1}"), s.bank(f"o{u - 1}"), u - 1)
                    elif not s.first:
                        unit_out(s.number(s.uses[0]) - 1, (s.bank(s.uses[0]) + 1) % MISC, NU - 1)
                    if u > 0:
                        for name in before_t:
                            do(s, name)
                    if not (s.last and u == NU - 1):
                        take_max(n + 1, (u + 1) % 2)
                    for name in between_t if u > 0 else before_t + between_t:
                        do(s, name)
                    if u == 1 and s.loads:
                        stats_1(s.b + 2, s.par, s.half + 1)
                    if s.first and u == 0:
                        dve.wait_ge(out_w_in, 64)
                    if not (s.last and u == NU - 1):
                        subtract_max(n + 1, (u + 1) % 2)
                    for name in after_t:
                        do(s, name)
                    if u == 0 and not s.last:
                        split(s.number("p_k"), s.b + 1, 1, split_k_link, k_split)

            def do(s, name):
                if s.has(name):
                    evacuate(name, s.number(name), s.bank(name), *s.entry(name))

            in_steps(dve, step)
            unit_out(END_USES - 1, (END_USES - 1) % MISC, NU - 1)
            for k, name in enumerate(EPILOGUE):
                evacuate(name, END_USES + k, (END_USES + k) % MISC, B - 1, 1)
                if name == "f_out":
                    dve_largest(dve)
            dve_experts(dve)

        @block.scalar
        def _(act):
            def take_abs(n, par):
                act.wait_ge(scores_full, n + 1)
                nc.scalar.activation(scores[:, par].rearrange("p j t k -> p (j t k)"),
                                     ps_scores.rearrange("p j n -> p (j n)"), ACT.Abs).then_inc(scores_abs, 1)

            def subtract_max(n, par):
                act.wait_ge(max_done, n + 1)
                for i in range(MAX_DVE, MAX_DVE + MAX_ACT):
                    pair = scores[:, par, i // ST, i % ST, :]
                    last = nc.scalar.activation(pair, pair, ACT.Identity, bias=neg_max[:, par, i:i + 1])
                last.then_inc(less_max[1], 1)

            def take_exp(n, s):
                act.wait_ge(probs_full, n * 4 + (s + 1))
                nc.scalar.activation(probs[:, s].rearrange("p j q -> p (j q)"), ps_probs[s % 2], ACT.Exp,
                                     scale=SCALE).then_inc(probs_done, 1)

            def normalise(ln, b, coeff, src, dst, ready):
                act.wait_ge(coeff, b + 1)
                for t in range(ST):
                    last = nc.scalar.activation(dst[:, t, :], src[:, t, :], ACT.Identity, scale=ln_rstd[:, ln, t:t + 1],
                                                bias=ln_shift[:, ln, t:t + 1])
                last.then_inc(ready, 1)

            def normalise_2(b, par, half):
                act.wait_ge(h_free[par], half * 16 + 16)
                normalise(1, b, ln2_coeff, x_bo[:, par], h[:, par], h_ready)

            def keep_x1(b, par):
                act.wait_ge(ln2_coeff, b + 1)
                nc.scalar.activation(x1[:, bass.ds(b * ST, ST), :], x_bo[:, par], ACT.Copy).then_inc(x1_done, 1)

            def keep_h_t(b, number):
                act.wait_ge(misc_read, number + 1)
                nc.scalar.activation(h_t[:, :, bass.ds(b * S, S)], h_tp[:, :, :], ACT.Copy).then_inc(h_t_done, 1)

            act.wait_ge(set_up, 7)
            nc.scalar.activation(table_mark[:, :], zeros[:, 0:1], ACT.Identity).then_inc(table_in, 1)
            act.wait_ge(entry_in[0], 32)
            normalise(0, 0, ln1_coeff, x_in[:, 0], xn[:, 0], xn_ready)
            act.wait_ge(entry_in[1], 32)
            normalise(0, 1, ln1_coeff, x_in[:, 1], xn[:, 1], xn_ready)
            take_abs(0, 0)
            subtract_max(0, 0)

            def step(s):
                nxt = 1 - s.par
                for u in range(NU):
                    n = s.b * NU + u
                    if not (s.last and u == NU - 1):
                        take_abs(n + 1, (u + 1) % 2)
                    for k in range(4):
                        take_exp(n, k)
                        if k == SUBTRACT_AFTER and not (s.last and u == NU - 1):
                            subtract_max(n + 1, (u + 1) % 2)
                        if (u, k) == KEEP_H_T_AT and not s.first:
                            keep_h_t(s.b - 1, s.number("f_h"))
                        if (u, k) == NORMALISE_2_AT and not s.first:
                            normalise_2(s.b - 1, nxt, entry_half(s) - 1)
                        if (u, k) == KEEP_X1_AT and not s.first:
                            keep_x1(s.b - 1, nxt)
                        if (u, k) == NORMALISE_1_AT and s.loads:
                            act.wait_ge(entry_in[s.par], s.half * 32 + 64)
                            normalise(0, s.b + 2, ln1_coeff, x_in[:, s.par], xn[:, s.par], xn_ready)

            in_steps(act, step)
            normalise_2(B - 1, 1, (B - 1) // 2)
            keep_x1(B - 1, 1)
            keep_h_t(B - 1, END_USES + EPILOGUE.index("f_h"))
            act_experts(act)

        @block.tensor
        def _(pe):
            def transposes(dst, sources):
                for i, src in enumerate(sources):
                    last = nc.tensor.transpose(dst[:, i * P:i * P + P], src, ident[:, :])
                return last

            def shared_use(name, number, bank, b, par):
                dst = ps_misc[bank]
                if not (isinstance(number, int) and number < MISC):
                    pe.wait_ge(misc_read, number + (1 - MISC))
                if name in ("p_x", "p_x_next"):
                    pe.wait_ge(xn_ready, b + 1)
                    last = transposes(dst, [xn[:, par, t, k * P:k * P + P] for k in range(KT) for t in range(ST)])
                elif name in ("p_q", "p_k"):
                    w, src = (wq, xn_t) if name == "p_q" else (wk, ctx_t)
                    for g in range(2):
                        for k in range(KT):
                            last = nc.tensor.matmul(dst[:, g * S:g * S + S], w[:, k, g * P:g * P + P], src[:, par, k, :],
                                                    start=(k == 0), stop=(k == KT - 1))
                elif name == "p_v":
                    for t in range(ST):
                        for k in range(KT):
                            last = nc.tensor.matmul(dst[:, t * D:t * D + D], ctx_t[:, par, k, t * P:t * P + P], wv[:, k, :],
                                                    start=(k == 0), stop=(k == KT - 1))
                elif name in ("f_slots0", "f_slots1"):
                    t = int(name[-1])
                    last = transposes(dst, [o_slots[:, u, t * P:t * P + P] for u in range(NU)])
                elif name == "f_heads":
                    last = transposes(dst, [o_norm[:, t, k * P:k * P + P] for k in range(KT) for t in range(ST)])
                elif name == "f_out":
                    for t in range(ST):
                        for k in range(KT):
                            last = nc.tensor.matmul(dst[:, t * D:t * D + D], o_t[:, k, t * P:t * P + P], wo[:, k, :],
                                                    start=(k == 0), stop=(k == KT - 1))
                elif name == "f_h":
                    pe.wait_ge(h_ready, b + 1)
                    last = transposes(dst, [h[:, par, t, k * P:k * P + P] for k in range(KT) for t in range(ST)])
                elif name == "f_router":
                    for t in range(ST):
                        for k in range(KT):
                            last = nc.tensor.matmul(dst[:, t * E:t * E + E], h_tp[:, k, t * P:t * P + P], rw[:, k, :],
                                                    start=(k == 0), stop=(k == KT - 1))
                last.then_inc(misc_full, 1)

            def unit_scores(n, u, par):
                if not (isinstance(n, int) and n == 0):
                    pe.wait_ge(scores_abs, n)
                for t in range(ST):
                    for j in range(4):
                        last = nc.tensor.matmul(ps_scores[:, j, t * S:t * S + S], q_rows[:, par, 4 * u + j, t * P:t * P + P],
                                                k_rows[:, par, 4 * u + j, :], start=True, stop=True)
                last.then_inc(scores_full, 1)

            def unit_transposes(n, u, s):
                key_tile, pair = s // 2, s % 2
                dst = ps_probs[s % 2]
                if s == 0:
                    pe.wait_ge(less_max[0], n + 1)
                    pe.wait_ge(less_max[1], n + 1)
                if s == 1:
                    pe.wait_ge(less_max[2], n + 1)
                if not (isinstance(n, int) and n * 4 + s < 2):
                    pe.wait_ge(probs_done, n * 4 + (s - 1))
                last = transposes(dst, [scores[:, u % 2, 2 * pair + jj, t, key_tile * P:key_tile * P + P]
                                        for jj in range(2) for t in range(ST)])
                last.then_inc(probs_full, 1)

            def unit_values(n, u, par, key_tile, number, bank):
                if key_tile == 0:
                    pe.wait_ge(misc_read, number + (1 - MISC))
                pe.wait_ge(probs_done, n * 4 + (2 * key_tile + 2))
                for j in range(4):
                    last = nc.tensor.matmul(ps_misc[bank][SLOT * j:SLOT * j + SLOT, 0:S], v_one[:, par, key_tile, 4 * u + j, :],
                                            probs[:, 2 * key_tile + j // 2, j % 2, :],
                                            start=(key_tile == 0), stop=(key_tile == 1), skip_group_check=True)
                if key_tile == 1:
                    last.then_inc(misc_full, 1)

            pe.wait_ge(entry_in[0], 32)
            pe.wait_ge(k_w_in, 32)
            for k, name in enumerate(PROLOGUE):
                if name == "p_x":
                    pe.wait_ge(const_in, 16)
                if name == "p_q":
                    pe.wait_ge(attn_w_in, 64)
                    pe.wait_ge(misc_read, PROLOGUE.index("p_x") + 1)
                shared_use(name, k, k % MISC, int(name == "p_x_next"), int(name == "p_x_next"))
            pe.wait_ge(qk_in[0][0], 96)
            unit_scores(0, 0, 0)

            def step(s):
                nxt = 1 - s.par

                def do(name):
                    if s.has(name):
                        if name == "p_q":
                            pe.wait_ge(entry_in[nxt], entry_half(s) * 32 + 32)
                        if READS.get(name) == s.before(name):
                            pe.wait_ge(misc_read, s.number(name))
                        shared_use(name, s.number(name), s.bank(name), *s.entry(name))

                for u, (before_t, between_t, after_t) in enumerate(PLAN):
                    n = s.b * NU + u
                    if not (s.last and u == NU - 1):
                        if u == NU - 1:
                            pe.wait_ge(qk_in[0][nxt], entry_half(s) * 96 + 96)
                            unit_scores(n + 1, 0, nxt)
                        else:
                            if u == 1:
                                pe.wait_ge(qk_in[1][s.par], s.half * 96 + 96)
                            unit_scores(n + 1, u + 1, s.par)
                    if u > 0:
                        unit_values(n - 1, u - 1, s.par, 1, s.number(f"o{u - 1}"), s.bank(f"o{u - 1}"))
                    elif not s.first:
                        unit_values(n - 1, NU - 1, nxt, 1, None, (s.bank(s.uses[0]) + 1) % MISC)
                    for name in before_t:
                        do(name)
                    unit_transposes(n, u, 0)
                    unit_transposes(n, u, 1)
                    for name in between_t:
                        do(name)
                    if s.first and u == 0:
                        pe.wait_ge(out_w_in, 64)
                    unit_transposes(n, u, 2)
                    unit_values(n, u, s.par, 0, s.number(f"o{u}"), s.bank(f"o{u}"))
                    unit_transposes(n, u, 3)
                    for name in after_t:
                        do(name)

            in_steps(pe, step)
            unit_values(B * NU - 1, NU - 1, 1, 1, None, (END_USES - 1) % MISC)
            meanwhile = {"f_out": (0, 1), "f_h": (2,), "f_router": (3,)}
            pe.wait_ge(expert_w_in, 16 * (3 + 2 * 4))
            pe.wait_ge(scores_abs, B * NU)
            pe.wait_ge(h_t_done, 2)
            for k, name in enumerate(EPILOGUE):
                pe.wait_ge(misc_read, END_USES + k)
                shared_use(name, END_USES + k, (END_USES + k) % MISC, B - 1, 1)
                pe_shared_gate_up(pe, 0, meanwhile.get(name, ()))
            pe_experts(pe)


_OUT_SHAPE = (B, S, D)


def _lay_out(inputs):
    arr = lambda name: np.asarray(inputs[name])
    rows = np.arange(P)
    g, r, j = np.meshgrid(np.arange(KT), np.arange(HD), np.arange(H // 2), indexing="ij")
    q_order = ((2 * j + g) * HD + r).reshape(-1)
    k_order = ((2 * j + g) * HD + (-r) % HD).reshape(-1)
    by_column = lambda v: v.reshape(KT, P).T
    a = {
        "x": arr("x"),
        "ctx_t": arr("ctx_1024").transpose(0, 2, 1),
        "wq": arr("L0_xattn_Wq")[q_order].T,
        "bq": by_column(arr("L0_xattn_bq")[q_order]),
        "wk": arr("L0_xattn_Wk")[k_order].T,
        "bk": by_column(arr("L0_xattn_bk")[k_order]),
        "wv": arr("L0_xattn_Wv").T,
        "bv": arr("L0_xattn_bv")[None, :],
        "wo": arr("L0_xattn_Wo").T,
        "bo": arr("L0_xattn_bo")[None, :],
        "rw": arr("L0_ffn_router_w").T,
        "rb": arr("L0_ffn_router_bias")[None, :],
        "gate": arr("L0_ffn_gate_proj"),
        "up": arr("L0_ffn_up_proj"),
        "down": arr("L0_ffn_down_proj"),
        "sh_gate": arr("L0_ffn_sh_gate").T,
        "sh_up": arr("L0_ffn_sh_up").T,
        "sh_down": arr("L0_ffn_sh_down").T,
        "ident": np.eye(P, dtype=np.float32),
        "expert_iota": np.tile(np.arange(E, dtype=np.float32), (P, 1)),
        "tile_iota": np.tile(np.arange(TILES, dtype=np.float32), (P, 1)),
        "row_iota": np.tile(rows.astype(np.float32), (P, 1)),
        "row_number": rows.astype(np.float32)[:, None],
    }
    return {name: np.ascontiguousarray(v) for name, v in a.items()}


def kernel(**inputs):
    import concourse.bacc as bacc
    from concourse.bass_utils import run_bass_kernel_spmd

    arrays = _lay_out(inputs)
    nc = bacc.Bacc("TRN2", target_bir_lowering=False, num_devices=1)
    aps = {name: nc.dram_tensor(f"in_{name}", v.shape, mybir.dt.from_np(v.dtype), kind="ExternalInput").ap()
           for name, v in arrays.items()}
    out = nc.dram_tensor("out_0", _OUT_SHAPE, F32, kind="ExternalOutput").ap()
    program(nc, aps, out)
    r = run_bass_kernel_spmd(nc, [{f"in_{name}": v for name, v in arrays.items()}], core_ids=[0])
    return r.results[0]["out_0"]
```
